# Optimizing a Trainium2 kernel written in Bass

```python
import numpy as np
import jax
import jax.numpy as jnp

def _softmax(x, axis=-1):
    return jax.nn.softmax(x, axis=axis)

def _gelu(x):
    return jax.nn.gelu(x, approximate=True)

def _silu(x):
    return jax.nn.silu(x)

def _sigmoid(x):
    return jax.nn.sigmoid(x)

def _layernorm(x, axis=-1, eps=1e-05):
    m = jnp.mean(x, axis=axis, keepdims=True)
    v = jnp.var(x, axis=axis, keepdims=True)
    return (x - m) / jnp.sqrt(v + eps)

def _scatter_add(tgt, idx, src, axis=0):
    return tgt.at[idx].add(src)

def _segment_sum(src, seg, n):
    return jax.ops.segment_sum(src, seg, n)
kernel_name = 'mk_audio_tower_d2_tok_audfeat256_r4_128345'

def setup_inputs(seed: int=0):
    np.random.seed(seed)
    _w = jnp.asarray

    def _rec_inputs():
        import jax
        import jax.numpy as jnp
        _rk = jax.random.key(seed)
        x = -0.000392918 + 0.999932 * jax.random.normal(jax.random.fold_in(_rk, 1), (8, 750, 64), jnp.float32)
        return x
    x = _rec_inputs()

    def _L0_tok_setup():
        import jax, jax.numpy as jnp
        import numpy as np
        from jax import lax
        B, S, CIN, COUT, K = (32, 512, 64, 64, 16)
        key = jax.random.key(seed)
        k1, k2, k3, k4 = jax.random.split(key, 4)
        x = jax.random.normal(k1, (B, S, CIN), dtype=jnp.float32)
        w_real = jax.random.normal(k2, (COUT, CIN, K), dtype=jnp.float32) * 0.1
        w_imag = jax.random.normal(k3, (COUT, CIN, K), dtype=jnp.float32) * 0.1
        phases = jax.random.normal(k4, (K,), dtype=jnp.float32) * 0.1
        return {'x': x, 'w_real': w_real, 'w_imag': w_imag, 'phases': phases}
    _L0_tok_all = _L0_tok_setup()
    _L0_tok_in = {k: v for k, v in _L0_tok_all.items() if k in ('w_real', 'w_imag', 'phases')}
    del _L0_tok_all

    def _L0_attn_setup():
        import jax, jax.numpy as jnp
        import numpy as np
        IN_C = 64
        KEY_C = 64
        VAL_C = 64
        HEADS = 8
        key = jax.random.key(seed)
        ks = jax.random.split(key, 9)
        s = 0.02
        return {'x': jax.random.normal(ks[0], (4, 2048, IN_C), dtype=jnp.float32), 'Wk': jax.random.normal(ks[1], (KEY_C, IN_C), dtype=jnp.float32) * s, 'bk': jax.random.normal(ks[2], (KEY_C,), dtype=jnp.float32) * s, 'Wq': jax.random.normal(ks[3], (KEY_C, IN_C), dtype=jnp.float32) * s, 'bq': jax.random.normal(ks[4], (KEY_C,), dtype=jnp.float32) * s, 'Wv': jax.random.normal(ks[5], (VAL_C, IN_C), dtype=jnp.float32) * s, 'bv': jax.random.normal(ks[6], (VAL_C,), dtype=jnp.float32) * s, 'Wr': jax.random.normal(ks[7], (IN_C, VAL_C), dtype=jnp.float32) * s, 'br': jax.random.normal(ks[8], (IN_C,), dtype=jnp.float32) * s}
    _L0_attn_all = _L0_attn_setup()
    _L0_attn_in = {k: v for k, v in _L0_attn_all.items() if k in ('Wk', 'bk', 'Wq', 'bq', 'Wv', 'bv', 'Wr', 'br')}
    del _L0_attn_all

    def _L0_ffn_setup():
        import jax, jax.numpy as jnp
        import numpy as np
        INPUT_WIDTH = 64
        DEPTH = 7
        OUTPUT_WIDTH = 64
        N_NODES = 2 ** (DEPTH + 1) - 1
        key = jax.random.key(seed)
        k_x, k_w1, k_w2 = jax.random.split(key, 3)
        init1 = 1.0 / np.sqrt(INPUT_WIDTH)
        x = jax.random.normal(k_x, (2, 256, INPUT_WIDTH), dtype=jnp.float32)
        w1s = jax.random.uniform(k_w1, (N_NODES, INPUT_WIDTH), jnp.float32, -init1, init1)
        b1s = jnp.zeros((N_NODES,), jnp.float32)
        w2s = jax.random.uniform(k_w2, (N_NODES, INPUT_WIDTH, OUTPUT_WIDTH), jnp.float32, -init1, init1)
        b2s = jnp.zeros((N_NODES, OUTPUT_WIDTH), jnp.float32)
        return {'x': x, 'w1s': w1s, 'b1s': b1s, 'w2s': w2s, 'b2s': b2s}
    _L0_ffn_all = _L0_ffn_setup()
    _L0_ffn_in = {k: v for k, v in _L0_ffn_all.items() if k in ('w1s', 'b1s', 'w2s', 'b2s')}
    del _L0_ffn_all

    def _L1_attn_setup():
        import jax, jax.numpy as jnp
        import numpy as np
        D_MODEL = 64
        D_STATE = 16
        key = jax.random.key(seed)
        ks = jax.random.split(key, 7)
        B, L = (8, 512)
        x = jax.random.normal(ks[0], (B, L, D_MODEL), dtype=jnp.float32)
        A_log = jax.random.normal(ks[1], (D_MODEL, D_STATE), dtype=jnp.float32)
        s = 1.0 / np.sqrt(D_MODEL)
        W_B = jax.random.uniform(ks[2], (D_STATE, D_MODEL), jnp.float32, -s, s)
        W_C = jax.random.uniform(ks[3], (D_STATE, D_MODEL), jnp.float32, -s, s)
        W_delta = jax.random.uniform(ks[4], (D_MODEL, D_MODEL), jnp.float32, -s, s)
        b_delta = jax.random.uniform(ks[5], (D_MODEL,), jnp.float32, -s, s)
        D_param = jnp.ones((D_MODEL,), dtype=jnp.float32)
        return {'x': x, 'A_log': A_log, 'W_B': W_B, 'W_C': W_C, 'W_delta': W_delta, 'b_delta': b_delta, 'D_param': D_param}
    _L1_attn_all = _L1_attn_setup()
    _L1_attn_in = {k: v for k, v in _L1_attn_all.items() if k in ('A_log', 'W_B', 'W_C', 'W_delta', 'b_delta', 'D_param')}
    del _L1_attn_all

    def _L1_ffn_setup():
        import jax, jax.numpy as jnp
        import numpy as np
        NUM_EXPERTS = 8
        TOP_K = 2
        B, S, D = (8, 2048, 64)

        def _moe(tokens, router_w, w1, b1, w2, b2):
            N = tokens.shape[0]
            E = router_w.shape[0]
            logits = tokens.astype(jnp.float32) @ router_w.astype(jnp.float32).T
            probs = jax.nn.softmax(logits, axis=-1)
            rw, re = jax.lax.top_k(probs, TOP_K)
            if TOP_K > 1:
                rw = rw / jnp.maximum(rw.sum(-1, keepdims=True), 1e-12)
            rw = rw.astype(tokens.dtype)
            combine = jnp.zeros((N, E), tokens.dtype).at[jnp.arange(N)[:, None], re].set(rw)
            out = tokens
            for e in range(E):
                h = jax.nn.gelu(tokens @ w1[e] + b1[e], approximate=False)
                y = h @ w2[e] + b2[e]
                out = out + combine[:, e:e + 1] * y
            return out
        key = jax.random.key(seed)
        ks = jax.random.split(key, 4)
        scale = 1.0 / np.sqrt(D).astype(np.float32)
        return {'input_embeddings': jax.random.normal(ks[0], (B, S, D), jnp.float32), 'router_w': jax.random.normal(ks[1], (NUM_EXPERTS, D), jnp.float32) * scale, 'w1': jax.random.normal(ks[2], (NUM_EXPERTS, D, D), jnp.float32) * scale, 'b1': jnp.zeros((NUM_EXPERTS, D), jnp.float32), 'w2': jax.random.normal(ks[3], (NUM_EXPERTS, D, D), jnp.float32) * scale, 'b2': jnp.zeros((NUM_EXPERTS, D), jnp.float32)}
    _L1_ffn_all = _L1_ffn_setup()
    _L1_ffn_in = {k: v for k, v in _L1_ffn_all.items() if k in ('router_w', 'w1', 'b1', 'w2', 'b2')}
    del _L1_ffn_all
    return {'x': x, 'L0_tok_w_real': _L0_tok_in['w_real'], 'L0_tok_w_imag': _L0_tok_in['w_imag'], 'L0_tok_phases': _L0_tok_in['phases'], 'L0_attn_Wk': _L0_attn_in['Wk'], 'L0_attn_bk': _L0_attn_in['bk'], 'L0_attn_Wq': _L0_attn_in['Wq'], 'L0_attn_bq': _L0_attn_in['bq'], 'L0_attn_Wv': _L0_attn_in['Wv'], 'L0_attn_bv': _L0_attn_in['bv'], 'L0_attn_Wr': _L0_attn_in['Wr'], 'L0_attn_br': _L0_attn_in['br'], 'L0_ffn_w1s': _L0_ffn_in['w1s'], 'L0_ffn_b1s': _L0_ffn_in['b1s'], 'L0_ffn_w2s': _L0_ffn_in['w2s'], 'L0_ffn_b2s': _L0_ffn_in['b2s'], 'L1_attn_A_log': _L1_attn_in['A_log'], 'L1_attn_W_B': _L1_attn_in['W_B'], 'L1_attn_W_C': _L1_attn_in['W_C'], 'L1_attn_W_delta': _L1_attn_in['W_delta'], 'L1_attn_b_delta': _L1_attn_in['b_delta'], 'L1_attn_D_param': _L1_attn_in['D_param'], 'L1_ffn_router_w': _L1_ffn_in['router_w'], 'L1_ffn_w1': _L1_ffn_in['w1'], 'L1_ffn_b1': _L1_ffn_in['b1'], 'L1_ffn_w2': _L1_ffn_in['w2'], 'L1_ffn_b2': _L1_ffn_in['b2']}

def reference(x, L0_tok_w_real, L0_tok_w_imag, L0_tok_phases, L0_attn_Wk, L0_attn_bk, L0_attn_Wq, L0_attn_bq, L0_attn_Wv, L0_attn_bv, L0_attn_Wr, L0_attn_br, L0_ffn_w1s, L0_ffn_b1s, L0_ffn_w2s, L0_ffn_b2s, L1_attn_A_log, L1_attn_W_B, L1_attn_W_C, L1_attn_W_delta, L1_attn_b_delta, L1_attn_D_param, L1_ffn_router_w, L1_ffn_w1, L1_ffn_b1, L1_ffn_w2, L1_ffn_b2):
    import jax
    import jax.numpy as jnp

    def _L0_tok_ref(x, w_real, w_imag, phases):
        import jax, jax.numpy as jnp
        import numpy as np
        from jax import lax
        B, S, CIN, COUT, K = (32, 512, 64, 64, 16)
        w_eff = jnp.cos(phases)[None, None, :] * w_real - jnp.sin(phases)[None, None, :] * w_imag
        y = lax.conv_general_dilated(jnp.transpose(x, (0, 2, 1)), w_eff, window_strides=(1,), padding='VALID', dimension_numbers=('NCH', 'OIH', 'NCH'))
        return jnp.transpose(y, (0, 2, 1))

    def _L0_attn_ref(x, Wk, bk, Wq, bq, Wv, bv, Wr, br):
        import jax, jax.numpy as jnp
        import numpy as np
        IN_C = 64
        KEY_C = 64
        VAL_C = 64
        HEADS = 8
        n, N, c = x.shape
        xi = x.reshape(n, c, N)
        K = jnp.einsum('oc,ncs->nos', Wk, xi) + bk[None, :, None]
        Q = jnp.einsum('oc,ncs->nos', Wq, xi) + bq[None, :, None]
        V = jnp.einsum('oc,ncs->nos', Wv, xi) + bv[None, :, None]
        dk = KEY_C // HEADS
        dv = VAL_C // HEADS
        Kh = K.reshape(n, HEADS, dk, N)
        Qh = Q.reshape(n, HEADS, dk, N)
        Vh = V.reshape(n, HEADS, dv, N)
        Kh = jax.nn.softmax(Kh, axis=3)
        Qh = jax.nn.softmax(Qh, axis=2)
        ctx = jnp.einsum('nhks,nhvs->nhkv', Kh, Vh)
        att = jnp.einsum('nhkv,nhks->nhvs', ctx, Qh)
        agg = att.reshape(n, VAL_C, N)
        rep = jnp.einsum('ov,nvs->nos', Wr, agg) + br[None, :, None]
        out = rep + xi
        return jnp.transpose(out, (0, 2, 1))

    def _L0_ffn_ref(x, w1s, b1s, w2s, b2s):
        import jax, jax.numpy as jnp
        import numpy as np
        INPUT_WIDTH = 64
        DEPTH = 7
        OUTPUT_WIDTH = 64
        N_NODES = 2 ** (DEPTH + 1) - 1
        B, S, D = x.shape
        flat_x = x.reshape(B * S, D)
        T = flat_x.shape[0]
        current = jnp.zeros((T,), dtype=jnp.int32)
        all_nodes = []
        all_logits = []
        for _ in range(DEPTH + 1):
            all_nodes.append(current)
            score = jnp.einsum('td,td->t', flat_x, w1s[current]) + b1s[current]
            all_logits.append(score)
            choice = ((jnp.sign(score) + 1.0) / 2.0).astype(jnp.int32)
            current = current * 2 + choice + 1
        logits = jnp.stack(all_logits, axis=1)
        path_weights = jax.nn.gelu(jnp.abs(logits), approximate=False)
        out = jnp.zeros((T, OUTPUT_WIDTH), dtype=x.dtype)
        for i in range(DEPTH + 1):
            nodes_i = all_nodes[i]
            t_i = jnp.einsum('td,tdo->to', flat_x, w2s[nodes_i]) + b2s[nodes_i]
            out = out + t_i * path_weights[:, i][:, None]
        return out.reshape(B, S, OUTPUT_WIDTH)

    def _L1_attn_ref(x, A_log, W_B, W_C, W_delta, b_delta, D_param):
        import jax, jax.numpy as jnp
        import numpy as np
        D_MODEL = 64
        D_STATE = 16
        delta = jax.nn.softplus(jnp.einsum('bld,ed->ble', x, W_delta) + b_delta)
        Bt = jnp.einsum('bld,nd->bln', x, W_B)
        Ct = jnp.einsum('bld,nd->bln', x, W_C)
        A = -jnp.exp(A_log)
        dA = jnp.exp(delta[..., None] * A)
        x_db = (x * delta)[..., None] * Bt[:, :, None, :]
        dA_t = jnp.moveaxis(dA, 1, 0)
        xdb_t = jnp.moveaxis(x_db, 1, 0)
        Ct_t = jnp.moveaxis(Ct, 1, 0)
        Bsz, L, Dm = x.shape
        h0 = jnp.zeros((Bsz, Dm, D_STATE), dtype=x.dtype)

        def step(h, inputs):
            da, xdb, c = inputs
            h = da * h + xdb
            y = jnp.einsum('bdn,bn->bd', h, c)
            return (h, y)
        _, y = jax.lax.scan(step, h0, (dA_t, xdb_t, Ct_t))
        y = jnp.moveaxis(y, 0, 1)
        return y + x * D_param

    def _L1_ffn_ref(input_embeddings, router_w, w1, b1, w2, b2):
        import jax, jax.numpy as jnp
        import numpy as np
        NUM_EXPERTS = 8
        TOP_K = 2
        B, S, D = (8, 2048, 64)

        def _moe(tokens, router_w, w1, b1, w2, b2):
            N = tokens.shape[0]
            E = router_w.shape[0]
            logits = tokens.astype(jnp.float32) @ router_w.astype(jnp.float32).T
            probs = jax.nn.softmax(logits, axis=-1)
            rw, re = jax.lax.top_k(probs, TOP_K)
            if TOP_K > 1:
                rw = rw / jnp.maximum(rw.sum(-1, keepdims=True), 1e-12)
            rw = rw.astype(tokens.dtype)
            combine = jnp.zeros((N, E), tokens.dtype).at[jnp.arange(N)[:, None], re].set(rw)
            out = tokens
            for e in range(E):
                h = jax.nn.gelu(tokens @ w1[e] + b1[e], approximate=False)
                y = h @ w2[e] + b2[e]
                out = out + combine[:, e:e + 1] * y
            return out
        b, s, d = input_embeddings.shape
        tokens = input_embeddings.reshape(b * s, d)
        return _moe(tokens, router_w, w1, b1, w2, b2).reshape(b, s, d)
    h = _L0_tok_ref(x, L0_tok_w_real, L0_tok_w_imag, L0_tok_phases)
    h = h + _L0_attn_ref(_layernorm(h, axis=-1), L0_attn_Wk, L0_attn_bk, L0_attn_Wq, L0_attn_bq, L0_attn_Wv, L0_attn_bv, L0_attn_Wr, L0_attn_br)
    h = h + _L0_ffn_ref(_layernorm(h, axis=-1), L0_ffn_w1s, L0_ffn_b1s, L0_ffn_w2s, L0_ffn_b2s)
    h = h + _L1_attn_ref(_layernorm(h, axis=-1), L1_attn_A_log, L1_attn_W_B, L1_attn_W_C, L1_attn_W_delta, L1_attn_b_delta, L1_attn_D_param)
    h = h + _L1_ffn_ref(_layernorm(h, axis=-1), L1_ffn_router_w, L1_ffn_w1, L1_ffn_b1, L1_ffn_w2, L1_ffn_b2)
    return h

_drawn_inputs = setup_inputs


def setup_inputs(seed=0):
    import zlib

    import numpy as np

    out = dict(_drawn_inputs(seed))
    spreads = {'L0_ffn_b1s': (0.0, 0.1),
     'L0_ffn_b2s': (0.0, 0.1),
     'L1_attn_D_param': (1.0, 0.2),
     'L1_ffn_b1': (0.0, 0.8),
     'L1_ffn_b2': (0.0, 0.605)}
    factors = {'L0_attn_Wk': 8.0,
     'L0_attn_bk': 64.0,
     'L0_attn_Wq': 8.0,
     'L0_attn_bq': 25.025,
     'L0_attn_Wv': 8.0,
     'L0_attn_bv': 5.338,
     'L0_attn_Wr': 4.701,
     'L1_attn_b_delta': 3.825}
    for name, (base, spread) in spreads.items():
        noise = np.random.default_rng([zlib.crc32(name.encode()), seed]).standard_normal(out[name].shape)
        drawn = base * np.exp(spread * noise) if base else spread * noise
        out[name] = jnp.asarray(drawn.astype(out[name].dtype))
    for name, factor in factors.items():
        out[name] = (out[name] * factor).astype(out[name].dtype)
    return out
```

```python
from contextlib import ExitStack

import numpy as np
import concourse.bass as bass
from concourse import mybir

F32 = mybir.dt.float32
BF16 = mybir.dt.bfloat16
I32 = mybir.dt.int32
ALU = mybir.AluOpType
ACT = mybir.ActivationFunctionType
AX = mybir.AxisListType.X

B, SIN, D = 8, 750, 64
TAPS = 16
S = SIN - TAPS + 1
J = 7
P = S // J
JA = 4
NA, NB = JA * P, (J - JA) * P
EPS = 1e-5
HEADS, DK = 8, 8
DEPTH = 8
NODES = 2 ** DEPTH - 1
INNER = 2 ** (DEPTH - 1) - 1
PRE = 32
SLOTS = 12
CH = SLOTS // 2
TILE = 128
NT = 78
ROW = 80
STATE = 16
EXPERTS = 8
BT = B * J
SW = S + 1
HALF = SW // 2
LANES = 16
assert (B * S + PRE * (TILE - 1)) // TILE <= NT


def after(step, times, names):
    return times * len(names) + names.index(step) + 1


def rounds(eng, body):
    for u in range(2):
        body(u, u, False)
    with eng.Fori(1, B // 2) as turn:
        for u in range(2):
            body(turn * 2 + u, u, True)


def skewed(eng, first, second):
    first(0, 0, False)
    first(1, 1, False)
    second(0, 0, False)
    first(2, 0, True)
    second(1, 1, False)
    with eng.Fori(1, B // 2 - 1) as turn:
        first(turn * 2 + 1, 1, True)
        second(turn * 2, 0, True)
        first(turn * 2 + 2, 0, True)
        second(turn * 2 + 1, 1, True)
    first(B - 1, 1, True)
    second(B - 2, 0, True)
    second(B - 1, 1, True)


def tiles(eng, seg, first, second=None):
    lo, hi = seg * SEGT, (seg + 1) * SEGT
    if second is None:
        first(lo, 0, seg > 0)
        first(lo + 1, 1, seg > 0)
        with eng.Fori(lo // 2 + 1, hi // 2) as turn:
            first(turn * 2, 0, True)
            first(turn * 2 + 1, 1, True)
        return
    first(lo, 0, seg > 0)
    first(lo + 1, 1, seg > 0)
    second(lo, 0, seg > 0)
    with eng.Fori(lo // 2 + 1, hi // 2) as turn:
        first(turn * 2, 0, True)
        second(turn * 2 - 1, 1, True)
        first(turn * 2 + 1, 1, True)
        second(turn * 2, 0, True)
    second(hi - 1, 1, True)


LN_VEC = ["sum", "mean", "centred", "square_sum", "normal"]
LN_ACT = ["square", "log", "rstd"]
A2V = ["kmax2", "nkmax", "qmax", "qsub", "qsum", "qrec", "qnorm"]
A2A = ["qv0", "qv1", "k0", "k1", "qexp"]
A2P = ["k", "qv"]
A3P = ["et", "qt", "ctx", "mix", "out"]
A3V = ["qt0", "qt1", "ctxm", "ksum", "krec", "mixn", "resid"]
A3A = ["et"]
T1P = ["xt", "st", "c0", "c1", "c2", "c3"]
SCP = ["xt", "z", "b0", "c0", "b1", "c1"]
SCA = ["xt0", "xt1", "z", "abs", "exp", "log", "b0", "c0", "b1", "c1"]
SCV = ["relu", "delta", "xd"]
FIV = ["skip", "h0", "h1"]
MOP = ["xt", "route", "ct"] + [f"{n}{g}" for g in range(4) for n in ("up", "rep")] + ["down"]
MOA = ["xt0", "xt1", "exp", "ct0", "ct1"] + [f"gelu{g}" for g in range(4)]
MOV = (["max", "sub", "sum", "rec", "prob", "top1", "eq1", "cand1", "first1", "hot1", "rest", "top2", "eq2", "cand2", "first2",
        "hot2", "both", "topsum", "guard", "guardrec", "kept", "comb"] + [f"gated{g}" for g in range(4)] + ["out"])
PREP_AT = {3: ["xt"], 6: ["z"], 15: ["b0", "c0", "b1", "c1"]}
CHUNKS = [(0, 2), (2, 4), (4, 6), (6, 7)]
T1A = ["xt0", "xt1", "s0", "s1", "s2", "s3"]
T1V = ["bit0", "bit1"] + [f"{n}{q}" for q in range(4) for n in ("pick", "hot")] + [f"lev{l}" for l in range(DEPTH)]


RK_ROWS = 37
RK_GROUPS = RK_ROWS + 4
SEG = 3
SEGT = NT // SEG


def program(nc, x, conv_r, conv_i, phase, att_k, att_qv, att_r, att_i, head_mask, ident, tree_1, tree_2, tree_b2,
            path, tri, tile_base, ssm_a, ssm_b, ssm_c, ssm_dt, ssm_bd, ssm_d, sel_d, sel_y,
            moe_r, moe_1, moe_2, moe_b2, sel_e, out):
    with ExitStack() as ctx:
        def sb(name, shape, dt=F32):
            return ctx.enter_context(nc.sbuf_tensor(name, shape, dt))

        def region(name, words):
            whole = sb(name, [128, words])

            def phase_buffers():
                at = [0]

                def take(shape, dt=F32):
                    n = int(np.prod(shape[1:]))
                    w = n if dt != BF16 else n // 2
                    ap = whole[0:shape[0], at[0]:at[0] + w]
                    at[0] += w
                    assert at[0] <= words, (name, at[0])
                    if dt != F32:
                        ap = ap.bitcast(dt)
                    if len(shape) == 3:
                        ap = ap.rearrange("p (a b) -> p a b", a=shape[1])
                    if len(shape) == 4:
                        ap = ap.rearrange("p (a b c) -> p a b c", a=shape[1], b=shape[2])
                    return ap
                return take
            return phase_buffers

        def sem(name):
            return ctx.enter_context(nc.semaphore(name))

        xi_dram = nc.dram_tensor("xi_dram", [B, S * D], F32, kind="Internal")
        sorted_dram = nc.dram_tensor("sorted_dram", [TILE * NT, ROW], F32, kind="Internal")
        y_dram = nc.dram_tensor("y_dram", [TILE * NT, D], F32, kind="Internal")

        ps = ctx.enter_context(nc.psum_tensor("ps", [128, 8, 512], F32))
        h = sb("h", [P, B, J * D])
        eps = sb("eps", [128, 1]); idm = sb("idm", [128, 128]); zero = sb("zero", [128, ROW])
        mu = sb("mu", [P, 2, J]); xc = sb("xc", [P, 2, J * D]); sq = sb("sq", [P, 2, J * D])
        vs = sb("vs", [P, 2, J]); lv = sb("lv", [P, 2, J]); rs = sb("rs", [P, 2, J])
        xn = sb("xn", [P, 2, J, D + 1])
        hot = sb("hot", [P, BT, PRE], BF16); lev = sb("lev", [P, BT, DEPTH])
        rows = sb("rows", [P, BT, ROW]); sli = sb("sli", [P, 4, BT], I32); pfi = sb("pfi", [1, NT], I32)
        w1t = sb("w1t", [65, NODES]); pth = sb("pth", [128, NODES + 1], BF16); trs = sb("trs", [P, 2 * P], BF16)
        base = sb("base", [1, NT])

        front = region("front", 13900)
        take = front()
        wr = take([128, 8 * D]); wi = take([128, 8 * D]); weff = take([128, 8 * D])
        ph = take([128, 6, 8]); phi = take([128, 8], I32); xw = take([128, 2, SIN])
        wk = take([65, D]); wqv = take([65, 2 * D]); wrt = take([D, D]); wid = take([65, D]); hm = take([D, D])
        xi = take([65, 2, S]); kmx = take([D, 2, 4]); ke = take([D, 2, S]); ksum = take([D, 2, 4])
        qv = take([P, 2, J * 2 * D]); qmx = take([P, 2, BT]); qs = take([P, 2, J * D]); qe = take([P, 2, J * D])
        qsm = take([P, 2, BT]); qn = take([P, 2, J * D]); et = take([P, 2, J * D]); qt = take([D, 2, S])
        ctm = take([D, 2, D]); kr = take([D, 2, 2]); mixn = take([D, 2, D])
        take = front()
        rt = take([128, NT, ROW]); ys = take([128, NT, D])
        take = front()
        yg = take([P, BT, D])
        xe = take([65, 2, SW]); ct = take([EXPERTS, 2, SW]); gl = take([128, 2, SW])
        gs = take([128, 4, SW])

        mid = region("mid", 10600)
        take = mid()
        xt = take([65, 2, S]); bits = take([128, 2, S + 1], BF16)
        scr = take([P, 2, 2 * NODES]); pick = take([P, 2, J * NODES])
        take = mid()
        tot = take([P, PRE, BT + 1]); inc = take([P, PRE, BT + 1]); rank = take([P, BT, PRE]); gel = take([P, 2, BT, DEPTH])
        side = take([P, 6, BT]); cnt = take([P, 2, PRE]); cnti = take([P, PRE], I32); slf = take([P, 3, BT])
        cmp = take([1, NT, PRE]); pff = take([1, 2, NT])
        take = mid()
        zt = take([128, 2, 7 * 128]); zz = take([128, 2, 7 * 128])

        take = mid()
        asc = take([128, 8]); wb = take([128, 128]); wc = take([128, 128]); wdt = take([128, 128]); bdc = take([128, 1])
        dsc = take([128, 1]); seld = take([128, 8 * 128]); sely = take([128, 248])
        za = take([128, SW]); zb = take([128, SW]); zl = take([128, SW]); zr = take([128, SW]); yt = take([128, SW]); xp = take([P, J, 2, D])
        mor = take([D, EXPERTS]); mo1 = take([65, EXPERTS * D]); mo2 = take([128, 4 * D]); mob = take([EXPERTS, D])
        sele = take([EXPERTS, EXPERTS * D]); rankw = take([P, EXPERTS])
        small = [take([P, 2, J * EXPERTS]) for _ in range(12)]
        tiny = [take([P, 2, J]) for _ in range(10)]
        oo = take([P, 2, J * D])

        rear = region("rear", PRE * CH * D + PRE * D)
        take = rear()
        w2t = take([128, PRE * CH * D]); b2t = take([SLOTS, PRE * D])

        take = rear()
        xs = take([128, 2, SW]); dl = take([128, 2, SW]); xd = take([128, 2, SW]); brep = take([128, 2, SW]); crep = take([128, 2, SW])
        da = take([128, 2, SW]); xdb = take([128, 2, SW]); hs = take([128, 2, SW]); hc = take([128, 2, SW])

        block = ctx.enter_context(nc.Block())
        s_w = sem("weights_in"); s_cw = sem("conv_weights_in"); s_x = [sem("xw_in0"), sem("xw_in1")]
        s_ph = sem("phase_vec"); s_pha = sem("phase_act"); s_const = sem("constants_set")
        conv_done = sem("conv_done"); h_set = sem("h_set")
        ln_vec = [sem(f"ln{n}_vec") for n in range(4)]; ln_act = [sem(f"ln{n}_act") for n in range(4)]
        xi_out = [sem("xi_out0"), sem("xi_out1")]; xi_in = [sem("xi_in0"), sem("xi_in1")]
        a2p = sem("proj_pe"); a2v = sem("proj_vec"); a2a = sem("proj_act")
        a3p = sem("mix_pe"); a3v = sem("mix_vec"); a3a = sem("mix_act")
        s_sw = sem("scan_weights_in"); sset = sem("scan_const_set"); scp = sem("scan_prep_pe"); sca = sem("scan_prep_act"); scv = sem("scan_prep_vec")
        d_pe = sem("delta_spread"); x_pe = sem("xdelta_spread"); da_act = sem("decay"); xdb_vec = sem("drive"); scan_vec = sem("scanned")
        hc_pool = sem("read_out"); y_sum = sem("y_sum"); fiv = sem("scan_out_vec"); back_pe = sem("back_pe")
        mop = sem("expert_pe"); moa = sem("expert_act"); mov = sem("expert_vec"); hx_pool = sem("residual_pool"); row_out = [sem("row_out0"), sem("row_out1")]
        s_tw = sem("tree_weights_in"); row_set = sem("row_set"); tset = sem("tree_const_set")
        t1p = sem("score_pe"); t1a = sem("score_act"); t1v = sem("score_vec")
        rkv = sem("rank_vec"); rkp = sem("rank_pe"); rka = sem("rank_act")
        zero_out = sem("zero_out"); scattered = sem("scattered"); sorted_in = [sem(f"sorted_in{n}") for n in range(SEG)]
        z_vec = sem("z_vec"); z_pool = sem("z_pool"); z_pe = sem("z_pe"); z_act = sem("z_act"); y_pe = sem("y_pe"); y_act = sem("y_act")
        y_out = sem("y_out"); gathered = [sem(f"gathered{b}") for b in range(B)]; h_tree = sem("h_tree")
        pe_gate = sem("pe_gate")

        def slot(b, u):
            return 8 * b + 16 - 8 * u

        def halves(ap):
            return ap.rearrange("p (n w) -> p n w", n=2)

        def v3(ap, j=J):
            return ap.rearrange("p (j d) -> p j d", j=j)

        @block.sync
        def _(sp):
            sp.dma_start(wr[:, :], conv_r).then_inc(s_cw, 16)
            sp.dma_start(wi[:, :], conv_i).then_inc(s_cw, 16)
            sp.dma_start(ph[:, 0, :], phase).then_inc(s_cw, 16)

            def load_window(b, u, again):
                if again:
                    sp.wait_ge(conv_done, b - 1)
                sp.dma_start(xw[0:64, u, :], x[:, b, :]).then_inc(s_x[u], 16)
                sp.dma_start(xw[64:128, u, 0:SIN - 1], x[:, b, 1:SIN]).then_inc(s_x[u], 16)

            def store_xi(b, u, again):
                sp.wait_ge(ln_vec[0], after("normal", b, LN_VEC))
                sp.dma_start(xi_dram[b].rearrange("(p j d) -> p j d", p=P, j=J), xn[:, u, :, 0:D]).then_inc(xi_out[u], 16)

            load_window(0, 0, False)
            load_window(1, 1, False)
            sp.dma_start(idm[:, :], ident).then_inc(s_w, 16)
            sp.dma_start(wk[:, :], att_k).then_inc(s_w, 16)
            sp.dma_start(wqv[:, :], att_qv).then_inc(s_w, 16)
            sp.dma_start(wrt[:, :], att_r).then_inc(s_w, 16)
            sp.dma_start(wid[:, :], att_i).then_inc(s_w, 16)
            sp.dma_start(hm[:, :], head_mask).then_inc(s_w, 16)
            with sp.Fori(0, B // 2 - 1) as turn:
                for u in range(2):
                    load_window(turn * 2 + 2 + u, u, True)
                    store_xi(turn * 2 + u, u, True)
            store_xi(B - 2, 0, True)
            store_xi(B - 1, 1, True)

            def load_xi(b, u, again):
                sp.wait_ge(xi_out[u], slot(b, u))
                if again:
                    sp.wait_ge(a3p, after("out", b - 2, A3P))
                sp.dma_start(xi[0:D, u, :], xi_dram[b].rearrange("(c s) -> c s", c=D)).then_inc(xi_in[u], 16)

            rounds(sp, load_xi)
            for n in range(SEG):
                sp.wait_ge(scattered, 16 * BT)
                sp.dma_start(rt[:, n * SEGT:(n + 1) * SEGT, :],
                             sorted_dram.ap().rearrange("(p g) w -> p g w", p=128)[:, n * SEGT:(n + 1) * SEGT, :]
                             ).then_inc(sorted_in[n], 16)
            for n in range(SEG):
                sp.wait_ge(y_act, (n + 1) * SEGT)
                sp.dma_start(y_dram.ap().rearrange("(p g) w -> p g w", p=128)[:, n * SEGT:(n + 1) * SEGT, :],
                             ys[:, n * SEGT:(n + 1) * SEGT, :]).then_inc(y_out, 16)
            sp.wait_ge(y_pe, NT)
            sp.wait_ge(z_act, NT)
            for dst, src in ((asc, ssm_a), (wb, ssm_b), (wc, ssm_c), (wdt, ssm_dt), (bdc, ssm_bd), (dsc, ssm_d), (seld, sel_d),
                             (sely, sel_y), (mor, moe_r), (mo1, moe_1), (mo2, moe_2), (mob, moe_b2), (sele, sel_e)):
                sp.dma_start(dst, src).then_inc(s_sw, 16)

            def store(b, u, again):
                sp.wait_ge(mov, after("out", b, MOV))
                sp.dma_start(out[b].rearrange("(p j) d -> p (j d)", j=J), oo[:, u, :]).then_inc(row_out[u], 16)

            rounds(sp, store)
            sp.wait_ge(row_out[0], slot(B - 2, 0))
            sp.wait_ge(row_out[1], slot(B - 1, 1))

        @block.gpsimd
        def _(pool):
            for dst, src in ((w1t, tree_1), (pth[:, 0:NODES], path), (trs, tri), (w2t, tree_2), (b2t, tree_b2), (base, tile_base)):
                pool.dma_start(dst[:, :], src).then_inc(s_tw, 16)
            pool.wait_ge(tset, 2)
            pool.dma_start(sorted_dram.ap().rearrange("(p g) w -> p g w", p=128),
                           zero[:, :].unsqueeze(1).broadcast_to([128, NT, ROW])).then_inc(zero_out, 16)

            def keep_rows(b, u, again):
                pool.wait_ge(ln_vec[1], after("normal", b, LN_VEC))
                pool.tensor_copy(rows[:, bass.ds(b * J, J), 0:D + 1], xn[:, u, :, :]).then_inc(row_set, 1)

            rounds(pool, keep_rows)
            pool.wait_ge(zero_out, 16)
            pool.wait_ge(row_set, B)
            pool.wait_ge(rkv, RK_ROWS)
            for i in range(BT):
                pool.indirect_dma_start(out=sorted_dram[:, :], out_offset=bass.IndirectOffsetOnAxis(ap=sli[:, 3, i:i + 1], axis=0),
                                        in_=rows[:, i, :], in_offset=None).then_inc(scattered, 16)

            def spread(g, u, again):
                if again:
                    pool.wait_ge(z_pe, g - 1)
                pool.tensor_tensor(zt[:, u, 512:768].rearrange("p (s d) -> p s d", s=4),
                                   rt[:, g, 76:80].unsqueeze(2).broadcast_to([128, 4, D]),
                                   rt[:, g, 0:D].unsqueeze(1).broadcast_to([128, 4, D]), ALU.mult).then_inc(z_pool, 1)

            for n in range(SEG):
                pool.wait_ge(sorted_in[n], 16)
                tiles(pool, n, spread)
            pool.wait_ge(y_out, 16 * SEG)
            for b in range(B):
                for i in range(b * J, (b + 1) * J):
                    pool.indirect_dma_start(out=yg[:, i, :], out_offset=None, in_=y_dram[:, :],
                                            in_offset=bass.IndirectOffsetOnAxis(ap=sli[:, 3, i:i + 1], axis=0)).then_inc(gathered[b], 16)
            for n in range(B // 2 * LANES):
                pool.wait_ge(scan_vec, n + 1)
                if n == 0:
                    pool.wait_ge(sca, after("c1", 0, SCA))
                elif n % LANES == 0:
                    pool.wait_ge(sca, after("c1", n // LANES, SCA))
                if n >= 2:
                    pool.wait_ge(y_sum, n - 1)
                pool.tensor_tensor(hc[:, n % 2, :], hs[:, n % 2, :], crep[:, n % LANES // 8, :], ALU.mult).then_inc(hc_pool, 1)

            def residual(b, u, again):
                pool.wait_ge(ln_vec[3], after("normal", b, LN_VEC))
                if again:
                    pool.wait_ge(row_out[u], slot(b - 2, u))
                pool.tensor_tensor(v3(oo[:, u, :]), v3(h[:, b, :]), xn[:, u, :, 0:D], ALU.add).then_inc(hx_pool, 1)

            rounds(pool, residual)

        @block.tensor
        def _(pe):
            pe.wait_ge(s_ph, 12)

            def conv(b, u, again):
                pe.wait_ge(s_x[u], 2 * slot(b, u))
                if again:
                    pe.wait_ge(h_set, b - 1)
                for j in range(J):
                    for k in range(TAPS // 2):
                        last = pe.matmul(ps[0:P, u, j * D:(j + 1) * D],
                                         xw[:, u, 2 * k + j:2 * k + j + J * (P - 1) + 1:J],
                                         weff[:, k * D:(k + 1) * D], start=(k == 0), stop=(k == TAPS // 2 - 1))
                last.then_inc(conv_done, 1)

            rounds(pe, conv)

            def project(b, u, again):
                pe.wait_ge(xi_in[u], slot(b, u))
                if not again and b == 0:
                    pe.wait_ge(h_set, B)
                    pe.wait_ge(s_w, 16 * 6)
                    pe.wait_ge(s_const, 2)
                else:
                    pe.wait_ge(a2a, after("k1", b - 1, A2A))
                pe.sem_inc(pe_gate)
                for n, (lo, hi) in enumerate(((0, 368), (368, S))):
                    last = pe.matmul(ps[0:D, n, 0:hi - lo], wk[:, :], xi[:, u, lo:hi], start=True, stop=True)
                last.then_inc(a2p, 1)
                for j in range(J):
                    last = pe.matmul(ps[0:P, 2 + j // 4, (j % 4) * 128:(j % 4 + 1) * 128], xi[:, u, j::J], wqv[:, :],
                                     start=True, stop=True)
                last.then_inc(a2p, 1)

            def mix(b, u, again):
                pe.wait_ge(a2a, after("k1", b, A2A))
                if not (not again and b == 0):
                    pe.wait_ge(a3v, after("ctxm", b - 1, A3V))
                pe.sem_inc(pe_gate)
                for j in range(J):
                    last = pe.transpose(ps[0:P, 4, j * D:(j + 1) * D], ke[:, u, j::J], idm[0:D, 0:D])
                last.then_inc(a3p, 1)
                pe.wait_ge(a2v, after("qnorm", b, A2V))
                pe.sem_inc(pe_gate)
                for j in range(J):
                    last = pe.transpose(ps[0:D, 5 + j // JA, (j % JA) * P:(j % JA + 1) * P],
                                        qn[:, u, j * D:(j + 1) * D], idm[0:P, 0:P])
                last.then_inc(a3p, 1)
                pe.wait_ge(a3a, after("et", b, A3A))
                pe.sem_inc(pe_gate)
                for j in range(J):
                    last = pe.matmul(ps[0:D, 4, 448:512], qv[:, u, j * 128 + 64:(j + 1) * 128],
                                     et[:, u, j * D:(j + 1) * D], start=(j == 0), stop=(j == J - 1))
                last.then_inc(a3p, 1)
                pe.wait_ge(a3v, after("ctxm", b, A3V))
                pe.sem_inc(pe_gate)
                pe.matmul(ps[0:D, 7, 448:512], ctm[:, u, :], wrt[:, :], start=True, stop=True).then_inc(a3p, 1)
                pe.wait_ge(a3v, after("mixn", b, A3V))
                pe.sem_inc(pe_gate)
                for j in range(J):
                    pe.matmul(ps[0:P, 7, j * D:(j + 1) * D], qt[:, u, j * P:(j + 1) * P], mixn[:, u, :],
                              start=True, stop=False)
                    last = pe.matmul(ps[0:P, 7, j * D:(j + 1) * D], xi[:, u, j::J], wid[:, :], start=False, stop=True)
                last.then_inc(a3p, 1)

            skewed(pe, project, mix)

            def scores(b, u, again):
                pe.wait_ge(ln_vec[1], after("normal", b, LN_VEC))
                if not again and b == 0:
                    pe.wait_ge(a3v, after("resid", B - 1, A3V))
                    pe.wait_ge(s_tw, 16 * 6)
                    pe.wait_ge(tset, 2)
                else:
                    pe.wait_ge(t1a, after("xt1", b - 1, T1A))
                pe.sem_inc(pe_gate)
                for j in range(J):
                    last = pe.transpose(ps[0:D + 1, j // JA, (j % JA) * P:(j % JA + 1) * P], xn[:, u, j, :], idm[0:P, 0:P])
                last.then_inc(t1p, 1)
                pe.wait_ge(t1a, after("xt1", b, T1A))
                if not (not again and b == 0):
                    pe.wait_ge(t1v, after("bit1", b - 1, T1V))
                pe.sem_inc(pe_gate)
                pe.matmul(ps[0:INNER, 2, 0:NA], w1t[:, 0:INNER], xt[:, u, 0:NA], start=True, stop=True)
                pe.matmul(ps[0:INNER, 3, 0:NB], w1t[:, 0:INNER], xt[:, u, NA:S], start=True, stop=True).then_inc(t1p, 1)
                for q, (lo, hi) in enumerate(CHUNKS):
                    if q >= 2:
                        pe.wait_ge(t1a, after(f"s{q - 2}", b, T1A))
                        pe.wait_ge(t1v, after(f"hot{q - 2}", b, T1V))
                        pe.sem_inc(pe_gate)
                    elif not (not again and b == 0):
                        pe.wait_ge(t1a, after(f"s{q + 2}", b - 1, T1A))
                        pe.wait_ge(t1v, after(f"hot{q + 2}", b - 1, T1V))
                        pe.sem_inc(pe_gate)
                    for j in range(lo, hi):
                        pe.matmul(ps[0:P, 4 + q % 2, (j - lo) * NODES:(j - lo + 1) * NODES], xt[:, u, j * P:(j + 1) * P], w1t[:, :],
                                  start=True, stop=True)
                    if q == 0:
                        pe.wait_ge(t1v, after("bit1", b, T1V))
                        pe.sem_inc(pe_gate)
                    for j in range(lo, hi):
                        last = pe.matmul(ps[0:P, 6 + q % 2, (j - lo) * NODES:(j - lo + 1) * NODES],
                                         bits[:, u, j * P:(j + 1) * P], pth[:, 0:NODES], start=True, stop=True)
                    last.then_inc(t1p, 1)

            rounds(pe, scores)
            pe.wait_ge(t1v, after("lev7", B - 1, T1V))
            flat = hot[:, :, :].rearrange("p i g -> p (i g)")
            for q in range(4):
                pe.matmul(ps[0:P, q, 0:448], trs[:, 0:P], flat[:, q * 448:(q + 1) * 448], start=True, stop=True)
            for q in range(4):
                last = pe.matmul(ps[0:P, 4 + q, 0:448], trs[:, P:2 * P], flat[:, q * 448:(q + 1) * 448], start=True, stop=True)
            last.then_inc(rkp, 1)

            def turn_round(g, u, again):
                pe.wait_ge(z_vec, g + 1)
                pe.wait_ge(z_pool, g + 1)
                if again:
                    pe.wait_ge(z_act, g - 1)
                pe.sem_inc(pe_gate)
                for c in range(7):
                    last = pe.transpose(ps[:, 2 * u + c // 4, (c % 4) * 128:(c % 4 + 1) * 128],
                                        zt[:, u, c * 128:(c + 1) * 128], idm[:, :])
                last.then_inc(z_pe, 1)

            def apply(g, u, again):
                pe.wait_ge(z_act, g + 1)
                if again:
                    pe.wait_ge(y_act, g - 1)
                pe.sem_inc(pe_gate)
                group = pe.value_load(pfi[0:1, bass.ds(g, 1)], min_val=0, max_val=PRE - 1)
                w2v = w2t[:, :].rearrange("p (g c d) -> p g c d", g=PRE, c=CH)
                for c in range(CH):
                    pe.matmul(ps[:, 4 + u, 0:D], zz[:, u, c * 128:(c + 1) * 128], w2v[:, group, c, :],
                              start=(c == 0), stop=False)
                pe.matmul(ps[:, 4 + u, 0:D], zz[0:SLOTS, u, 768:896], b2t[:, :].rearrange("p (g d) -> p g d", g=PRE)[:, group, :],
                          start=False, stop=True).then_inc(y_pe, 1)

            pe.wait_ge(rkv, RK_GROUPS)
            for n in range(SEG):
                pe.wait_ge(sorted_in[n], 16)
                tiles(pe, n, turn_round, apply)

            def prepare(q, part):
                u = q % 2
                if part == "xt":
                    pe.wait_ge(ln_vec[2], after("normal", 2 * q + 1, LN_VEC))
                    if q == 0:
                        pe.wait_ge(y_act, NT)
                        pe.wait_ge(s_sw, 16 * 13)
                    if q >= 2:
                        pe.wait_ge(fiv, after("h1", q - 2, FIV))
                    for j in range(J):
                        last = pe.transpose(ps[:, 6 + j // JA, (j % JA) * P:(j % JA + 1) * P], xp[:, j, :, :].rearrange("p b d -> p (b d)"), idm[0:P, 0:P])
                    last.then_inc(scp, 1)
                if part == "z":
                    pe.wait_ge(sca, after("xt1", q, SCA))
                    pe.wait_ge(sset, 1)
                    for n in range(2):
                        last = pe.matmul(ps[:, 6 + n, 0:HALF], wdt, xs[:, u, n * HALF:(n + 1) * HALF], start=True, stop=True)
                    last.then_inc(scp, 1)
                if part in ("b0", "c0", "b1", "c1"):
                    if part == "b0":
                        pe.wait_ge(sca, after("z", q, SCA))
                    else:
                        pe.wait_ge(sca, after({"c0": "b0", "b1": "c0", "c1": "b1"}[part], q, SCA))
                    r = 64 * int(part[1])
                    w = wb if part[0] == "b" else wc
                    for n in range(2):
                        last = pe.matmul(ps[:, 6 + n, 0:HALF], w[r:r + 64, :], xs[r:r + 64, u, n * HALF:(n + 1) * HALF],
                                         start=True, stop=True)
                    last.then_inc(scp, 1)

            for part in SCP:
                prepare(0, part)

            def sum_states(n):
                pe.wait_ge(hc_pool, n + 1)
                if n % LANES == 0 and n:
                    pe.wait_ge(fiv, after("skip", n // LANES - 1, FIV))
                for m in range(2):
                    last = pe.matmul(ps[:, 4 + m, 0:HALF], sely[:, 120 - 8 * (n % LANES):248 - 8 * (n % LANES)],
                                     hc[:, n % 2, m * HALF:(m + 1) * HALF], start=(n % LANES == 0), stop=(n % LANES == LANES - 1))
                last.then_inc(y_sum, 1)

            def back(q):
                pe.wait_ge(fiv, after("skip", q, FIV))
                if q < B // 2 - 1:
                    pe.wait_ge(sca, after("c1", q + 1, SCA))
                for j in range(J):
                    last = pe.transpose(ps[0:P, 6 + j // 4, (j % 4) * 128:(j % 4 + 1) * 128], yt[:, j:S:J], idm[:, :])
                last.then_inc(back_pe, 1)

            for q in range(B // 2):
                u = q % 2
                for k in range(LANES):
                    n = q * LANES + k
                    r, g = 64 * (k // 8), k % 8
                    if k == 0:
                        pe.wait_ge(scv, after("xd", q, SCV))
                    if n:
                        pe.wait_ge(da_act, n)
                    for m in range(2):
                        last = pe.matmul(ps[:, m, 0:HALF], seld[r:r + 64, g * 128:(g + 1) * 128], dl[r:r + 64, u, m * HALF:(m + 1) * HALF],
                                         start=True, stop=True)
                    last.then_inc(d_pe, 1)
                    if n:
                        pe.wait_ge(xdb_vec, n)
                    for m in range(2):
                        last = pe.matmul(ps[:, 2 + m, 0:HALF], seld[r:r + 64, g * 128:(g + 1) * 128], xd[r:r + 64, u, m * HALF:(m + 1) * HALF],
                                         start=True, stop=True)
                    last.then_inc(x_pe, 1)
                    if k:
                        sum_states(n - 1)
                    if q < B // 2 - 1 and k in PREP_AT:
                        for part in PREP_AT[k]:
                            prepare(q + 1, part)
                sum_states(q * LANES + LANES - 1)
                back(q)


            def first(b, u, again):
                pe.wait_ge(ln_vec[3], after("normal", b, LN_VEC))
                if not again and b == 0:
                    pe.wait_ge(fiv, after("h1", B // 2 - 1, FIV))
                else:
                    pe.wait_ge(moa, after("ct1", b - 1, MOA))
                pe.sem_inc(pe_gate)
                for j in range(J):
                    last = pe.transpose(ps[0:D + 1, j // JA, (j % JA) * P:(j % JA + 1) * P], xn[:, u, j, :], idm[0:P, 0:P])
                last.then_inc(mop, 1)
                pe.wait_ge(moa, after("xt1", b, MOA))
                if not (not again and b == 0):
                    pe.wait_ge(mov, after("sub", b - 1, MOV))
                pe.sem_inc(pe_gate)
                for j in range(J):
                    last = pe.matmul(ps[0:P, 2, j * EXPERTS:(j + 1) * EXPERTS], xe[0:D, u, j * P:(j + 1) * P], mor, start=True, stop=True)
                last.then_inc(mop, 1)
                pe.wait_ge(mov, after("comb", b, MOV))
                pe.sem_inc(pe_gate)
                for j in range(J):
                    last = pe.transpose(ps[0:EXPERTS, j // JA, (j % JA) * P:(j % JA + 1) * P],
                                        small[11][:, u, j * EXPERTS:(j + 1) * EXPERTS], idm[0:P, 0:P])
                last.then_inc(mop, 1)
                for g in range(4):
                    if g:
                        pe.wait_ge(moa, after(f"gelu{g - 1}", b, MOA))
                    else:
                        pe.wait_ge(moa, after("ct1", b, MOA))
                    pe.sem_inc(pe_gate)
                    for m in range(2):
                        last = pe.matmul(ps[:, 4 + m, 0:HALF], mo1[:, g * 128:(g + 1) * 128], xe[:, u, m * HALF:(m + 1) * HALF],
                                         start=True, stop=True)
                    last.then_inc(mop, 1)
                    if g:
                        pe.wait_ge(mov, after(f"gated{g - 1}", b, MOV))
                        pe.sem_inc(pe_gate)
                    for m in range(2):
                        last = pe.matmul(ps[:, 6 + m, 0:HALF], sele[:, g * 128:(g + 1) * 128], ct[:, u, m * HALF:(m + 1) * HALF],
                                         start=True, stop=True)
                    last.then_inc(mop, 1)
                pe.wait_ge(mov, after("gated3", b, MOV))
                pe.sem_inc(pe_gate)
                for j in range(J):
                    o = ps[0:P, 3, j * D:(j + 1) * D]
                    for g in range(4):
                        pe.matmul(o, gs[:, g, j * P:(j + 1) * P], mo2[:, g * D:(g + 1) * D], start=(g == 0), stop=False)
                    last = pe.matmul(o, ct[:, u, j * P:(j + 1) * P], mob, start=False, stop=True)
                last.then_inc(mop, 1)

            rounds(pe, first)

        def ln_act_steps(act, n, b, u):
            act.wait_ge(ln_vec[n], after("centred", b, LN_VEC))
            act.activation(sq[:, u, :], xc[:, u, :], ACT.Square).then_inc(ln_act[n], 1)
            act.wait_ge(ln_vec[n], after("square_sum", b, LN_VEC))
            act.activation(lv[:, u, :], vs[:, u, :], ACT.Ln, bias=eps[0:P, :], scale=1.0 / D).then_inc(ln_act[n], 1)
            act.wait_ge(ln_act[n], after("log", b, LN_ACT))
            act.activation(rs[:, u, :], lv[:, u, :], ACT.Exp, scale=-0.5).then_inc(ln_act[n], 1)

        def ln_vec_steps(dve, n, b, u, dst):
            src = v3(h[:, b, :])
            dve.tensor_reduce(mu[:, u, :], src, AX, ALU.add).then_inc(ln_vec[n], 1)
            dve.wait_ge(ln_vec[n], after("sum", b, LN_VEC))
            dve.tensor_scalar(mu[:, u, :], mu[:, u, :], 1.0 / D, None, ALU.mult).then_inc(ln_vec[n], 1)
            dve.wait_ge(ln_vec[n], after("mean", b, LN_VEC))
            dve.tensor_tensor(v3(xc[:, u, :]), src, mu[:, u, :].unsqueeze(2).broadcast_to([P, J, D]),
                              ALU.subtract).then_inc(ln_vec[n], 1)
            dve.wait_ge(ln_act[n], after("square", b, LN_ACT))
            dve.tensor_reduce(vs[:, u, :], v3(sq[:, u, :]), AX, ALU.add).then_inc(ln_vec[n], 1)
            dve.wait_ge(ln_act[n], after("rstd", b, LN_ACT))
            dve.tensor_tensor(dst, v3(xc[:, u, :]), rs[:, u, :].unsqueeze(2).broadcast_to([P, J, D]),
                              ALU.mult).then_inc(ln_vec[n], 1)

        @block.scalar
        def _(act):
            act.wait_ge(s_ph, 9)
            act.activation(ph[:, 4, :], ph[:, 2, :], ACT.Sin).then_inc(s_pha, 1)
            act.activation(ph[:, 5, :], ph[:, 3, :], ACT.Sin).then_inc(s_pha, 1)
            act.wait_ge(s_const, 2)

            def conv_out(b, u, again):
                act.wait_ge(conv_done, b + 1)
                act.activation(h[:, b, :], ps[0:P, u, 0:448], ACT.Copy).then_inc(h_set, 1)
                ln_act_steps(act, 0, b, u)

            rounds(act, conv_out)

            def project(b, u, again):
                act.wait_ge(a2p, after("qv", b, A2P))
                if again:
                    act.wait_ge(a3p, after("ctx", b - 2, A3P))
                act.activation(qv[:, u, 0:512], ps[0:P, 2, :], ACT.Copy).then_inc(a2a, 1)
                act.activation(qv[:, u, 512:896], ps[0:P, 3, 0:384], ACT.Copy).then_inc(a2a, 1)
                act.wait_ge(a2v, after("nkmax", b, A2V))
                if again:
                    act.wait_ge(a3v, after("ksum", b - 2, A3V))
                act.activation(ke[:, u, 0:368], ps[0:D, 0, 0:368], ACT.Exp, bias=kmx[:, u, 2:3],
                               accum_out=ksum[:, u, 0:1]).then_inc(a2a, 1)
                act.activation(ke[:, u, 368:S], ps[0:D, 1, 0:S - 368], ACT.Exp, bias=kmx[:, u, 2:3],
                               accum_out=ksum[:, u, 1:2]).then_inc(a2a, 1)
                act.wait_ge(a2v, after("qsub", b, A2V))
                act.activation(qe[:, u, :], qs[:, u, :], ACT.Exp).then_inc(a2a, 1)

            def mix(b, u, again):
                act.wait_ge(a3p, after("et", b, A3P))
                act.activation(et[:, u, :], ps[0:P, 4, 0:448], ACT.Copy).then_inc(a3a, 1)

            skewed(act, project, mix)

            def norm_tree(b, u, again):
                ln_act_steps(act, 1, b, u)

            def scores(b, u, again):
                act.wait_ge(t1p, after("xt", b, T1P))
                act.activation(xt[:, u, 0:NA], ps[0:D + 1, 0, 0:NA], ACT.Copy).then_inc(t1a, 1)
                act.activation(xt[:, u, NA:S], ps[0:D + 1, 1, 0:NB], ACT.Copy).then_inc(t1a, 1)
                for q, (lo, hi) in enumerate(CHUNKS):
                    act.wait_ge(t1p, after(f"c{q}", b, T1P))
                    if q >= 2:
                        act.wait_ge(t1v, after(f"pick{q - 2}", b, T1V))
                    elif not (not again and b == 0):
                        act.wait_ge(t1v, after(f"pick{q + 2}" if q == 0 else "pick3", b - 1, T1V))
                    n = (hi - lo) * NODES
                    act.activation(scr[:, q % 2, 0:n], ps[0:P, 4 + q % 2, 0:n], ACT.Copy).then_inc(t1a, 1)

            skewed(act, norm_tree, scores)
            act.wait_ge(t1v, after("lev7", B - 1, T1V))
            act.activation(gel[:, 0, :, :], lev[:, :, :], ACT.Abs).then_inc(rka, 1)
            act.wait_ge(rka, 1)
            act.activation(gel[:, 1, :, :], gel[:, 0, :, :], ACT.Gelu).then_inc(rka, 1)

            def turned(g, u, again):
                act.wait_ge(z_pe, g + 1)
                if again:
                    act.wait_ge(y_pe, g - 1)
                act.activation(zz[:, u, :], ps[:, 2 * u:2 * u + 2, :].rearrange("p a c -> p (a c)")[:, 0:896], ACT.Copy).then_inc(z_act, 1)

            def result(g, u, again):
                act.wait_ge(y_pe, g + 1)
                act.activation(ys[:, g, :], ps[:, 4 + u, 0:D], ACT.Copy).then_inc(y_act, 1)

            for n in range(SEG):
                tiles(act, n, turned, result)

            def prepare(q, part):
                u = q % 2
                if part == "xt":
                    if q == 0:
                        act.wait_ge(s_sw, 16 * 13)
                        act.wait_ge(sset, 1)
                        act.activation(asc, asc, ACT.Exp).then_inc(sset, 1)
                    for b in (2 * q, 2 * q + 1):
                        ln_act_steps(act, 2, b, b % 2)
                    act.wait_ge(scp, after("xt", q, SCP))
                    dst = xs[:, u, 0:S].rearrange("c (p j) -> c j p", j=J)
                    act.activation(dst[:, 0:JA, :], ps[:, 6, 0:NA].rearrange("c (j p) -> c j p", p=P), ACT.Copy).then_inc(sca, 1)
                    act.activation(dst[:, JA:J, :], ps[:, 7, 0:NB].rearrange("c (j p) -> c j p", p=P), ACT.Copy).then_inc(sca, 1)
                if part == "z":
                    act.wait_ge(scp, after("z", q, SCP))
                    if q:
                        act.wait_ge(scv, after("relu", q - 1, SCV))
                    act.activation(halves(zb), ps[:, 6:8, 0:HALF], ACT.Identity, bias=bdc).then_inc(sca, 1)
                    act.wait_ge(sca, after("z", q, SCA))
                    act.activation(za, zb, ACT.Abs).then_inc(sca, 1)
                    act.wait_ge(sca, after("abs", q, SCA))
                    act.activation(za, za, ACT.Exp, scale=-1.0).then_inc(sca, 1)
                    act.wait_ge(sca, after("exp", q, SCA))
                    if q:
                        act.wait_ge(scv, after("delta", q - 1, SCV))
                    act.activation(zl, za, ACT.Ln, bias=1.0).then_inc(sca, 1)
                if part in ("b0", "c0", "b1", "c1"):
                    if part == "b0" and q:
                        act.wait_ge(xdb_vec, LANES * q)
                        act.wait_ge(hc_pool, LANES * q)
                    act.wait_ge(scp, after(part, q, SCP))
                    dst = (brep if part[0] == "b" else crep)[:, int(part[1]), :]
                    act.activation(halves(dst), ps[:, 6:8, 0:HALF], ACT.Copy).then_inc(sca, 1)

            for part in SCP:
                prepare(0, part)
            for q in range(B // 2):
                for k in range(LANES):
                    n = q * LANES + k
                    act.wait_ge(d_pe, n + 1)
                    if n >= 2:
                        act.wait_ge(scan_vec, n - 1)
                    if n == 0:
                        act.wait_ge(sset, 3)
                    act.activation(halves(da[:, n % 2, :]), ps[:, 0:2, 0:HALF], ACT.Exp, scale=asc[:, k % 8:k % 8 + 1]).then_inc(da_act, 1)
                    if q < B // 2 - 1 and k in PREP_AT:
                        for part in PREP_AT[k]:
                            prepare(q + 1, part)


            def first(b, u, again):
                act.wait_ge(mop, after("xt", b, MOP))
                act.activation(xe[:, u, 0:NA], ps[0:D + 1, 0, 0:NA], ACT.Copy).then_inc(moa, 1)
                act.activation(xe[:, u, NA:S], ps[0:D + 1, 1, 0:NB], ACT.Copy).then_inc(moa, 1)
                act.wait_ge(mov, after("sub", b, MOV))
                act.activation(small[1][:, u, :], small[0][:, u, :], ACT.Exp).then_inc(moa, 1)
                act.wait_ge(mop, after("ct", b, MOP))
                act.activation(ct[:, u, 0:NA], ps[0:EXPERTS, 0, 0:NA], ACT.Copy).then_inc(moa, 1)
                act.activation(ct[:, u, NA:S], ps[0:EXPERTS, 1, 0:NB], ACT.Copy).then_inc(moa, 1)
                for g in range(4):
                    act.wait_ge(mop, after(f"up{g}", b, MOP))
                    if g >= 2:
                        act.wait_ge(mov, after(f"gated{g - 2}", b, MOV))
                    act.activation(halves(gl[:, g % 2, :]), ps[:, 4:6, 0:HALF], ACT.Gelu).then_inc(moa, 1)

            def norm_moe(b, u, again):
                ln_act_steps(act, 3, b, u)

            skewed(act, norm_moe, first)

        @block.vector
        def _(dve):
            dve.memset(zero[:, :], 0.0).then_inc(tset, 1)
            dve.memset(rows[:, :, :], 0.0)
            dve.memset(bits[:, :, :], 1.0)
            dve.memset(xn[:, :, :, D:D + 1], 1.0).then_inc(tset, 1)
            dve.memset(eps[:, :], EPS).then_inc(s_const, 1)
            dve.memset(xi[64:65, :, :], 1.0).then_inc(s_const, 1)
            dve.wait_ge(s_cw, 48)
            two_pi = 2.0 * np.pi
            hi = float(np.float32(6.28125))
            dve.tensor_scalar(ph[:, 1, :], ph[:, 0, :], float(1.0 / two_pi), None, ALU.mult).then_inc(s_ph, 1)
            dve.wait_ge(s_ph, 1)
            dve.tensor_copy(phi[:, :], ph[:, 1, :]).then_inc(s_ph, 1)
            dve.wait_ge(s_ph, 2)
            dve.tensor_copy(ph[:, 1, :], phi[:, :]).then_inc(s_ph, 1)
            dve.wait_ge(s_ph, 3)
            dve.scalar_tensor_tensor(ph[:, 2, :], ph[:, 1, :], -hi, ph[:, 0, :], ALU.mult, ALU.add).then_inc(s_ph, 1)
            dve.wait_ge(s_ph, 4)
            dve.scalar_tensor_tensor(ph[:, 2, :], ph[:, 1, :], -float(two_pi - hi), ph[:, 2, :], ALU.mult, ALU.add).then_inc(s_ph, 1)
            dve.wait_ge(s_ph, 5)
            dve.tensor_scalar(ph[:, 2, :], ph[:, 2, :], 3.1415925, -3.1415925, ALU.min, ALU.max).then_inc(s_ph, 1)
            dve.wait_ge(s_ph, 6)
            dve.tensor_scalar(ph[:, 3, :], ph[:, 2, :], -1.0, None, ALU.mult).then_inc(s_ph, 1)
            dve.wait_ge(s_ph, 7)
            dve.tensor_tensor(ph[:, 3, :], ph[:, 2, :], ph[:, 3, :], ALU.min).then_inc(s_ph, 1)
            dve.wait_ge(s_ph, 8)
            dve.tensor_scalar(ph[:, 3, :], ph[:, 3, :], float(np.pi / 2), None, ALU.add).then_inc(s_ph, 1)
            dve.wait_ge(s_pha, 2)

            def per_tap(row):
                return ph[:, row, :].unsqueeze(2).broadcast_to([128, 8, D])
            dve.tensor_tensor(v3(wr[:, :], 8), v3(wr[:, :], 8), per_tap(5), ALU.mult).then_inc(s_ph, 1)
            dve.tensor_tensor(v3(wi[:, :], 8), v3(wi[:, :], 8), per_tap(4), ALU.mult).then_inc(s_ph, 1)
            dve.wait_ge(s_ph, 11)
            dve.tensor_tensor(weff[:, :], wr[:, :], wi[:, :], ALU.subtract).then_inc(s_ph, 1)

            dve.wait_ge(s_w, 16 * 6)

            def norm_conv(b, u, again):
                dve.wait_ge(h_set, b + 1)
                if again:
                    dve.wait_ge(xi_out[u], slot(b - 2, u))
                ln_vec_steps(dve, 0, b, u, xn[:, u, :, 0:D])

            rounds(dve, norm_conv)

            def project(b, u, again):
                dve.wait_ge(a2p, after("k", b, A2P))
                if again:
                    dve.wait_ge(a2a, after("k1", b - 2, A2A))
                dve.tensor_reduce(kmx[:, u, 0:1], ps[0:D, 0, 0:368], AX, ALU.max)
                dve.tensor_reduce(kmx[:, u, 1:2], ps[0:D, 1, 0:S - 368], AX, ALU.max).then_inc(a2v, 1)
                dve.wait_ge(a2v, after("kmax2", b, A2V))
                dve.tensor_reduce(kmx[:, u, 2:3], kmx[:, u, 0:2], AX, ALU.max, negate=True).then_inc(a2v, 1)
                dve.wait_ge(a2a, after("qv1", b, A2A))
                q = qv[:, u, :].rearrange("p (j w) -> p j w", j=J)[:, :, 0:D].rearrange("p j (g k) -> p j g k", g=HEADS)

                def heads(ap):
                    return ap.rearrange("p (j g k) -> p j g k", j=J, g=HEADS)

                def per_head(ap):
                    return ap.rearrange("p (j g) -> p j g", j=J)
                bc = [P, J, HEADS, DK]
                dve.tensor_reduce(per_head(qmx[:, u, :]), q, AX, ALU.max).then_inc(a2v, 1)
                dve.wait_ge(a2v, after("qmax", b, A2V))
                dve.tensor_tensor(heads(qs[:, u, :]), q, per_head(qmx[:, u, :]).unsqueeze(3).broadcast_to(bc),
                                  ALU.subtract).then_inc(a2v, 1)
                dve.wait_ge(a2a, after("qexp", b, A2A))
                dve.tensor_reduce(per_head(qsm[:, u, :]), heads(qe[:, u, :]), AX, ALU.add).then_inc(a2v, 1)
                dve.wait_ge(a2v, after("qsum", b, A2V))
                dve.reciprocal(qmx[:, u, :], qsm[:, u, :]).then_inc(a2v, 1)
                dve.wait_ge(a2v, after("qrec", b, A2V))
                if again:
                    dve.wait_ge(a3p, after("qt", b - 2, A3P))
                dve.tensor_tensor(heads(qn[:, u, :]), heads(qe[:, u, :]),
                                  per_head(qmx[:, u, :]).unsqueeze(3).broadcast_to(bc), ALU.mult).then_inc(a2v, 1)

            def mix(b, u, again):
                dve.wait_ge(a3p, after("qt", b, A3P))
                dve.tensor_copy(qt[:, u, 0:NA], ps[0:D, 5, 0:NA]).then_inc(a3v, 1)
                dve.tensor_copy(qt[:, u, NA:S], ps[0:D, 6, 0:NB]).then_inc(a3v, 1)
                dve.wait_ge(a3p, after("ctx", b, A3P))
                dve.tensor_tensor(ctm[:, u, :], ps[0:D, 4, 448:512], hm[:, :], ALU.mult).then_inc(a3v, 1)
                dve.tensor_tensor(kr[:, u, 0:1], ksum[:, u, 0:1], ksum[:, u, 1:2], ALU.add).then_inc(a3v, 1)
                dve.wait_ge(a3v, after("ksum", b, A3V))
                dve.reciprocal(kr[:, u, 1:2], kr[:, u, 0:1]).then_inc(a3v, 1)
                dve.wait_ge(a3v, after("krec", b, A3V))
                dve.wait_ge(a3p, after("mix", b, A3P))
                dve.tensor_scalar(mixn[:, u, :], ps[0:D, 7, 448:512], kr[:, u, 1:2], None, ALU.mult).then_inc(a3v, 1)
                dve.wait_ge(a3p, after("out", b, A3P))
                dve.tensor_tensor(h[:, b, :], ps[0:P, 7, 0:448], h[:, b, :], ALU.add).then_inc(a3v, 1)

            skewed(dve, project, mix)

            def norm_tree(b, u, again):
                if again:
                    dve.wait_ge(t1p, after("xt", b - 2, T1P))
                    dve.wait_ge(row_set, b - 1)
                ln_vec_steps(dve, 1, b, u, xn[:, u, :, 0:D])

            def scores(b, u, again):
                dve.wait_ge(t1p, after("st", b, T1P))
                dve.tensor_scalar(bits[0:INNER, u, 0:NA], ps[0:INNER, 2, 0:NA], 0.0, None, ALU.is_gt).then_inc(t1v, 1)
                dve.tensor_scalar(bits[0:INNER, u, NA:S], ps[0:INNER, 3, 0:NB], 0.0, None, ALU.is_gt).then_inc(t1v, 1)
                for q, (lo, hi) in enumerate(CHUNKS):
                    n = (hi - lo) * NODES
                    dve.wait_ge(t1a, after(f"s{q}", b, T1A))
                    dve.scalar_tensor_tensor(pick[:, u, lo * NODES:lo * NODES + n], ps[0:P, 6 + q % 2, 0:n], 0.0, scr[:, q % 2, 0:n],
                                             ALU.is_equal, ALU.mult).then_inc(t1v, 1)
                    dve.tensor_scalar(hot[:, bass.ds(b * J + lo, hi - lo), :],
                                      ps[0:P, 6 + q % 2, 0:n].rearrange("p (j n) -> p j n", n=NODES)[:, :, PRE - 1:2 * PRE - 1],
                                      0.0, None, ALU.is_equal).then_inc(t1v, 1)
                dve.wait_ge(t1v, after("hot3", b, T1V))
                for l in range(DEPTH):
                    src = pick[:, u, :].rearrange("p (j n) -> p j n", n=NODES)[:, :, 2 ** l - 1:2 ** (l + 1) - 1]
                    dve.tensor_reduce(lev[:, bass.ds(b * J, J), l], src, AX, ALU.add).then_inc(t1v, 1)

            skewed(dve, norm_tree, scores)
            n_rk = [0]

            def step(ins):
                n_rk[0] += 1
                ins.then_inc(rkv, 1)
                dve.wait_ge(rkv, n_rk[0])

            dve.wait_ge(rkp, 1)
            for q in range(4):
                step(dve.tensor_copy(tot[:, :, 14 * q:14 * q + 14].rearrange("p g i -> p i g"),
                                     ps[0:P, 4 + q, 0:448].rearrange("p (i g) -> p i g", g=PRE)))
            step(dve.tensor_reduce(cnt[:, 0, :], tot[:, :, 0:BT], AX, ALU.add))
            step(dve.tensor_scalar(cnti[:, :], cnt[:, 0, :], float(TILE - 1), None, ALU.add))
            step(dve.tensor_scalar(cnti[:, :], cnti[:, :], 7, 7, ALU.logical_shift_right, ALU.logical_shift_left))
            step(dve.tensor_copy(cnt[:, 1, :], cnti[:, :]))
            step(dve.tensor_tensor(tot[:, :, BT], cnt[:, 1, :], cnt[:, 0, :], ALU.subtract))
            tf, nf = (t[:, :, :].rearrange("p g i -> p (g i)") for t in (tot, inc))
            step(dve.tensor_tensor_scan(nf, tf, tf, 0.0, ALU.add, ALU.max))
            step(dve.tensor_tensor(tf, nf, tf, ALU.subtract))
            for q in range(4):
                step(dve.tensor_tensor(rank[:, 14 * q:14 * q + 14, :], ps[0:P, q, 0:448].rearrange("p (i g) -> p i g", g=PRE),
                                       tot[:, :, 14 * q:14 * q + 14].rearrange("p g i -> p i g"), ALU.add))
            step(dve.tensor_tensor(rank[:, :, :], rank[:, :, :], hot[:, :, :], ALU.mult))
            step(dve.tensor_reduce(slf[:, 0, :], rank[:, :, :], AX, ALU.add))
            step(dve.tensor_copy(sli[:, 0, :], slf[:, 0, :]))
            step(dve.tensor_scalar(sli[:, 1, :], sli[:, 0, :], TILE - 1, None, ALU.bitwise_and))
            step(dve.tensor_scalar(sli[:, 2, :], sli[:, 0, :], 7, None, ALU.logical_shift_right))
            step(dve.tensor_copy(slf[:, 1, :], sli[:, 1, :]))
            step(dve.tensor_copy(slf[:, 2, :], sli[:, 2, :]))
            step(dve.scalar_tensor_tensor(slf[:, 0, :], slf[:, 1, :], float(NT), slf[:, 2, :], ALU.mult, ALU.add))
            step(dve.tensor_copy(sli[:, 3, :], slf[:, 0, :]))
            dve.wait_ge(rka, 2)
            for k, (lv_, op) in enumerate(((5, ALU.is_le), (5, ALU.is_gt), (6, ALU.is_le), (6, ALU.is_gt))):
                step(dve.tensor_scalar(side[:, k, :], lev[:, :, lv_], 0.0, None, op))
            step(dve.tensor_tensor(side[:, 4, :], gel[:, 1, :, 7], side[:, 0, :], ALU.mult))
            step(dve.tensor_tensor(side[:, 5, :], gel[:, 1, :, 7], side[:, 1, :], ALU.mult))
            step(dve.tensor_copy(rows[:, :, 68:74], gel[:, 1, :, 0:6]))
            for k in range(2):
                step(dve.tensor_tensor(rows[:, :, 74 + k], gel[:, 1, :, 6], side[:, k, :], ALU.mult))
            for k in range(4):
                step(dve.tensor_tensor(rows[:, :, 76 + k], side[:, 4 + k // 2, :], side[:, 2 + k % 2, :], ALU.mult))
            assert n_rk[0] == RK_ROWS
            step(dve.tensor_tensor(cmp[:, :, :], base[:, :].unsqueeze(2).broadcast_to([1, NT, PRE]),
                                   inc[0:1, :, BT].unsqueeze(1).broadcast_to([1, NT, PRE]), ALU.is_ge))
            step(dve.tensor_reduce(pff[:, 0, :], cmp[:, :, :], AX, ALU.add))
            step(dve.tensor_scalar(pff[:, 1, :], pff[:, 0, :], float(PRE - 1), None, ALU.min))
            step(dve.tensor_copy(pfi[:, :], pff[:, 1, :]))
            assert n_rk[0] == RK_GROUPS
            step(dve.memset(zt[:, :, 768:896], 0.0))

            def spread(g, u, again):
                if again:
                    dve.wait_ge(z_pe, g - 1)
                dve.tensor_tensor(zt[:, u, 0:512].rearrange("p (s d) -> p s d", s=8),
                                  rt[:, g, 68:76].unsqueeze(2).broadcast_to([128, 8, D]),
                                  rt[:, g, 0:D].unsqueeze(1).broadcast_to([128, 8, D]), ALU.mult)
                dve.tensor_copy(zt[:, u, 768:768 + SLOTS], rt[:, g, 68:80]).then_inc(z_vec, 1)

            for n in range(SEG):
                dve.wait_ge(sorted_in[n], 16)
                tiles(dve, n, spread)
            def prepare(q, part):
                u = q % 2
                if part == "xt":
                    if q == 0:
                        dve.wait_ge(s_sw, 16 * 13)
                        dve.wait_ge(y_pe, NT)
                        dve.memset(xs[:, :, S:SW], 0.0).then_inc(sset, 1)
                        dve.wait_ge(sset, 2)
                        dve.tensor_scalar(asc, asc, -1.0, None, ALU.mult).then_inc(sset, 1)
                    for b in (2 * q, 2 * q + 1):
                        dve.wait_ge(gathered[b], 16 * J)
                        dve.tensor_tensor(h[:, b, :], yg[:, b * J:(b + 1) * J, :].rearrange("p j d -> p (j d)"), h[:, b, :],
                                          ALU.add).then_inc(h_tree, 1)
                    for b in (2 * q, 2 * q + 1):
                        dve.wait_ge(h_tree, b + 1)
                        if q:
                            dve.wait_ge(scp, after("xt", q - 1, SCP))
                        ln_vec_steps(dve, 2, b, b % 2, xp[:, :, b % 2, :])
                if part == "z":
                    dve.wait_ge(sca, after("z", q, SCA))
                    dve.tensor_scalar(zr, zb, 0.0, None, ALU.max).then_inc(scv, 1)
                    dve.wait_ge(scv, after("relu", q, SCV))
                    dve.wait_ge(sca, after("log", q, SCA))
                    if q >= 2:
                        dve.wait_ge(x_pe, LANES * (q - 1))
                    dve.tensor_tensor(dl[:, u, :], zr, zl, ALU.add).then_inc(scv, 1)
                    dve.wait_ge(scv, after("delta", q, SCV))
                    dve.tensor_tensor(xd[:, u, :], xs[:, u, :], dl[:, u, :], ALU.mult).then_inc(scv, 1)

            for part in SCP:
                prepare(0, part)
            for q in range(B // 2):
                for k in range(LANES):
                    n = q * LANES + k
                    dve.wait_ge(x_pe, n + 1)
                    if k % 8 == 0:
                        dve.wait_ge(sca, after(f"b{k // 8}", q, SCA))
                    if n >= 2:
                        dve.wait_ge(scan_vec, n - 1)
                    dve.tensor_tensor(halves(xdb[:, n % 2, :]), ps[:, 2:4, 0:HALF], halves(brep[:, k // 8, :]), ALU.mult).then_inc(xdb_vec, 1)
                    dve.wait_ge(xdb_vec, n + 1)
                    dve.wait_ge(da_act, n + 1)
                    if n >= 2:
                        dve.wait_ge(hc_pool, n - 1)
                    dve.tensor_tensor_scan(hs[:, n % 2, :], da[:, n % 2, :], xdb[:, n % 2, :], 0.0, ALU.mult, ALU.add).then_inc(scan_vec, 1)
                    if q < B // 2 - 1 and k in PREP_AT:
                        for part in PREP_AT[k]:
                            prepare(q + 1, part)
                dve.wait_ge(y_sum, LANES * (q + 1))
                if q:
                    dve.wait_ge(back_pe, q)
                dve.scalar_tensor_tensor(halves(yt), halves(xs[:, q % 2, :]), dsc, ps[:, 4:6, 0:HALF], ALU.mult, ALU.add).then_inc(fiv, 1)
                dve.wait_ge(back_pe, q + 1)
                for n, (lo, hi) in enumerate(((0, 4), (4, 7))):
                    hv = h[:, 2 * q:2 * q + 2, :].rearrange("p b (j d) -> p j b d", j=J)[:, lo:hi]
                    dve.tensor_tensor(hv, ps[0:P, 6 + n, 0:(hi - lo) * 128].rearrange("p (j b d) -> p j b d", b=2, d=D), hv,
                                      ALU.add).then_inc(fiv, 1)

            dve.wait_ge(fiv, after("h1", B // 2 - 1, FIV))
            for e in range(EXPERTS):
                dve.memset(rankw[:, e:e + 1], float(EXPERTS - e))
            dve.memset(xe[:, :, S:SW], 0.0)
            dve.memset(ct[:, :, S:SW], 0.0).then_inc(sset, 1)
            dve.wait_ge(sset, 4)

            def norm_moe(b, u, again):
                if again:
                    dve.wait_ge(mop, after("xt", b - 2, MOP))
                    dve.wait_ge(hx_pool, b - 1)
                elif b == 0:
                    dve.wait_ge(scp, after("xt", B // 2 - 1, SCP))
                ln_vec_steps(dve, 3, b, u, xn[:, u, :, 0:D])

            def first(b, u, again):
                e3 = [t[:, u, :].rearrange("p (j e) -> p j e", e=EXPERTS) for t in small]
                t2 = [t[:, u, :] for t in tiny]

                def wide(ap):
                    return ap.unsqueeze(2).broadcast_to([P, J, EXPERTS])
                rw = rankw[:, :].unsqueeze(1).broadcast_to([P, J, EXPERTS])
                lg = ps[0:P, 2, 0:J * EXPERTS].rearrange("p (j e) -> p j e", e=EXPERTS)

                def next_(name, ins):
                    ins.then_inc(mov, 1)
                    dve.wait_ge(mov, after(name, b, MOV))

                dve.wait_ge(mop, after("route", b, MOP))
                next_("max", dve.tensor_reduce(t2[0], lg, AX, ALU.max))
                next_("sub", dve.tensor_tensor(e3[0], lg, wide(t2[0]), ALU.subtract))
                dve.wait_ge(moa, after("exp", b, MOA))
                next_("sum", dve.tensor_reduce(t2[1], e3[1], AX, ALU.add))
                next_("rec", dve.reciprocal(t2[2], t2[1]))
                next_("prob", dve.tensor_tensor(e3[2], e3[1], wide(t2[2]), ALU.mult))
                next_("top1", dve.tensor_reduce(t2[3], e3[2], AX, ALU.max))
                next_("eq1", dve.tensor_tensor(e3[3], e3[2], wide(t2[3]), ALU.is_equal))
                next_("cand1", dve.tensor_tensor(e3[4], e3[3], rw, ALU.mult))
                next_("first1", dve.tensor_reduce(t2[4], e3[4], AX, ALU.max))
                next_("hot1", dve.tensor_tensor(e3[5], e3[4], wide(t2[4]), ALU.is_equal))
                next_("rest", dve.scalar_tensor_tensor(e3[6], e3[5], -2.0, e3[2], ALU.mult, ALU.add))
                next_("top2", dve.tensor_reduce(t2[5], e3[6], AX, ALU.max))
                next_("eq2", dve.tensor_tensor(e3[7], e3[6], wide(t2[5]), ALU.is_equal))
                next_("cand2", dve.tensor_tensor(e3[8], e3[7], rw, ALU.mult))
                next_("first2", dve.tensor_reduce(t2[6], e3[8], AX, ALU.max))
                next_("hot2", dve.tensor_tensor(e3[9], e3[8], wide(t2[6]), ALU.is_equal))
                next_("both", dve.tensor_tensor(e3[10], e3[5], e3[9], ALU.add))
                next_("topsum", dve.tensor_tensor(t2[7], t2[3], t2[5], ALU.add))
                next_("guard", dve.tensor_scalar(t2[8], t2[7], 1e-12, None, ALU.max))
                next_("guardrec", dve.reciprocal(t2[9], t2[8]))
                next_("kept", dve.tensor_tensor(e3[10], e3[10], e3[2], ALU.mult))
                next_("comb", dve.tensor_tensor(e3[11], e3[10], wide(t2[9]), ALU.mult))
                for g in range(4):
                    dve.wait_ge(moa, after(f"gelu{g}", b, MOA))
                    dve.wait_ge(mop, after(f"rep{g}", b, MOP))
                    dve.tensor_tensor(halves(gs[:, g, :]), halves(gl[:, g % 2, :]), ps[:, 6:8, 0:HALF], ALU.mult).then_inc(mov, 1)
                dve.wait_ge(mop, after("down", b, MOP))
                dve.wait_ge(hx_pool, b + 1)
                dve.tensor_tensor(oo[:, u, :], ps[0:P, 3, 0:448], oo[:, u, :], ALU.add).then_inc(mov, 1)

            skewed(dve, norm_moe, first)


def constants():
    c = {}
    c["head_mask"] = np.kron(np.eye(HEADS), np.ones((DK, DK))).astype(np.float32)
    c["ident"] = np.eye(128, dtype=np.float32)
    path = np.zeros((INNER + 1, NODES), np.float32)
    for n in range(NODES):
        child = n
        while child:
            parent = (child - 1) // 2
            right = child == 2 * parent + 2
            path[parent, n] = 1.0 if right else -1.0
            path[INNER, n] -= 1.0 if right else 0.0
            child = parent
    c["path"] = path
    tri = np.zeros((P, 2, P), np.float32)
    tri[:, 0, :] = np.triu(np.ones((P, P)), 1)
    tri[:, 1, :] = 1.0
    c["tri"] = tri.reshape(P, 2 * P)
    c["tile_base"] = (np.arange(NT, dtype=np.float32) * TILE).reshape(1, NT)
    sel_d = np.zeros((128, 8, 8, STATE), np.float32)
    for r in range(128):
        sel_d[r, (r % 64) // 8, r % 8, :] = 1.0
    c["sel_d"] = sel_d.reshape(128, 8 * 128)
    sel_y = np.zeros((128, 248), np.float32)
    for r in range(128):
        sel_y[r, 120 + r // STATE] = 1.0
    c["sel_y"] = sel_y
    c["sel_e"] = np.kron(np.eye(EXPERTS), np.ones((1, D))).astype(np.float32)
    return c


def layout(inputs):
    g = {k: np.asarray(v) for k, v in inputs.items()}
    a = {}
    a["x"] = g["x"].transpose(2, 0, 1)
    for name, key in (("conv_r", "L0_tok_w_real"), ("conv_i", "L0_tok_w_imag")):
        a[name] = g[key].reshape(D, D, TAPS // 2, 2).transpose(3, 1, 2, 0).reshape(128, TAPS // 2 * D)
    a["phase"] = np.repeat(g["L0_tok_phases"].reshape(TAPS // 2, 2).T, D, axis=0)
    a["att_k"] = np.concatenate([g["L0_attn_Wk"].T, g["L0_attn_bk"][None]])
    a["att_qv"] = np.concatenate([np.concatenate([g["L0_attn_Wq"].T, g["L0_attn_bq"][None]]),
                                  np.concatenate([g["L0_attn_Wv"].T, g["L0_attn_bv"][None]])], axis=1)
    a["att_r"] = g["L0_attn_Wr"].T
    a["att_i"] = np.concatenate([np.eye(D, dtype=np.float32), g["L0_attn_br"][None]])
    a["tree_1"] = np.concatenate([g["L0_ffn_w1s"].T, g["L0_ffn_b1s"][None]])
    node = np.zeros((PRE, SLOTS), np.int64)
    for q in range(PRE):
        node[q] = ([2 ** s - 1 + (q >> (5 - s)) for s in range(6)] + [63 + 2 * q + s for s in range(2)]
                   + [127 + 4 * q + s for s in range(4)])
    w2 = g["L0_ffn_w2s"][node].reshape(PRE, CH, 2, D, D)
    a["tree_2"] = w2.transpose(2, 3, 0, 1, 4).reshape(128, PRE * CH * D)
    a["tree_b2"] = g["L0_ffn_b2s"][node].transpose(1, 0, 2).reshape(SLOTS, PRE * D)
    a["ssm_a"] = g["L1_attn_A_log"].reshape(8, 8 * STATE).T
    a["ssm_b"] = np.tile(g["L1_attn_W_B"].T, (2, 8))
    a["ssm_c"] = np.tile(g["L1_attn_W_C"].T, (2, 8))
    zero = np.zeros((D, D), np.float32)
    a["ssm_dt"] = np.block([[g["L1_attn_W_delta"].T, zero], [zero, g["L1_attn_W_delta"].T]])
    a["ssm_bd"] = np.tile(g["L1_attn_b_delta"], 2)[:, None]
    a["ssm_d"] = np.tile(g["L1_attn_D_param"], 2)[:, None]
    a["moe_r"] = g["L1_ffn_router_w"].T
    w1 = g["L1_ffn_w1"].transpose(1, 0, 2).reshape(D, EXPERTS * D)
    a["moe_1"] = np.concatenate([w1, g["L1_ffn_b1"].reshape(1, EXPERTS * D)])
    a["moe_2"] = g["L1_ffn_w2"].reshape(4, 128, D).transpose(1, 0, 2).reshape(128, 4 * D)
    a["moe_b2"] = g["L1_ffn_b2"]
    return a


_ORDER = ["x", "conv_r", "conv_i", "phase", "att_k", "att_qv", "att_r", "att_i", "head_mask", "ident", "tree_1",
          "tree_2", "tree_b2", "path", "tri", "tile_base", "ssm_a", "ssm_b", "ssm_c", "ssm_dt", "ssm_bd", "ssm_d",
          "sel_d", "sel_y", "moe_r", "moe_1", "moe_2", "moe_b2", "sel_e"]


def kernel(**inputs):
    import concourse.bacc as _bacc
    from concourse.bass_utils import run_bass_kernel_spmd as _run

    nc = _bacc.Bacc("TRN2", target_bir_lowering=False, num_devices=1)
    arrays = {**layout(inputs), **constants()}
    arrays = {name: np.ascontiguousarray(arrays[name]) for name in _ORDER}
    aps = [nc.dram_tensor(f"in_{name}", a.shape, mybir.dt.from_np(a.dtype), kind="ExternalInput").ap()
           for name, a in arrays.items()]
    out = nc.dram_tensor("out", (B, S, D), F32, kind="ExternalOutput").ap()
    program(nc, *aps, out)
    r = _run(nc, [{f"in_{name}": a for name, a in arrays.items()}], core_ids=[0])
    return r.results[0]["out"]
```

```python
from contextlib import ExitStack

import numpy as np
import concourse.bass as bass
from concourse import mybir

F32 = mybir.dt.float32
BF16 = mybir.dt.bfloat16
I32 = mybir.dt.int32
ALU = mybir.AluOpType
ACT = mybir.ActivationFunctionType
AX = mybir.AxisListType.X

B, SIN, D = 8, 750, 64
TAPS = 16
S = SIN - TAPS + 1
J = 7
P = S // J
JA = 4
NA, NB = JA * P, (J - JA) * P
EPS = 1e-5
HEADS, DK = 8, 8
DEPTH = 8
NODES = 2 ** DEPTH - 1
INNER = 2 ** (DEPTH - 1) - 1
PRE = 32
SLOTS = 12
CH = SLOTS // 2
TILE = 128
NT = 78
ROW = 80
STATE = 16
EXPERTS = 8
BT = B * J
SW = S + 1
HALF = SW // 2
LANES = 16
assert (B * S + PRE * (TILE - 1)) // TILE <= NT


def after(step, times, names):
    return times * len(names) + names.index(step) + 1


def rounds(eng, body):
    for u in range(2):
        body(u, u, False)
    with eng.Fori(1, B // 2) as turn:
        for u in range(2):
            body(turn * 2 + u, u, True)


def skewed(eng, first, second):
    first(0, 0, False)
    first(1, 1, False)
    second(0, 0, False)
    first(2, 0, True)
    second(1, 1, False)
    with eng.Fori(1, B // 2 - 1) as turn:
        first(turn * 2 + 1, 1, True)
        second(turn * 2, 0, True)
        first(turn * 2 + 2, 0, True)
        second(turn * 2 + 1, 1, True)
    first(B - 1, 1, True)
    second(B - 2, 0, True)
    second(B - 1, 1, True)


def tiles(eng, seg, first, second=None):
    lo, hi = seg * SEGT, (seg + 1) * SEGT
    if second is None:
        first(lo, 0, seg > 0)
        first(lo + 1, 1, seg > 0)
        with eng.Fori(lo // 2 + 1, hi // 2) as turn:
            first(turn * 2, 0, True)
            first(turn * 2 + 1, 1, True)
        return
    first(lo, 0, seg > 0)
    first(lo + 1, 1, seg > 0)
    second(lo, 0, seg > 0)
    with eng.Fori(lo // 2 + 1, hi // 2) as turn:
        first(turn * 2, 0, True)
        second(turn * 2 - 1, 1, True)
        first(turn * 2 + 1, 1, True)
        second(turn * 2, 0, True)
    second(hi - 1, 1, True)


LN_VEC = ["sum", "mean", "centred", "square_sum", "normal"]
LN_ACT = ["square", "log", "rstd"]
A2V = ["kmax2", "nkmax", "qmax", "qsub", "qsum", "qrec", "qnorm"]
A2A = ["qv0", "qv1", "k0", "k1", "qexp"]
A2P = ["k", "qv"]
A3P = ["et", "qt", "ctx", "mix", "out"]
A3V = ["qt0", "qt1", "ctxm", "ksum", "krec", "mixn", "resid"]
A3A = ["et"]
T1P = ["xt", "st", "c0", "c1", "c2", "c3"]
SCP = ["xt", "z", "b0", "c0", "b1", "c1"]
SCA = ["xt0", "xt1", "z", "abs", "exp", "log", "b0", "c0", "b1", "c1"]
SCV = ["relu", "delta", "xd"]
SPA = ["d1", "x1", "d2", "x2"]
SPP = ["dr", "xr", "d3", "x3"]
FIV = ["skip", "h0", "h1"]
ROP = ["xa", "xb", "route", "ct"]
ROA = ["square", "log", "rstd", "xa", "xb", "exp", "ct"]
ROV = ["sum", "mean", "centred", "square_sum", "normal", "max", "sub", "sum_exp", "rec", "prob", "top1", "eq1", "cand1", "first1",
       "hot1", "rest", "top2", "eq2", "cand2", "first2", "hot2", "both", "topsum", "guard", "guardrec", "kept", "comb",
       "high", "left", "middle", "low"]
ROUTE = ["centre", "norm", "turn", "turned", "logits", "top", "back"]
ROUTE_AT = {0: "centre", 1: "norm", 2: "turn", 3: "turned", 4: "logits", 5: "top", 6: "back"}
ROUTE_AT_SCAN = {2: "centre", 4: "norm", 6: "turn", 7: "turned", 9: "logits", 10: "top", 13: "back"}
UNITS = 8
PW = P + 1
NPARTS = 3
PREP_AT = {2: ["xt"], 5: ["z", "high"], 8: ["middle"], 15: ["b0", "c0", "b1", "c1"]}
CHUNKS = [(0, 2), (2, 4), (4, 6), (6, 7)]
T1A = ["xt0", "xt1", "s0", "s1", "s2", "s3"]
T1V = ["bit0", "bit1"] + [f"{n}{q}" for q in range(4) for n in ("pick", "hot")] + [f"lev{l}" for l in range(DEPTH)]


RK_ROWS = 37
RK_GROUPS = RK_ROWS + 4
SEG = 3
SEGT = NT // SEG


def program(nc, x, conv_r, conv_i, phase, att_k, att_qv, att_r, att_i, head_mask, ident, tree_1, tree_2, tree_b2,
            path, tri, tile_base, ssm_a, ssm_b, ssm_c, ssm_dt, ssm_bd, ssm_d, sel_d, sel_y,
            moe_r, moe_1, moe_b1, moe_2, moe_b2, sel_e, out):
    with ExitStack() as ctx:
        def sb(name, shape, dt=F32):
            return ctx.enter_context(nc.sbuf_tensor(name, shape, dt))

        def region(name, words):
            whole = sb(name, [128, words])

            def phase_buffers():
                at = [0]

                def take(shape, dt=F32):
                    n = int(np.prod(shape[1:]))
                    w = n if dt != BF16 else n // 2
                    ap = whole[0:shape[0], at[0]:at[0] + w]
                    at[0] += w
                    assert at[0] <= words, (name, at[0])
                    if dt != F32:
                        ap = ap.bitcast(dt)
                    if len(shape) == 3:
                        ap = ap.rearrange("p (a b) -> p a b", a=shape[1])
                    if len(shape) == 4:
                        ap = ap.rearrange("p (a b c) -> p a b c", a=shape[1], b=shape[2])
                    return ap
                return take
            return phase_buffers

        def sem(name):
            return ctx.enter_context(nc.semaphore(name))

        xi_dram = nc.dram_tensor("xi_dram", [B, S * D], F32, kind="Internal")
        sorted_dram = nc.dram_tensor("sorted_dram", [TILE * NT, ROW], F32, kind="Internal")
        y_dram = nc.dram_tensor("y_dram", [TILE * NT, D], F32, kind="Internal")

        ps = ctx.enter_context(nc.psum_tensor("ps", [128, 8, 512], F32))
        h = sb("h", [P, B, J * D])
        eps = sb("eps", [128, 1]); idm = sb("idm", [128, 128]); idb = sb("idb", [128, 128], BF16); zero = sb("zero", [128, ROW])
        mu = sb("mu", [P, 2, J]); xc = sb("xc", [P, 2, J * D]); sq = sb("sq", [P, 2, J * D])
        vs = sb("vs", [P, 2, J]); lv = sb("lv", [P, 2, J]); rs = sb("rs", [P, 2, J])
        xn = sb("xn", [P, 2, J, D + 1])
        hot = sb("hot", [P, BT, PRE], BF16); lev = sb("lev", [P, BT, DEPTH])
        rows = sb("rows", [P, BT, ROW]); sli = sb("sli", [P, 4, BT], I32); pfi = sb("pfi", [1, NT], I32)
        w1t = sb("w1t", [65, NODES]); pth = sb("pth", [128, NODES + 1], BF16); trs = sb("trs", [P, 2 * P], BF16)
        base = sb("base", [1, NT])

        front = region("front", 13900)
        take = front()
        wr = take([128, 8 * D]); wi = take([128, 8 * D]); weff = take([128, 8 * D])
        ph = take([128, 6, 8]); phi = take([128, 8], I32); xw = take([128, 2, SIN])
        wk = take([65, D]); wqv = take([65, 2 * D]); wrt = take([D, D]); wid = take([65, D]); hm = take([D, D])
        xi = take([65, 2, S]); kmx = take([D, 2, 4]); ke = take([D, 2, S]); ksum = take([D, 2, 4])
        qv = take([P, 2, J * 2 * D]); qmx = take([P, 2, BT]); qs = take([P, 2, J * D]); qe = take([P, 2, J * D])
        qsm = take([P, 2, BT]); qn = take([P, 2, J * D]); et = take([P, 2, J * D]); qt = take([D, 2, S])
        ctm = take([D, 2, D]); kr = take([D, 2, 2]); mixn = take([D, 2, D])
        take = front()
        rt = take([128, NT, ROW]); ys = take([128, NT, D])
        take = front()
        yg = take([P, BT, D])
        take = front()
        take([P, BT, D])
        stk = take([96, 2, 4, 2 * SW], BF16)
        take = front()
        take([P, BT, D])
        take([96, 2, 4, 2 * SW], BF16)
        xe = take([128, 2, SW]); ct = take([2 * NPARTS * EXPERTS, 2, SW], BF16)
        mo1 = take([128, 2 * EXPERTS * D]); sele = take([2 * NPARTS * EXPERTS, 2 * EXPERTS * D], BF16)
        take = front()
        gl = take([128, 2, SW]); gs = take([128, 2, SW])

        mid = region("mid", 10960)
        take = mid()
        xt = take([65, 2, S]); bits = take([128, 2, S + 1], BF16)
        scr = take([P, 2, 2 * NODES]); pick = take([P, 2, J * NODES])
        take = mid()
        tot = take([P, PRE, BT + 1]); inc = take([P, PRE, BT + 1]); rank = take([P, BT, PRE]); gel = take([P, 2, BT, DEPTH])
        side = take([P, 6, BT]); cnt = take([P, 2, PRE]); cnti = take([P, PRE], I32); slf = take([P, 3, BT])
        cmp = take([1, NT, PRE]); pff = take([1, 2, NT])
        take = mid()
        zt = take([128, 2, 7 * 128]); zz = take([128, 2, 7 * 128])

        take = mid()
        asc = take([128, 8]); wb = take([128, 256]); wc = take([128, 256]); wdt = take([128, 128]); bdc = take([128, 1])
        dsc = take([128, 1]); seld = take([96, 4 * 128], BF16); rest = take([128, 2, SW]); sely = take([128, 248])
        za = take([128, SW]); zb = take([128, SW]); zl = take([128, SW]); zr = take([128, SW]); yt = take([128, SW]); xp = take([P, J, 2, D])
        mor = take([128, 2 * EXPERTS]); mb1 = take([128, 4]); mo2 = take([128, 4 * D]); mb2 = take([2 * NPARTS * EXPERTS, 2 * D])
        b2l = take([2 * NPARTS * EXPERTS, 2 * D]); b2p = take([2 * NPARTS * EXPERTS, NPARTS, 2 * D], BF16); rankw = take([P, EXPERTS])
        small = [take([P, 2 * J * EXPERTS]) for _ in range(12)]
        tiny = [take([P, 2 * J]) for _ in range(10)]
        combl = take([P, 2 * J * EXPERTS]); combp = take([P, 2 * J, NPARTS * EXPERTS], BF16)
        oo = take([P, 2, J * D])

        rear = region("rear", PRE * CH * D + PRE * D)
        take = rear()
        w2t = take([128, PRE * CH * D]); b2t = take([SLOTS, PRE * D])

        take = rear()
        xs = take([128, 2, SW]); dx = take([128, 2, SW]); part3 = take([128, 3, 2, SW], BF16); brep = take([128, 2, SW]); crep = take([128, 2, SW])
        da = take([128, 2, SW]); xdb = take([128, 2, SW]); hs = take([128, 2, SW]); hc = take([128, 2, SW])

        block = ctx.enter_context(nc.Block())
        s_w = sem("weights_in"); s_cw = sem("conv_weights_in"); s_x = [sem("xw_in0"), sem("xw_in1")]
        s_ph = sem("phase_vec"); s_pha = sem("phase_act"); s_const = sem("constants_set")
        conv_done = sem("conv_done"); h_set = sem("h_set")
        ln_vec = [sem(f"ln{n}_vec") for n in range(3)]; ln_act = [sem(f"ln{n}_act") for n in range(3)]
        xi_out = [sem("xi_out0"), sem("xi_out1")]; xi_in = [sem("xi_in0"), sem("xi_in1")]
        a2p = sem("proj_pe"); a2v = sem("proj_vec"); a2a = sem("proj_act")
        a3p = sem("mix_pe"); a3v = sem("mix_vec"); a3a = sem("mix_act")
        s_sw = sem("scan_weights_in"); sset = sem("scan_const_set"); spa = sem("parts_act"); spp = sem("parts_pool"); stk_in = [sem("stacked0"), sem("stacked1")]; s_sel = sem("selectors_in")
        scp = sem("scan_prep_pe"); sca = sem("scan_prep_act"); scv = sem("scan_prep_vec")
        d_pe = sem("delta_spread"); x_pe = sem("xdelta_spread"); da_act = sem("decay"); xdb_vec = sem("drive"); scan_vec = sem("scanned")
        hc_pool = sem("read_out"); y_sum = sem("y_sum"); fiv = sem("scan_out_vec"); back_pe = sem("back_pe")
        rop = sem("route_pe"); roa = sem("route_act"); rov = sem("route_vec"); b2_split = sem("b2_split")
        up_pe = sem("expert_up"); rep_pe = sem("weights_spread"); gelu_act = sem("expert_gelu"); gated_vec = sem("expert_gated")
        down_pe = sem("expert_down"); row_vec = sem("row_result"); hx_pool = sem("residual_pool"); row_out = [sem("row_out0"), sem("row_out1")]
        s_tw = sem("tree_weights_in"); row_set = sem("row_set"); tset = sem("tree_const_set")
        t1p = sem("score_pe"); t1a = sem("score_act"); t1v = sem("score_vec")
        rkv = sem("rank_vec"); rkp = sem("rank_pe"); rka = sem("rank_act")
        zero_out = sem("zero_out"); scattered = sem("scattered"); sorted_in = [sem(f"sorted_in{n}") for n in range(SEG)]
        z_vec = sem("z_vec"); z_pool = sem("z_pool"); z_pe = sem("z_pe"); z_act = sem("z_act"); y_pe = sem("y_pe"); y_act = sem("y_act")
        y_out = sem("y_out"); gathered = [sem(f"gathered{b}") for b in range(B)]; h_tree = sem("h_tree")
        pe_gate = sem("pe_gate")

        def slot(b, u):
            return 8 * b + 16 - 8 * u

        def halves(ap):
            return ap.rearrange("p (n w) -> p n w", n=2)

        def v3(ap, j=J):
            return ap.rearrange("p (j d) -> p j d", j=j)

        @block.sync
        def _(sp):
            sp.dma_start(wr[:, :], conv_r).then_inc(s_cw, 16)
            sp.dma_start(wi[:, :], conv_i).then_inc(s_cw, 16)
            sp.dma_start(ph[:, 0, :], phase).then_inc(s_cw, 16)

            def load_window(b, u, again):
                if again:
                    sp.wait_ge(conv_done, b - 1)
                sp.dma_start(xw[0:64, u, :], x[:, b, :]).then_inc(s_x[u], 16)
                sp.dma_start(xw[64:128, u, 0:SIN - 1], x[:, b, 1:SIN]).then_inc(s_x[u], 16)

            def store_xi(b, u, again):
                sp.wait_ge(ln_vec[0], after("normal", b, LN_VEC))
                sp.dma_start(xi_dram[b].rearrange("(p j d) -> p j d", p=P, j=J), xn[:, u, :, 0:D]).then_inc(xi_out[u], 16)

            load_window(0, 0, False)
            load_window(1, 1, False)
            sp.dma_start(idm[:, :], ident).then_inc(s_w, 16)
            sp.dma_start(wk[:, :], att_k).then_inc(s_w, 16)
            sp.dma_start(wqv[:, :], att_qv).then_inc(s_w, 16)
            sp.dma_start(wrt[:, :], att_r).then_inc(s_w, 16)
            sp.dma_start(wid[:, :], att_i).then_inc(s_w, 16)
            sp.dma_start(hm[:, :], head_mask).then_inc(s_w, 16)
            with sp.Fori(0, B // 2 - 1) as turn:
                for u in range(2):
                    load_window(turn * 2 + 2 + u, u, True)
                    store_xi(turn * 2 + u, u, True)
            store_xi(B - 2, 0, True)
            store_xi(B - 1, 1, True)

            def load_xi(b, u, again):
                sp.wait_ge(xi_out[u], slot(b, u))
                if again:
                    sp.wait_ge(a3p, after("out", b - 2, A3P))
                sp.dma_start(xi[0:D, u, :], xi_dram[b].rearrange("(c s) -> c s", c=D)).then_inc(xi_in[u], 16)

            rounds(sp, load_xi)
            for n in range(SEG):
                sp.wait_ge(scattered, 16 * BT)
                sp.dma_start(rt[:, n * SEGT:(n + 1) * SEGT, :],
                             sorted_dram.ap().rearrange("(p g) w -> p g w", p=128)[:, n * SEGT:(n + 1) * SEGT, :]
                             ).then_inc(sorted_in[n], 16)
            for n in range(SEG):
                sp.wait_ge(y_act, (n + 1) * SEGT)
                sp.dma_start(y_dram.ap().rearrange("(p g) w -> p g w", p=128)[:, n * SEGT:(n + 1) * SEGT, :],
                             ys[:, n * SEGT:(n + 1) * SEGT, :]).then_inc(y_out, 16)
            sp.wait_ge(y_pe, NT)
            sp.wait_ge(z_act, NT)
            sp.wait_ge(y_out, 16 * SEG)
            for dst, src in ((asc, ssm_a), (wb, ssm_b), (wc, ssm_c), (wdt, ssm_dt), (bdc, ssm_bd), (dsc, ssm_d),
                             (sely, sel_y), (mor, moe_r), (mo1, moe_1), (mb1, moe_b1), (mo2, moe_2), (mb2, moe_b2)):
                sp.dma_start(dst, src).then_inc(s_sw, 16)
            for q in range(B // 2):
                if q >= 2:
                    sp.wait_ge(x_pe, LANES * (q - 1))
                sp.wait_ge(spa, after("x2", q, SPA))
                sp.wait_ge(spp, after("x3", q, SPP))
                for r in range(4):
                    for i in range(3):
                        sp.dma_start(stk[32 * i:32 * i + 32, q % 2, r, :],
                                     part3[32 * r:32 * r + 32, i, :, :].rearrange("p a w -> p (a w)")).then_inc(stk_in[q % 2], 16)

            def store(b, u, again):
                sp.wait_ge(row_vec, b + 1)
                sp.dma_start(out[b].rearrange("(p j) d -> p (j d)", j=J), oo[:, u, :]).then_inc(row_out[u], 16)

            rounds(sp, store)
            sp.wait_ge(row_out[0], slot(B - 2, 0))
            sp.wait_ge(row_out[1], slot(B - 1, 1))

        @block.gpsimd
        def _(pool):
            for dst, src in ((w1t, tree_1), (pth[:, 0:NODES], path), (trs, tri), (w2t, tree_2), (b2t, tree_b2), (base, tile_base), (idb, ident)):
                pool.dma_start(dst[:, :], src).then_inc(s_tw, 16)
            pool.wait_ge(tset, 2)
            pool.dma_start(sorted_dram.ap().rearrange("(p g) w -> p g w", p=128),
                           zero[:, :].unsqueeze(1).broadcast_to([128, NT, ROW])).then_inc(zero_out, 16)

            def keep_rows(b, u, again):
                pool.wait_ge(ln_vec[1], after("normal", b, LN_VEC))
                pool.tensor_copy(rows[:, bass.ds(b * J, J), 0:D + 1], xn[:, u, :, :]).then_inc(row_set, 1)

            rounds(pool, keep_rows)
            pool.wait_ge(zero_out, 16)
            pool.wait_ge(row_set, B)
            pool.wait_ge(rkv, RK_ROWS)
            for i in range(BT):
                pool.indirect_dma_start(out=sorted_dram[:, :], out_offset=bass.IndirectOffsetOnAxis(ap=sli[:, 3, i:i + 1], axis=0),
                                        in_=rows[:, i, :], in_offset=None).then_inc(scattered, 16)

            def spread(g, u, again):
                if again:
                    pool.wait_ge(z_pe, g - 1)
                pool.tensor_tensor(zt[:, u, 512:768].rearrange("p (s d) -> p s d", s=4),
                                   rt[:, g, 76:80].unsqueeze(2).broadcast_to([128, 4, D]),
                                   rt[:, g, 0:D].unsqueeze(1).broadcast_to([128, 4, D]), ALU.mult).then_inc(z_pool, 1)

            for n in range(SEG):
                pool.wait_ge(sorted_in[n], 16)
                tiles(pool, n, spread)
            pool.wait_ge(y_out, 16 * SEG)
            pool.wait_ge(y_pe, NT)
            pool.wait_ge(z_act, NT)
            pool.dma_start(seld, sel_d).then_inc(s_sel, 16)
            pool.dma_start(sele, sel_e).then_inc(s_sel, 16)
            for b in range(B):
                for i in range(b * J, (b + 1) * J):
                    pool.indirect_dma_start(out=yg[:, i, :], out_offset=None, in_=y_dram[:, :],
                                            in_offset=bass.IndirectOffsetOnAxis(ap=sli[:, 3, i:i + 1], axis=0)).then_inc(gathered[b], 16)

            def remainders(q):
                for k, name in enumerate(("d1", "x1")):
                    pool.wait_ge(spa, after(name, q, SPA))
                    pool.tensor_tensor(rest[:, k, :], dx[:, k, :], part3[:, 0, k, :], ALU.subtract).then_inc(spp, 1)

            def low_parts(q):
                for k, name in enumerate(("d2", "x2")):
                    pool.wait_ge(spa, after(name, q, SPA))
                    pool.tensor_tensor(part3[:, 2, k, :], rest[:, k, :], part3[:, 1, k, :], ALU.subtract).then_inc(spp, 1)

            remainders(0)
            low_parts(0)
            for n in range(B // 2 * LANES):
                pool.wait_ge(scan_vec, n + 1)
                if n == 0:
                    pool.wait_ge(sca, after("c1", 0, SCA))
                elif n % LANES == 0:
                    pool.wait_ge(sca, after("c1", n // LANES, SCA))
                if n >= 2:
                    pool.wait_ge(y_sum, n - 1)
                pool.tensor_tensor(hc[:, n % 2, :], hs[:, n % 2, :], crep[:, n % LANES // 8, :], ALU.mult).then_inc(hc_pool, 1)
                if n % LANES == 6 and n // LANES < B // 2 - 1:
                    remainders(n // LANES + 1)
                if n % LANES == 9 and n // LANES < B // 2 - 1:
                    low_parts(n // LANES + 1)

            pool.wait_ge(s_sw, 16 * 12)
            pool.tensor_copy(b2p[:, 0, :], mb2).then_inc(b2_split, 1)
            pool.wait_ge(b2_split, 1)
            pool.tensor_tensor(b2l, mb2, b2p[:, 0, :], ALU.subtract).then_inc(b2_split, 1)
            pool.wait_ge(b2_split, 2)
            pool.tensor_copy(b2p[:, 1, :], b2l).then_inc(b2_split, 1)
            pool.wait_ge(b2_split, 3)
            pool.tensor_tensor(b2p[:, 2, :], b2l, b2p[:, 1, :], ALU.subtract).then_inc(b2_split, 1)

            for q in range(B // 2):
                pool.wait_ge(rov, after("normal", q, ROV))
                for r in range(2):
                    pool.tensor_tensor(v3(h[:, 2 * q + r, :]), v3(h[:, 2 * q + r, :]), xp[:, :, r, :], ALU.add).then_inc(hx_pool, 1)

        @block.tensor
        def _(pe):
            pe.wait_ge(s_ph, 12)

            def conv(b, u, again):
                pe.wait_ge(s_x[u], 2 * slot(b, u))
                if again:
                    pe.wait_ge(h_set, b - 1)
                for j in range(J):
                    for k in range(TAPS // 2):
                        last = pe.matmul(ps[0:P, u, j * D:(j + 1) * D],
                                         xw[:, u, 2 * k + j:2 * k + j + J * (P - 1) + 1:J],
                                         weff[:, k * D:(k + 1) * D], start=(k == 0), stop=(k == TAPS // 2 - 1))
                last.then_inc(conv_done, 1)

            rounds(pe, conv)

            def project(b, u, again):
                pe.wait_ge(xi_in[u], slot(b, u))
                if not again and b == 0:
                    pe.wait_ge(h_set, B)
                    pe.wait_ge(s_w, 16 * 6)
                    pe.wait_ge(s_const, 2)
                else:
                    pe.wait_ge(a2a, after("k1", b - 1, A2A))
                pe.sem_inc(pe_gate)
                for n, (lo, hi) in enumerate(((0, 368), (368, S))):
                    last = pe.matmul(ps[0:D, n, 0:hi - lo], wk[:, :], xi[:, u, lo:hi], start=True, stop=True)
                last.then_inc(a2p, 1)
                for j in range(J):
                    last = pe.matmul(ps[0:P, 2 + j // 4, (j % 4) * 128:(j % 4 + 1) * 128], xi[:, u, j::J], wqv[:, :],
                                     start=True, stop=True)
                last.then_inc(a2p, 1)

            def mix(b, u, again):
                pe.wait_ge(a2a, after("k1", b, A2A))
                if not (not again and b == 0):
                    pe.wait_ge(a3v, after("ctxm", b - 1, A3V))
                pe.sem_inc(pe_gate)
                for j in range(J):
                    last = pe.transpose(ps[0:P, 4, j * D:(j + 1) * D], ke[:, u, j::J], idm[0:D, 0:D])
                last.then_inc(a3p, 1)
                pe.wait_ge(a2v, after("qnorm", b, A2V))
                pe.sem_inc(pe_gate)
                for j in range(J):
                    last = pe.transpose(ps[0:D, 5 + j // JA, (j % JA) * P:(j % JA + 1) * P],
                                        qn[:, u, j * D:(j + 1) * D], idm[0:P, 0:P])
                last.then_inc(a3p, 1)
                pe.wait_ge(a3a, after("et", b, A3A))
                pe.sem_inc(pe_gate)
                for j in range(J):
                    last = pe.matmul(ps[0:D, 4, 448:512], qv[:, u, j * 128 + 64:(j + 1) * 128],
                                     et[:, u, j * D:(j + 1) * D], start=(j == 0), stop=(j == J - 1))
                last.then_inc(a3p, 1)
                pe.wait_ge(a3v, after("ctxm", b, A3V))
                pe.sem_inc(pe_gate)
                pe.matmul(ps[0:D, 7, 448:512], ctm[:, u, :], wrt[:, :], start=True, stop=True).then_inc(a3p, 1)
                pe.wait_ge(a3v, after("mixn", b, A3V))
                pe.sem_inc(pe_gate)
                for j in range(J):
                    pe.matmul(ps[0:P, 7, j * D:(j + 1) * D], qt[:, u, j * P:(j + 1) * P], mixn[:, u, :],
                              start=True, stop=False)
                    last = pe.matmul(ps[0:P, 7, j * D:(j + 1) * D], xi[:, u, j::J], wid[:, :], start=False, stop=True)
                last.then_inc(a3p, 1)

            skewed(pe, project, mix)

            def scores(b, u, again):
                pe.wait_ge(ln_vec[1], after("normal", b, LN_VEC))
                if not again and b == 0:
                    pe.wait_ge(a3v, after("resid", B - 1, A3V))
                    pe.wait_ge(s_tw, 16 * 7)
                    pe.wait_ge(tset, 2)
                else:
                    pe.wait_ge(t1a, after("xt1", b - 1, T1A))
                pe.sem_inc(pe_gate)
                for j in range(J):
                    last = pe.transpose(ps[0:D + 1, j // JA, (j % JA) * P:(j % JA + 1) * P], xn[:, u, j, :], idm[0:P, 0:P])
                last.then_inc(t1p, 1)
                pe.wait_ge(t1a, after("xt1", b, T1A))
                if not (not again and b == 0):
                    pe.wait_ge(t1v, after("bit1", b - 1, T1V))
                pe.sem_inc(pe_gate)
                pe.matmul(ps[0:INNER, 2, 0:NA], w1t[:, 0:INNER], xt[:, u, 0:NA], start=True, stop=True)
                pe.matmul(ps[0:INNER, 3, 0:NB], w1t[:, 0:INNER], xt[:, u, NA:S], start=True, stop=True).then_inc(t1p, 1)
                for q, (lo, hi) in enumerate(CHUNKS):
                    if q >= 2:
                        pe.wait_ge(t1a, after(f"s{q - 2}", b, T1A))
                        pe.wait_ge(t1v, after(f"hot{q - 2}", b, T1V))
                        pe.sem_inc(pe_gate)
                    elif not (not again and b == 0):
                        pe.wait_ge(t1a, after(f"s{q + 2}", b - 1, T1A))
                        pe.wait_ge(t1v, after(f"hot{q + 2}", b - 1, T1V))
                        pe.sem_inc(pe_gate)
                    for j in range(lo, hi):
                        pe.matmul(ps[0:P, 4 + q % 2, (j - lo) * NODES:(j - lo + 1) * NODES], xt[:, u, j * P:(j + 1) * P], w1t[:, :],
                                  start=True, stop=True)
                    if q == 0:
                        pe.wait_ge(t1v, after("bit1", b, T1V))
                        pe.sem_inc(pe_gate)
                    for j in range(lo, hi):
                        last = pe.matmul(ps[0:P, 6 + q % 2, (j - lo) * NODES:(j - lo + 1) * NODES],
                                         bits[:, u, j * P:(j + 1) * P], pth[:, 0:NODES], start=True, stop=True)
                    last.then_inc(t1p, 1)

            rounds(pe, scores)
            pe.wait_ge(t1v, after("lev7", B - 1, T1V))
            flat = hot[:, :, :].rearrange("p i g -> p (i g)")
            for q in range(4):
                pe.matmul(ps[0:P, q, 0:448], trs[:, 0:P], flat[:, q * 448:(q + 1) * 448], start=True, stop=True)
            for q in range(4):
                last = pe.matmul(ps[0:P, 4 + q, 0:448], trs[:, P:2 * P], flat[:, q * 448:(q + 1) * 448], start=True, stop=True)
            last.then_inc(rkp, 1)

            def turn_round(g, u, again):
                pe.wait_ge(z_vec, g + 1)
                pe.wait_ge(z_pool, g + 1)
                if again:
                    pe.wait_ge(z_act, g - 1)
                pe.sem_inc(pe_gate)
                for c in range(7):
                    last = pe.transpose(ps[:, 2 * u + c // 4, (c % 4) * 128:(c % 4 + 1) * 128],
                                        zt[:, u, c * 128:(c + 1) * 128], idm[:, :])
                last.then_inc(z_pe, 1)

            def apply(g, u, again):
                pe.wait_ge(z_act, g + 1)
                if again:
                    pe.wait_ge(y_act, g - 1)
                pe.sem_inc(pe_gate)
                group = pe.value_load(pfi[0:1, bass.ds(g, 1)], min_val=0, max_val=PRE - 1)
                w2v = w2t[:, :].rearrange("p (g c d) -> p g c d", g=PRE, c=CH)
                for c in range(CH):
                    pe.matmul(ps[:, 4 + u, 0:D], zz[:, u, c * 128:(c + 1) * 128], w2v[:, group, c, :],
                              start=(c == 0), stop=False)
                pe.matmul(ps[:, 4 + u, 0:D], zz[0:SLOTS, u, 768:896], b2t[:, :].rearrange("p (g d) -> p g d", g=PRE)[:, group, :],
                          start=False, stop=True).then_inc(y_pe, 1)

            pe.wait_ge(rkv, RK_GROUPS)
            for n in range(SEG):
                pe.wait_ge(sorted_in[n], 16)
                tiles(pe, n, turn_round, apply)

            def prepare(q, part):
                u = q % 2
                if part == "xt":
                    pe.wait_ge(ln_vec[2], after("normal", 2 * q + 1, LN_VEC))
                    if q == 0:
                        pe.wait_ge(y_act, NT)
                        pe.wait_ge(s_sw, 16 * 12)
                    if q >= 2:
                        pe.wait_ge(fiv, after("h1", q - 2, FIV))
                    for j in range(J):
                        last = pe.transpose(ps[:, 6 + j // JA, (j % JA) * P:(j % JA + 1) * P], xp[:, j, :, :].rearrange("p b d -> p (b d)"), idm[0:P, 0:P])
                    last.then_inc(scp, 1)
                if part == "z":
                    pe.wait_ge(sca, after("xt1", q, SCA))
                    pe.wait_ge(sset, 1)
                    for n in range(2):
                        last = pe.matmul(ps[:, 6 + n, 0:HALF], wdt, xs[:, u, n * HALF:(n + 1) * HALF], start=True, stop=True)
                    last.then_inc(scp, 1)
                if part in ("b0", "c0", "b1", "c1"):
                    if part == "b0":
                        pe.wait_ge(sca, after("z", q, SCA))
                    else:
                        pe.wait_ge(sca, after({"c0": "b0", "b1": "c0", "c1": "b1"}[part], q, SCA))
                    w = (wb if part[0] == "b" else wc)[:, 128 * int(part[1]):128 * int(part[1]) + 128]
                    for n in range(2):
                        last = pe.matmul(ps[:, 6 + n, 0:HALF], w, xs[:, u, n * HALF:(n + 1) * HALF],
                                         start=True, stop=True)
                    last.then_inc(scp, 1)

            def route(q, stage):
                u = q % 2
                if stage == "turn":
                    pe.wait_ge(rov, after("normal", q, ROV))
                    if q == 0:
                        pe.wait_ge(back_pe, B // 2 - 1)
                        pe.wait_ge(fiv, after("h1", B // 2 - 2, FIV))
                    else:
                        pe.wait_ge(roa, after("ct", q - 1, ROA))
                    for j in range(JA):
                        last = pe.transpose(ps[:, 7, j * P:(j + 1) * P], xp[:, j, :, :].rearrange("p b d -> p (b d)"), idm[0:P, 0:P])
                    last.then_inc(rop, 1)
                if stage == "turned":
                    pe.wait_ge(roa, after("xa", q, ROA))
                    for j in range(JA, J):
                        last = pe.transpose(ps[:, 7, (j - JA) * P:(j - JA + 1) * P], xp[:, j, :, :].rearrange("p b d -> p (b d)"),
                                            idm[0:P, 0:P])
                    last.then_inc(rop, 1)
                if stage == "logits":
                    pe.wait_ge(roa, after("xb", q, ROA))
                    for j in range(J):
                        last = pe.matmul(ps[0:P, 7, j * 2 * EXPERTS:(j + 1) * 2 * EXPERTS], xe[:, u, j * P:(j + 1) * P], mor,
                                         start=True, stop=True)
                    last.then_inc(rop, 1)
                if stage == "back":
                    pe.wait_ge(rov, after("low", q, ROV))
                    for j in range(J):
                        last = pe.transpose(ps[0:2 * NPARTS * EXPERTS, 7, 0:PW // 2 * J].bitcast(BF16)[:, j * PW:j * PW + P],
                                            combp[:, 2 * j:2 * j + 2, :].rearrange("p r e -> p (r e)"), idb[0:P, 0:P])
                    last.then_inc(rop, 1)

            for part in SCP:
                prepare(0, part)

            def sum_states(n):
                pe.wait_ge(hc_pool, n + 1)
                if n % LANES == 0 and n:
                    pe.wait_ge(fiv, after("skip", n // LANES - 1, FIV))
                for m in range(2):
                    last = pe.matmul(ps[:, 4 + m, 0:HALF], sely[:, 120 - 8 * (n % LANES):248 - 8 * (n % LANES)],
                                     hc[:, n % 2, m * HALF:(m + 1) * HALF], start=(n % LANES == 0), stop=(n % LANES == LANES - 1))
                last.then_inc(y_sum, 1)

            def back(q):
                pe.wait_ge(fiv, after("skip", q, FIV))
                if q < B // 2 - 1:
                    pe.wait_ge(sca, after("c1", q + 1, SCA))
                for j in range(J):
                    last = pe.transpose(ps[0:P, 6 + j // 4, (j % 4) * 128:(j % 4 + 1) * 128], yt[:, j:S:J], idm[:, :])
                last.then_inc(back_pe, 1)

            for q in range(B // 2):
                u = q % 2
                for k in range(LANES):
                    n = q * LANES + k
                    sel = seld[:, k % 4 * 128:(k % 4 + 1) * 128]
                    if k == 0:
                        pe.wait_ge(stk_in[u], 16 * 12 * (q // 2 + 1))
                    if n == 0:
                        pe.wait_ge(s_sel, 32)
                    if n:
                        pe.wait_ge(da_act, n)
                    for m in range(2):
                        last = pe.matmul(ps[:, m, 0:HALF], sel, stk[:, u, k // 4, m * HALF:(m + 1) * HALF],
                                         start=True, stop=True)
                    last.then_inc(d_pe, 1)
                    if n:
                        pe.wait_ge(xdb_vec, n)
                    for m in range(2):
                        last = pe.matmul(ps[:, 2 + m, 0:HALF], sel, stk[:, u, k // 4, SW + m * HALF:SW + (m + 1) * HALF],
                                         start=True, stop=True)
                    last.then_inc(x_pe, 1)
                    if k:
                        sum_states(n - 1)
                    if q < B // 2 - 1 and k in PREP_AT:
                        for part in PREP_AT[k]:
                            prepare(q + 1, part)
                    if q == B // 2 - 1 and k in ROUTE_AT_SCAN:
                        route(0, ROUTE_AT_SCAN[k])
                sum_states(q * LANES + LANES - 1)
                back(q)


            experts = range(B // 2 * UNITS)

            def up(n):
                q, k = divmod(n, UNITS)
                r, g = divmod(k, 4)
                if k == 0:
                    pe.wait_ge(roa, after("xb", q, ROA))
                if n == 0:
                    pe.wait_ge(fiv, after("h1", B // 2 - 1, FIV))
                    pe.wait_ge(da_act, B // 2 * LANES)
                if n >= 2:
                    pe.wait_ge(gelu_act, n - 1)
                for m in range(2):
                    last = pe.matmul(ps[:, 2 * (n % 2) + m, 0:HALF], mo1[:, (4 * r + g) * 128:(4 * r + g + 1) * 128],
                                     xe[:, q % 2, m * HALF:(m + 1) * HALF], start=True, stop=True)
                last.then_inc(up_pe, 1)

            def spread_weights(n):
                q, k = divmod(n, UNITS)
                if k == 0:
                    pe.wait_ge(roa, after("ct", q, ROA))
                if n:
                    pe.wait_ge(gated_vec, n)
                for m in range(2):
                    last = pe.matmul(ps[:, 4 + m, 0:HALF], sele[:, k * 128:(k + 1) * 128], ct[:, q % 2, m * HALF:(m + 1) * HALF],
                                     start=True, stop=True)
                last.then_inc(rep_pe, 1)

            def down(n):
                q, k = divmod(n, UNITS)
                r, g = divmod(k, 4)
                pe.wait_ge(gated_vec, n + 1)
                if g == 0 and n:
                    pe.wait_ge(row_vec, n // 4)
                if n == 3:
                    pe.wait_ge(b2_split, 4)
                for j in range(J):
                    o = ps[0:P, 6, j * D:(j + 1) * D]
                    last = pe.matmul(o, gs[:, n % 2, j * P:(j + 1) * P], mo2[:, g * D:(g + 1) * D], start=(g == 0 and j == 0), stop=False)
                    for i in range(NPARTS if g == 3 else 0):
                        last = pe.matmul(o, ct[:, q % 2, j * P:(j + 1) * P], b2p[:, i, r * D:(r + 1) * D],
                                         start=False, stop=(j == J - 1 and i == NPARTS - 1))
                last.then_inc(down_pe, 1)

            up(0)
            for n in experts:
                spread_weights(n)
                if n:
                    down(n - 1)
                if n + 1 < len(experts):
                    up(n + 1)
                q, k = divmod(n, UNITS)
                if q < B // 2 - 1 and k in ROUTE_AT:
                    route(q + 1, ROUTE_AT[k])
            down(len(experts) - 1)

        def ln_act_steps(act, n, b, u):
            act.wait_ge(ln_vec[n], after("centred", b, LN_VEC))
            act.activation(sq[:, u, :], xc[:, u, :], ACT.Square).then_inc(ln_act[n], 1)
            act.wait_ge(ln_vec[n], after("square_sum", b, LN_VEC))
            act.activation(lv[:, u, :], vs[:, u, :], ACT.Ln, bias=eps[0:P, :], scale=1.0 / D).then_inc(ln_act[n], 1)
            act.wait_ge(ln_act[n], after("log", b, LN_ACT))
            act.activation(rs[:, u, :], lv[:, u, :], ACT.Exp, scale=-0.5).then_inc(ln_act[n], 1)

        def ln_vec_steps(dve, n, b, u, dst):
            src = v3(h[:, b, :])
            dve.tensor_reduce(mu[:, u, :], src, AX, ALU.add).then_inc(ln_vec[n], 1)
            dve.wait_ge(ln_vec[n], after("sum", b, LN_VEC))
            dve.tensor_scalar(mu[:, u, :], mu[:, u, :], 1.0 / D, None, ALU.mult).then_inc(ln_vec[n], 1)
            dve.wait_ge(ln_vec[n], after("mean", b, LN_VEC))
            dve.tensor_tensor(v3(xc[:, u, :]), src, mu[:, u, :].unsqueeze(2).broadcast_to([P, J, D]),
                              ALU.subtract).then_inc(ln_vec[n], 1)
            dve.wait_ge(ln_act[n], after("square", b, LN_ACT))
            dve.tensor_reduce(vs[:, u, :], v3(sq[:, u, :]), AX, ALU.add).then_inc(ln_vec[n], 1)
            dve.wait_ge(ln_act[n], after("rstd", b, LN_ACT))
            dve.tensor_tensor(dst, v3(xc[:, u, :]), rs[:, u, :].unsqueeze(2).broadcast_to([P, J, D]),
                              ALU.mult).then_inc(ln_vec[n], 1)

        @block.scalar
        def _(act):
            act.wait_ge(s_ph, 9)
            act.activation(ph[:, 4, :], ph[:, 2, :], ACT.Sin).then_inc(s_pha, 1)
            act.activation(ph[:, 5, :], ph[:, 3, :], ACT.Sin).then_inc(s_pha, 1)
            act.wait_ge(s_const, 2)

            def conv_out(b, u, again):
                act.wait_ge(conv_done, b + 1)
                act.activation(h[:, b, :], ps[0:P, u, 0:448], ACT.Copy).then_inc(h_set, 1)
                ln_act_steps(act, 0, b, u)

            rounds(act, conv_out)

            def project(b, u, again):
                act.wait_ge(a2p, after("qv", b, A2P))
                if again:
                    act.wait_ge(a3p, after("ctx", b - 2, A3P))
                act.activation(qv[:, u, 0:512], ps[0:P, 2, :], ACT.Copy).then_inc(a2a, 1)
                act.activation(qv[:, u, 512:896], ps[0:P, 3, 0:384], ACT.Copy).then_inc(a2a, 1)
                act.wait_ge(a2v, after("nkmax", b, A2V))
                if again:
                    act.wait_ge(a3v, after("ksum", b - 2, A3V))
                act.activation(ke[:, u, 0:368], ps[0:D, 0, 0:368], ACT.Exp, bias=kmx[:, u, 2:3],
                               accum_out=ksum[:, u, 0:1]).then_inc(a2a, 1)
                act.activation(ke[:, u, 368:S], ps[0:D, 1, 0:S - 368], ACT.Exp, bias=kmx[:, u, 2:3],
                               accum_out=ksum[:, u, 1:2]).then_inc(a2a, 1)
                act.wait_ge(a2v, after("qsub", b, A2V))
                act.activation(qe[:, u, :], qs[:, u, :], ACT.Exp).then_inc(a2a, 1)

            def mix(b, u, again):
                act.wait_ge(a3p, after("et", b, A3P))
                act.activation(et[:, u, :], ps[0:P, 4, 0:448], ACT.Copy).then_inc(a3a, 1)

            skewed(act, project, mix)

            def norm_tree(b, u, again):
                ln_act_steps(act, 1, b, u)

            def scores(b, u, again):
                act.wait_ge(t1p, after("xt", b, T1P))
                act.activation(xt[:, u, 0:NA], ps[0:D + 1, 0, 0:NA], ACT.Copy).then_inc(t1a, 1)
                act.activation(xt[:, u, NA:S], ps[0:D + 1, 1, 0:NB], ACT.Copy).then_inc(t1a, 1)
                for q, (lo, hi) in enumerate(CHUNKS):
                    act.wait_ge(t1p, after(f"c{q}", b, T1P))
                    if q >= 2:
                        act.wait_ge(t1v, after(f"pick{q - 2}", b, T1V))
                    elif not (not again and b == 0):
                        act.wait_ge(t1v, after(f"pick{q + 2}" if q == 0 else "pick3", b - 1, T1V))
                    n = (hi - lo) * NODES
                    act.activation(scr[:, q % 2, 0:n], ps[0:P, 4 + q % 2, 0:n], ACT.Copy).then_inc(t1a, 1)

            skewed(act, norm_tree, scores)
            act.wait_ge(t1v, after("lev7", B - 1, T1V))
            act.activation(gel[:, 0, :, :], lev[:, :, :], ACT.Abs).then_inc(rka, 1)
            act.wait_ge(rka, 1)
            act.activation(gel[:, 1, :, :], gel[:, 0, :, :], ACT.Gelu).then_inc(rka, 1)

            def turned(g, u, again):
                act.wait_ge(z_pe, g + 1)
                if again:
                    act.wait_ge(y_pe, g - 1)
                act.activation(zz[:, u, :], ps[:, 2 * u:2 * u + 2, :].rearrange("p a c -> p (a c)")[:, 0:896], ACT.Copy).then_inc(z_act, 1)

            def result(g, u, again):
                act.wait_ge(y_pe, g + 1)
                act.activation(ys[:, g, :], ps[:, 4 + u, 0:D], ACT.Copy).then_inc(y_act, 1)

            for n in range(SEG):
                tiles(act, n, turned, result)

            def prepare(q, part):
                u = q % 2
                if part == "xt":
                    if q == 0:
                        act.wait_ge(s_sw, 16 * 12)
                        act.wait_ge(sset, 1)
                        act.activation(asc, asc, ACT.Exp).then_inc(sset, 1)
                    for b in (2 * q, 2 * q + 1):
                        ln_act_steps(act, 2, b, b % 2)
                    act.wait_ge(scp, after("xt", q, SCP))
                    dst = xs[:, u, 0:S].rearrange("c (p j) -> c j p", j=J)
                    act.activation(dst[:, 0:JA, :], ps[:, 6, 0:NA].rearrange("c (j p) -> c j p", p=P), ACT.Copy).then_inc(sca, 1)
                    act.activation(dst[:, JA:J, :], ps[:, 7, 0:NB].rearrange("c (j p) -> c j p", p=P), ACT.Copy).then_inc(sca, 1)
                if part == "z":
                    act.wait_ge(scp, after("z", q, SCP))
                    if q:
                        act.wait_ge(scv, after("relu", q - 1, SCV))
                    act.activation(halves(zb), ps[:, 6:8, 0:HALF], ACT.Identity, bias=bdc).then_inc(sca, 1)
                    act.wait_ge(sca, after("z", q, SCA))
                    act.activation(za, zb, ACT.Abs).then_inc(sca, 1)
                    act.wait_ge(sca, after("abs", q, SCA))
                    act.activation(za, za, ACT.Exp, scale=-1.0).then_inc(sca, 1)
                    act.wait_ge(sca, after("exp", q, SCA))
                    if q:
                        act.wait_ge(scv, after("delta", q - 1, SCV))
                    act.activation(zl, za, ACT.Ln, bias=1.0).then_inc(sca, 1)
                if part == "high":
                    if q:
                        act.wait_ge(stk_in[(q - 1) % 2], 16 * 12 * ((q - 1) // 2 + 1))
                    for k, name in enumerate(("delta", "xd")):
                        act.wait_ge(scv, after(name, q, SCV))
                        act.activation(part3[:, 0, k, :], dx[:, k, :], ACT.Copy).then_inc(spa, 1)
                if part == "middle":
                    for k, name in enumerate(("dr", "xr")):
                        act.wait_ge(spp, after(name, q, SPP))
                        act.activation(part3[:, 1, k, :], rest[:, k, :], ACT.Copy).then_inc(spa, 1)
                if part in ("b0", "c0", "b1", "c1"):
                    if part == "b0" and q:
                        act.wait_ge(xdb_vec, LANES * q)
                        act.wait_ge(hc_pool, LANES * q)
                    act.wait_ge(scp, after(part, q, SCP))
                    dst = (brep if part[0] == "b" else crep)[:, int(part[1]), :]
                    act.activation(halves(dst), ps[:, 6:8, 0:HALF], ACT.Copy).then_inc(sca, 1)

            def route(q, stage):
                u = q % 2
                if stage == "centre":
                    act.wait_ge(rov, after("centred", q, ROV))
                    act.activation(sq[:, :, :], xc[:, :, :], ACT.Square).then_inc(roa, 1)
                if stage == "norm":
                    act.wait_ge(rov, after("square_sum", q, ROV))
                    act.activation(lv[:, :, :], vs[:, :, :], ACT.Ln, bias=eps[0:P, :], scale=1.0 / D).then_inc(roa, 1)
                    act.wait_ge(roa, after("log", q, ROA))
                    act.activation(rs[:, :, :], lv[:, :, :], ACT.Exp, scale=-0.5).then_inc(roa, 1)
                if stage == "turn":
                    act.wait_ge(rop, after("xa", q, ROP))
                    act.activation(xe[:, u, 0:NA], ps[:, 7, 0:NA], ACT.Copy).then_inc(roa, 1)
                if stage == "turned":
                    act.wait_ge(rop, after("xb", q, ROP))
                    act.activation(xe[:, u, NA:S], ps[:, 7, 0:NB], ACT.Copy).then_inc(roa, 1)
                if stage == "logits":
                    act.wait_ge(rov, after("sub", q, ROV))
                    act.activation(small[1], small[0], ACT.Exp).then_inc(roa, 1)
                if stage == "back":
                    act.wait_ge(rop, after("ct", q, ROP))
                    act.activation(v3(ct[:, u, 0:S]), v3(ps[0:2 * NPARTS * EXPERTS, 7, 0:PW // 2 * J].bitcast(BF16))[:, :, 0:P], ACT.Copy).then_inc(roa, 1)

            for part in ("xt", "z", "high", "middle", "b0", "c0", "b1", "c1"):
                prepare(0, part)
            for q in range(B // 2):
                for k in range(LANES):
                    n = q * LANES + k
                    act.wait_ge(d_pe, n + 1)
                    if n >= 2:
                        act.wait_ge(scan_vec, n - 1)
                    if n == 0:
                        act.wait_ge(sset, 3)
                    act.activation(halves(da[:, n % 2, :]), ps[:, 0:2, 0:HALF], ACT.Exp, scale=asc[:, k % 8:k % 8 + 1]).then_inc(da_act, 1)
                    if q < B // 2 - 1 and k in PREP_AT:
                        for part in PREP_AT[k]:
                            prepare(q + 1, part)
                    if q == B // 2 - 1 and k in ROUTE_AT_SCAN:
                        route(0, ROUTE_AT_SCAN[k])


            for n in range(B // 2 * UNITS):
                q, k = divmod(n, UNITS)
                act.wait_ge(up_pe, n + 1)
                if n == 0:
                    act.wait_ge(fiv, after("h1", B // 2 - 1, FIV))
                if n >= 2:
                    act.wait_ge(gated_vec, n - 1)
                act.activation(halves(gl[:, n % 2, :]), ps[:, 2 * (n % 2):2 * (n % 2) + 2, 0:HALF], ACT.Gelu,
                               bias=mb1[:, k % 4:k % 4 + 1]).then_inc(gelu_act, 1)
                if q < B // 2 - 1 and k in ROUTE_AT:
                    route(q + 1, ROUTE_AT[k])

        @block.vector
        def _(dve):
            dve.memset(zero[:, :], 0.0).then_inc(tset, 1)
            dve.memset(rows[:, :, :], 0.0)
            dve.memset(bits[:, :, :], 1.0)
            dve.memset(xn[:, :, :, D:D + 1], 1.0).then_inc(tset, 1)
            dve.memset(eps[:, :], EPS).then_inc(s_const, 1)
            dve.memset(xi[64:65, :, :], 1.0).then_inc(s_const, 1)
            dve.wait_ge(s_cw, 48)
            two_pi = 2.0 * np.pi
            hi = float(np.float32(6.28125))
            dve.tensor_scalar(ph[:, 1, :], ph[:, 0, :], float(1.0 / two_pi), None, ALU.mult).then_inc(s_ph, 1)
            dve.wait_ge(s_ph, 1)
            dve.tensor_copy(phi[:, :], ph[:, 1, :]).then_inc(s_ph, 1)
            dve.wait_ge(s_ph, 2)
            dve.tensor_copy(ph[:, 1, :], phi[:, :]).then_inc(s_ph, 1)
            dve.wait_ge(s_ph, 3)
            dve.scalar_tensor_tensor(ph[:, 2, :], ph[:, 1, :], -hi, ph[:, 0, :], ALU.mult, ALU.add).then_inc(s_ph, 1)
            dve.wait_ge(s_ph, 4)
            dve.scalar_tensor_tensor(ph[:, 2, :], ph[:, 1, :], -float(two_pi - hi), ph[:, 2, :], ALU.mult, ALU.add).then_inc(s_ph, 1)
            dve.wait_ge(s_ph, 5)
            dve.tensor_scalar(ph[:, 2, :], ph[:, 2, :], 3.1415925, -3.1415925, ALU.min, ALU.max).then_inc(s_ph, 1)
            dve.wait_ge(s_ph, 6)
            dve.tensor_scalar(ph[:, 3, :], ph[:, 2, :], -1.0, None, ALU.mult).then_inc(s_ph, 1)
            dve.wait_ge(s_ph, 7)
            dve.tensor_tensor(ph[:, 3, :], ph[:, 2, :], ph[:, 3, :], ALU.min).then_inc(s_ph, 1)
            dve.wait_ge(s_ph, 8)
            dve.tensor_scalar(ph[:, 3, :], ph[:, 3, :], float(np.pi / 2), None, ALU.add).then_inc(s_ph, 1)
            dve.wait_ge(s_pha, 2)

            def per_tap(row):
                return ph[:, row, :].unsqueeze(2).broadcast_to([128, 8, D])
            dve.tensor_tensor(v3(wr[:, :], 8), v3(wr[:, :], 8), per_tap(5), ALU.mult).then_inc(s_ph, 1)
            dve.tensor_tensor(v3(wi[:, :], 8), v3(wi[:, :], 8), per_tap(4), ALU.mult).then_inc(s_ph, 1)
            dve.wait_ge(s_ph, 11)
            dve.tensor_tensor(weff[:, :], wr[:, :], wi[:, :], ALU.subtract).then_inc(s_ph, 1)

            dve.wait_ge(s_w, 16 * 6)

            def norm_conv(b, u, again):
                dve.wait_ge(h_set, b + 1)
                if again:
                    dve.wait_ge(xi_out[u], slot(b - 2, u))
                ln_vec_steps(dve, 0, b, u, xn[:, u, :, 0:D])

            rounds(dve, norm_conv)

            def project(b, u, again):
                dve.wait_ge(a2p, after("k", b, A2P))
                if again:
                    dve.wait_ge(a2a, after("k1", b - 2, A2A))
                dve.tensor_reduce(kmx[:, u, 0:1], ps[0:D, 0, 0:368], AX, ALU.max)
                dve.tensor_reduce(kmx[:, u, 1:2], ps[0:D, 1, 0:S - 368], AX, ALU.max).then_inc(a2v, 1)
                dve.wait_ge(a2v, after("kmax2", b, A2V))
                dve.tensor_reduce(kmx[:, u, 2:3], kmx[:, u, 0:2], AX, ALU.max, negate=True).then_inc(a2v, 1)
                dve.wait_ge(a2a, after("qv1", b, A2A))
                q = qv[:, u, :].rearrange("p (j w) -> p j w", j=J)[:, :, 0:D].rearrange("p j (g k) -> p j g k", g=HEADS)

                def heads(ap):
                    return ap.rearrange("p (j g k) -> p j g k", j=J, g=HEADS)

                def per_head(ap):
                    return ap.rearrange("p (j g) -> p j g", j=J)
                bc = [P, J, HEADS, DK]
                dve.tensor_reduce(per_head(qmx[:, u, :]), q, AX, ALU.max).then_inc(a2v, 1)
                dve.wait_ge(a2v, after("qmax", b, A2V))
                dve.tensor_tensor(heads(qs[:, u, :]), q, per_head(qmx[:, u, :]).unsqueeze(3).broadcast_to(bc),
                                  ALU.subtract).then_inc(a2v, 1)
                dve.wait_ge(a2a, after("qexp", b, A2A))
                dve.tensor_reduce(per_head(qsm[:, u, :]), heads(qe[:, u, :]), AX, ALU.add).then_inc(a2v, 1)
                dve.wait_ge(a2v, after("qsum", b, A2V))
                dve.reciprocal(qmx[:, u, :], qsm[:, u, :]).then_inc(a2v, 1)
                dve.wait_ge(a2v, after("qrec", b, A2V))
                if again:
                    dve.wait_ge(a3p, after("qt", b - 2, A3P))
                dve.tensor_tensor(heads(qn[:, u, :]), heads(qe[:, u, :]),
                                  per_head(qmx[:, u, :]).unsqueeze(3).broadcast_to(bc), ALU.mult).then_inc(a2v, 1)

            def mix(b, u, again):
                dve.wait_ge(a3p, after("qt", b, A3P))
                dve.tensor_copy(qt[:, u, 0:NA], ps[0:D, 5, 0:NA]).then_inc(a3v, 1)
                dve.tensor_copy(qt[:, u, NA:S], ps[0:D, 6, 0:NB]).then_inc(a3v, 1)
                dve.wait_ge(a3p, after("ctx", b, A3P))
                dve.tensor_tensor(ctm[:, u, :], ps[0:D, 4, 448:512], hm[:, :], ALU.mult).then_inc(a3v, 1)
                dve.tensor_tensor(kr[:, u, 0:1], ksum[:, u, 0:1], ksum[:, u, 1:2], ALU.add).then_inc(a3v, 1)
                dve.wait_ge(a3v, after("ksum", b, A3V))
                dve.reciprocal(kr[:, u, 1:2], kr[:, u, 0:1]).then_inc(a3v, 1)
                dve.wait_ge(a3v, after("krec", b, A3V))
                dve.wait_ge(a3p, after("mix", b, A3P))
                dve.tensor_scalar(mixn[:, u, :], ps[0:D, 7, 448:512], kr[:, u, 1:2], None, ALU.mult).then_inc(a3v, 1)
                dve.wait_ge(a3p, after("out", b, A3P))
                dve.tensor_tensor(h[:, b, :], ps[0:P, 7, 0:448], h[:, b, :], ALU.add).then_inc(a3v, 1)

            skewed(dve, project, mix)

            def norm_tree(b, u, again):
                if again:
                    dve.wait_ge(t1p, after("xt", b - 2, T1P))
                    dve.wait_ge(row_set, b - 1)
                ln_vec_steps(dve, 1, b, u, xn[:, u, :, 0:D])

            def scores(b, u, again):
                dve.wait_ge(t1p, after("st", b, T1P))
                dve.tensor_scalar(bits[0:INNER, u, 0:NA], ps[0:INNER, 2, 0:NA], 0.0, None, ALU.is_gt).then_inc(t1v, 1)
                dve.tensor_scalar(bits[0:INNER, u, NA:S], ps[0:INNER, 3, 0:NB], 0.0, None, ALU.is_gt).then_inc(t1v, 1)
                for q, (lo, hi) in enumerate(CHUNKS):
                    n = (hi - lo) * NODES
                    dve.wait_ge(t1a, after(f"s{q}", b, T1A))
                    dve.scalar_tensor_tensor(pick[:, u, lo * NODES:lo * NODES + n], ps[0:P, 6 + q % 2, 0:n], 0.0, scr[:, q % 2, 0:n],
                                             ALU.is_equal, ALU.mult).then_inc(t1v, 1)
                    dve.tensor_scalar(hot[:, bass.ds(b * J + lo, hi - lo), :],
                                      ps[0:P, 6 + q % 2, 0:n].rearrange("p (j n) -> p j n", n=NODES)[:, :, PRE - 1:2 * PRE - 1],
                                      0.0, None, ALU.is_equal).then_inc(t1v, 1)
                dve.wait_ge(t1v, after("hot3", b, T1V))
                for l in range(DEPTH):
                    src = pick[:, u, :].rearrange("p (j n) -> p j n", n=NODES)[:, :, 2 ** l - 1:2 ** (l + 1) - 1]
                    dve.tensor_reduce(lev[:, bass.ds(b * J, J), l], src, AX, ALU.add).then_inc(t1v, 1)

            skewed(dve, norm_tree, scores)
            n_rk = [0]

            def step(ins):
                n_rk[0] += 1
                ins.then_inc(rkv, 1)
                dve.wait_ge(rkv, n_rk[0])

            dve.wait_ge(rkp, 1)
            for q in range(4):
                step(dve.tensor_copy(tot[:, :, 14 * q:14 * q + 14].rearrange("p g i -> p i g"),
                                     ps[0:P, 4 + q, 0:448].rearrange("p (i g) -> p i g", g=PRE)))
            step(dve.tensor_reduce(cnt[:, 0, :], tot[:, :, 0:BT], AX, ALU.add))
            step(dve.tensor_scalar(cnti[:, :], cnt[:, 0, :], float(TILE - 1), None, ALU.add))
            step(dve.tensor_scalar(cnti[:, :], cnti[:, :], 7, 7, ALU.logical_shift_right, ALU.logical_shift_left))
            step(dve.tensor_copy(cnt[:, 1, :], cnti[:, :]))
            step(dve.tensor_tensor(tot[:, :, BT], cnt[:, 1, :], cnt[:, 0, :], ALU.subtract))
            tf, nf = (t[:, :, :].rearrange("p g i -> p (g i)") for t in (tot, inc))
            step(dve.tensor_tensor_scan(nf, tf, tf, 0.0, ALU.add, ALU.max))
            step(dve.tensor_tensor(tf, nf, tf, ALU.subtract))
            for q in range(4):
                step(dve.tensor_tensor(rank[:, 14 * q:14 * q + 14, :], ps[0:P, q, 0:448].rearrange("p (i g) -> p i g", g=PRE),
                                       tot[:, :, 14 * q:14 * q + 14].rearrange("p g i -> p i g"), ALU.add))
            step(dve.tensor_tensor(rank[:, :, :], rank[:, :, :], hot[:, :, :], ALU.mult))
            step(dve.tensor_reduce(slf[:, 0, :], rank[:, :, :], AX, ALU.add))
            step(dve.tensor_copy(sli[:, 0, :], slf[:, 0, :]))
            step(dve.tensor_scalar(sli[:, 1, :], sli[:, 0, :], TILE - 1, None, ALU.bitwise_and))
            step(dve.tensor_scalar(sli[:, 2, :], sli[:, 0, :], 7, None, ALU.logical_shift_right))
            step(dve.tensor_copy(slf[:, 1, :], sli[:, 1, :]))
            step(dve.tensor_copy(slf[:, 2, :], sli[:, 2, :]))
            step(dve.scalar_tensor_tensor(slf[:, 0, :], slf[:, 1, :], float(NT), slf[:, 2, :], ALU.mult, ALU.add))
            step(dve.tensor_copy(sli[:, 3, :], slf[:, 0, :]))
            dve.wait_ge(rka, 2)
            for k, (lv_, op) in enumerate(((5, ALU.is_le), (5, ALU.is_gt), (6, ALU.is_le), (6, ALU.is_gt))):
                step(dve.tensor_scalar(side[:, k, :], lev[:, :, lv_], 0.0, None, op))
            step(dve.tensor_tensor(side[:, 4, :], gel[:, 1, :, 7], side[:, 0, :], ALU.mult))
            step(dve.tensor_tensor(side[:, 5, :], gel[:, 1, :, 7], side[:, 1, :], ALU.mult))
            step(dve.tensor_copy(rows[:, :, 68:74], gel[:, 1, :, 0:6]))
            for k in range(2):
                step(dve.tensor_tensor(rows[:, :, 74 + k], gel[:, 1, :, 6], side[:, k, :], ALU.mult))
            for k in range(4):
                step(dve.tensor_tensor(rows[:, :, 76 + k], side[:, 4 + k // 2, :], side[:, 2 + k % 2, :], ALU.mult))
            assert n_rk[0] == RK_ROWS
            step(dve.tensor_tensor(cmp[:, :, :], base[:, :].unsqueeze(2).broadcast_to([1, NT, PRE]),
                                   inc[0:1, :, BT].unsqueeze(1).broadcast_to([1, NT, PRE]), ALU.is_ge))
            step(dve.tensor_reduce(pff[:, 0, :], cmp[:, :, :], AX, ALU.add))
            step(dve.tensor_scalar(pff[:, 1, :], pff[:, 0, :], float(PRE - 1), None, ALU.min))
            step(dve.tensor_copy(pfi[:, :], pff[:, 1, :]))
            assert n_rk[0] == RK_GROUPS
            step(dve.memset(zt[:, :, 768:896], 0.0))

            def spread(g, u, again):
                if again:
                    dve.wait_ge(z_pe, g - 1)
                dve.tensor_tensor(zt[:, u, 0:512].rearrange("p (s d) -> p s d", s=8),
                                  rt[:, g, 68:76].unsqueeze(2).broadcast_to([128, 8, D]),
                                  rt[:, g, 0:D].unsqueeze(1).broadcast_to([128, 8, D]), ALU.mult)
                dve.tensor_copy(zt[:, u, 768:768 + SLOTS], rt[:, g, 68:80]).then_inc(z_vec, 1)

            for n in range(SEG):
                dve.wait_ge(sorted_in[n], 16)
                tiles(dve, n, spread)
            def prepare(q, part):
                u = q % 2
                if part == "xt":
                    if q == 0:
                        dve.wait_ge(s_sw, 16 * 12)
                        dve.wait_ge(y_pe, NT)
                        dve.memset(xs[:, :, S:SW], 0.0).then_inc(sset, 1)
                        dve.wait_ge(sset, 2)
                        dve.tensor_scalar(asc, asc, -1.0, None, ALU.mult).then_inc(sset, 1)
                    for b in (2 * q, 2 * q + 1):
                        dve.wait_ge(gathered[b], 16 * J)
                        dve.tensor_tensor(h[:, b, :], yg[:, b * J:(b + 1) * J, :].rearrange("p j d -> p (j d)"), h[:, b, :],
                                          ALU.add).then_inc(h_tree, 1)
                    for b in (2 * q, 2 * q + 1):
                        dve.wait_ge(h_tree, b + 1)
                        if q:
                            dve.wait_ge(scp, after("xt", q - 1, SCP))
                        ln_vec_steps(dve, 2, b, b % 2, xp[:, :, b % 2, :])
                if part == "z":
                    dve.wait_ge(sca, after("z", q, SCA))
                    dve.tensor_scalar(zr, zb, 0.0, None, ALU.max).then_inc(scv, 1)
                    dve.wait_ge(scv, after("relu", q, SCV))
                    dve.wait_ge(sca, after("log", q, SCA))
                    if q:
                        dve.wait_ge(spp, after("xr", q - 1, SPP))
                    dve.tensor_tensor(dx[:, 0, :], zr, zl, ALU.add).then_inc(scv, 1)
                    dve.wait_ge(scv, after("delta", q, SCV))
                    dve.tensor_tensor(dx[:, 1, :], xs[:, u, :], dx[:, 0, :], ALU.mult).then_inc(scv, 1)

            def route(q, stage):
                def pair(ap):
                    return ap.rearrange("p b (j d) -> p b j d", j=J)

                def wide(ap, n):
                    return ap.unsqueeze(len(ap.shape)).broadcast_to(list(ap.shape) + [n])

                def next_(name, ins):
                    ins.then_inc(rov, 1)
                    dve.wait_ge(rov, after(name, q, ROV))

                src = pair(h[:, 2 * q:2 * q + 2, :])
                e3 = [t.rearrange("p (j e) -> p j e", e=EXPERTS) for t in small]
                rw = rankw[:, :].unsqueeze(1).broadcast_to([P, 2 * J, EXPERTS])
                lg = ps[0:P, 7, 0:2 * J * EXPERTS].rearrange("p (j e) -> p j e", e=EXPERTS)
                if stage == "centre":
                    if q == 0:
                        dve.wait_ge(scp, after("xt", B // 2 - 1, SCP))
                        for e in range(EXPERTS):
                            dve.memset(rankw[:, e:e + 1], float(EXPERTS - e))
                        dve.memset(xe[:, :, S:SW], 0.0)
                        dve.memset(ct[:, :, S:SW], 0.0).then_inc(sset, 1)
                        dve.wait_ge(sset, 4)
                    dve.wait_ge(fiv, after("h1", q, FIV))
                    next_("sum", dve.tensor_reduce(mu[:, :, :], src, AX, ALU.add))
                    next_("mean", dve.tensor_scalar(mu[:, :, :], mu[:, :, :], 1.0 / D, None, ALU.mult))
                    dve.tensor_tensor(pair(xc[:, :, :]), src, wide(mu[:, :, :], D), ALU.subtract).then_inc(rov, 1)
                if stage == "norm":
                    dve.wait_ge(roa, after("square", q, ROA))
                    dve.tensor_reduce(vs[:, :, :], pair(sq[:, :, :]), AX, ALU.add).then_inc(rov, 1)
                if stage == "turn":
                    dve.wait_ge(roa, after("rstd", q, ROA))
                    if q:
                        dve.wait_ge(hx_pool, 2 * q)
                        dve.wait_ge(rop, after("xb", q - 1, ROP))
                    dve.tensor_tensor(xp.rearrange("p j b d -> p b j d"), pair(xc[:, :, :]), wide(rs[:, :, :], D),
                                      ALU.mult).then_inc(rov, 1)
                if stage == "logits":
                    dve.wait_ge(rop, after("route", q, ROP))
                    next_("max", dve.tensor_reduce(tiny[0], lg, AX, ALU.max))
                    dve.tensor_tensor(e3[0], lg, wide(tiny[0], EXPERTS), ALU.subtract).then_inc(rov, 1)
                if stage == "top":
                    dve.wait_ge(roa, after("exp", q, ROA))
                    next_("sum_exp", dve.tensor_reduce(tiny[1], e3[1], AX, ALU.add))
                    next_("rec", dve.reciprocal(tiny[2], tiny[1]))
                    next_("prob", dve.tensor_tensor(e3[2], e3[1], wide(tiny[2], EXPERTS), ALU.mult))
                    next_("top1", dve.tensor_reduce(tiny[3], e3[2], AX, ALU.max))
                    next_("eq1", dve.tensor_tensor(e3[3], e3[2], wide(tiny[3], EXPERTS), ALU.is_equal))
                    next_("cand1", dve.tensor_tensor(e3[4], e3[3], rw, ALU.mult))
                    next_("first1", dve.tensor_reduce(tiny[4], e3[4], AX, ALU.max))
                    next_("hot1", dve.tensor_tensor(e3[5], e3[4], wide(tiny[4], EXPERTS), ALU.is_equal))
                    next_("rest", dve.scalar_tensor_tensor(e3[6], e3[5], -2.0, e3[2], ALU.mult, ALU.add))
                    next_("top2", dve.tensor_reduce(tiny[5], e3[6], AX, ALU.max))
                    next_("eq2", dve.tensor_tensor(e3[7], e3[6], wide(tiny[5], EXPERTS), ALU.is_equal))
                    next_("cand2", dve.tensor_tensor(e3[8], e3[7], rw, ALU.mult))
                    next_("first2", dve.tensor_reduce(tiny[6], e3[8], AX, ALU.max))
                    next_("hot2", dve.tensor_tensor(e3[9], e3[8], wide(tiny[6], EXPERTS), ALU.is_equal))
                    next_("both", dve.tensor_tensor(e3[10], e3[5], e3[9], ALU.add))
                    next_("topsum", dve.tensor_tensor(tiny[7], tiny[3], tiny[5], ALU.add))
                    next_("guard", dve.tensor_scalar(tiny[8], tiny[7], 1e-12, None, ALU.max))
                    next_("guardrec", dve.reciprocal(tiny[9], tiny[8]))
                    next_("kept", dve.tensor_tensor(e3[10], e3[10], e3[2], ALU.mult))
                    next_("comb", dve.tensor_tensor(e3[11], e3[10], wide(tiny[9], EXPERTS), ALU.mult))
                    if q:
                        dve.wait_ge(rop, after("ct", q - 1, ROP))
                    left = combl.rearrange("p (j e) -> p j e", e=EXPERTS)
                    high, middle, low = (combp[:, :, i * EXPERTS:(i + 1) * EXPERTS] for i in range(NPARTS))
                    next_("high", dve.tensor_copy(high, e3[11]))
                    next_("left", dve.tensor_tensor(left, e3[11], high, ALU.subtract))
                    next_("middle", dve.tensor_copy(middle, left))
                    dve.tensor_tensor(low, left, middle, ALU.subtract).then_inc(rov, 1)

            def row_result(b):
                dve.wait_ge(down_pe, 4 * b + 4)
                dve.wait_ge(hx_pool, b + 1)
                if b >= 2:
                    dve.wait_ge(row_out[b % 2], slot(b - 2, b % 2))
                dve.tensor_tensor(oo[:, b % 2, :], ps[0:P, 6, 0:448], h[:, b, :], ALU.add).then_inc(row_vec, 1)

            for part in SCP:
                prepare(0, part)
            for q in range(B // 2):
                for k in range(LANES):
                    n = q * LANES + k
                    dve.wait_ge(x_pe, n + 1)
                    if k % 8 == 0:
                        dve.wait_ge(sca, after(f"b{k // 8}", q, SCA))
                    if n >= 2:
                        dve.wait_ge(scan_vec, n - 1)
                    dve.tensor_tensor(halves(xdb[:, n % 2, :]), ps[:, 2:4, 0:HALF], halves(brep[:, k // 8, :]), ALU.mult).then_inc(xdb_vec, 1)
                    dve.wait_ge(xdb_vec, n + 1)
                    dve.wait_ge(da_act, n + 1)
                    if n >= 2:
                        dve.wait_ge(hc_pool, n - 1)
                    dve.tensor_tensor_scan(hs[:, n % 2, :], da[:, n % 2, :], xdb[:, n % 2, :], 0.0, ALU.mult, ALU.add).then_inc(scan_vec, 1)
                    if q < B // 2 - 1 and k in PREP_AT:
                        for part in PREP_AT[k]:
                            prepare(q + 1, part)
                    if q == B // 2 - 1 and k in ROUTE_AT_SCAN:
                        route(0, ROUTE_AT_SCAN[k])
                dve.wait_ge(y_sum, LANES * (q + 1))
                if q:
                    dve.wait_ge(back_pe, q)
                dve.scalar_tensor_tensor(halves(yt), halves(xs[:, q % 2, :]), dsc, ps[:, 4:6, 0:HALF], ALU.mult, ALU.add).then_inc(fiv, 1)
                dve.wait_ge(back_pe, q + 1)
                for n, (lo, hi) in enumerate(((0, 4), (4, 7))):
                    hv = h[:, 2 * q:2 * q + 2, :].rearrange("p b (j d) -> p j b d", j=J)[:, lo:hi]
                    dve.tensor_tensor(hv, ps[0:P, 6 + n, 0:(hi - lo) * 128].rearrange("p (j b d) -> p j b d", b=2, d=D), hv,
                                      ALU.add).then_inc(fiv, 1)

            for n in range(B // 2 * UNITS):
                q, k = divmod(n, UNITS)
                dve.wait_ge(gelu_act, n + 1)
                dve.wait_ge(rep_pe, n + 1)
                if n >= 2:
                    dve.wait_ge(down_pe, n - 1)
                dve.tensor_tensor(halves(gs[:, n % 2, :]), halves(gl[:, n % 2, :]), ps[:, 4:6, 0:HALF], ALU.mult).then_inc(gated_vec, 1)
                if q < B // 2 - 1 and k in ROUTE_AT:
                    route(q + 1, ROUTE_AT[k])
                if k % 4 == 0 and n:
                    row_result(n // 4 - 1)
            row_result(B - 1)


def constants():
    c = {}
    c["head_mask"] = np.kron(np.eye(HEADS), np.ones((DK, DK))).astype(np.float32)
    c["ident"] = np.eye(128, dtype=np.float32)
    path = np.zeros((INNER + 1, NODES), np.float32)
    for n in range(NODES):
        child = n
        while child:
            parent = (child - 1) // 2
            right = child == 2 * parent + 2
            path[parent, n] = 1.0 if right else -1.0
            path[INNER, n] -= 1.0 if right else 0.0
            child = parent
    c["path"] = path
    tri = np.zeros((P, 2, P), np.float32)
    tri[:, 0, :] = np.triu(np.ones((P, P)), 1)
    tri[:, 1, :] = 1.0
    c["tri"] = tri.reshape(P, 2 * P)
    c["tile_base"] = (np.arange(NT, dtype=np.float32) * TILE).reshape(1, NT)
    sel_d = np.zeros((96, 4, 8, STATE), np.float32)
    for r in range(96):
        sel_d[r, (r % 32) // 8, r % 8, :] = 1.0
    c["sel_d"] = sel_d.reshape(96, 4 * 128)
    sel_y = np.zeros((128, 248), np.float32)
    for r in range(128):
        sel_y[r, 120 + r // STATE] = 1.0
    c["sel_y"] = sel_y
    one = np.tile(np.kron(np.eye(EXPERTS), np.ones((1, D))), (NPARTS, 1))
    c["sel_e"] = np.kron(np.eye(2), one).astype(np.float32)
    return c


def layout(inputs):
    g = {k: np.asarray(v) for k, v in inputs.items()}
    a = {}
    a["x"] = g["x"].transpose(2, 0, 1)
    for name, key in (("conv_r", "L0_tok_w_real"), ("conv_i", "L0_tok_w_imag")):
        a[name] = g[key].reshape(D, D, TAPS // 2, 2).transpose(3, 1, 2, 0).reshape(128, TAPS // 2 * D)
    a["phase"] = np.repeat(g["L0_tok_phases"].reshape(TAPS // 2, 2).T, D, axis=0)
    a["att_k"] = np.concatenate([g["L0_attn_Wk"].T, g["L0_attn_bk"][None]])
    a["att_qv"] = np.concatenate([np.concatenate([g["L0_attn_Wq"].T, g["L0_attn_bq"][None]]),
                                  np.concatenate([g["L0_attn_Wv"].T, g["L0_attn_bv"][None]])], axis=1)
    a["att_r"] = g["L0_attn_Wr"].T
    a["att_i"] = np.concatenate([np.eye(D, dtype=np.float32), g["L0_attn_br"][None]])
    a["tree_1"] = np.concatenate([g["L0_ffn_w1s"].T, g["L0_ffn_b1s"][None]])
    node = np.zeros((PRE, SLOTS), np.int64)
    for q in range(PRE):
        node[q] = ([2 ** s - 1 + (q >> (5 - s)) for s in range(6)] + [63 + 2 * q + s for s in range(2)]
                   + [127 + 4 * q + s for s in range(4)])
    w2 = g["L0_ffn_w2s"][node].reshape(PRE, CH, 2, D, D)
    a["tree_2"] = w2.transpose(2, 3, 0, 1, 4).reshape(128, PRE * CH * D)
    a["tree_b2"] = g["L0_ffn_b2s"][node].transpose(1, 0, 2).reshape(SLOTS, PRE * D)
    a["ssm_a"] = g["L1_attn_A_log"].reshape(8, 8 * STATE).T
    zero = np.zeros((D, D), np.float32)
    for name, key in (("ssm_b", "L1_attn_W_B"), ("ssm_c", "L1_attn_W_C")):
        w = np.tile(g[key].T, (1, 8))
        a[name] = np.block([[w, np.zeros_like(w)], [np.zeros_like(w), w]])
    a["ssm_dt"] = np.block([[g["L1_attn_W_delta"].T, zero], [zero, g["L1_attn_W_delta"].T]])
    a["ssm_bd"] = np.tile(g["L1_attn_b_delta"], 2)[:, None]
    a["ssm_d"] = np.tile(g["L1_attn_D_param"], 2)[:, None]
    def two_rows(w):
        return np.block([[w, np.zeros_like(w)], [np.zeros_like(w), w]])

    a["moe_r"] = two_rows(g["L1_ffn_router_w"].T)
    a["moe_1"] = two_rows(g["L1_ffn_w1"].transpose(1, 0, 2).reshape(D, EXPERTS * D))
    a["moe_b1"] = g["L1_ffn_b1"].reshape(4, 128).T
    a["moe_2"] = g["L1_ffn_w2"].reshape(4, 128, D).transpose(1, 0, 2).reshape(128, 4 * D)
    a["moe_b2"] = two_rows(np.tile(g["L1_ffn_b2"], (NPARTS, 1)))
    return a


_ORDER = ["x", "conv_r", "conv_i", "phase", "att_k", "att_qv", "att_r", "att_i", "head_mask", "ident", "tree_1",
          "tree_2", "tree_b2", "path", "tri", "tile_base", "ssm_a", "ssm_b", "ssm_c", "ssm_dt", "ssm_bd", "ssm_d",
          "sel_d", "sel_y", "moe_r", "moe_1", "moe_b1", "moe_2", "moe_b2", "sel_e"]


def kernel(**inputs):
    import concourse.bacc as _bacc
    from concourse.bass_utils import run_bass_kernel_spmd as _run

    nc = _bacc.Bacc("TRN2", target_bir_lowering=False, num_devices=1)
    arrays = {**layout(inputs), **constants()}
    arrays = {name: np.ascontiguousarray(arrays[name]) for name in _ORDER}
    aps = [nc.dram_tensor(f"in_{name}", a.shape, mybir.dt.from_np(a.dtype), kind="ExternalInput").ap()
           for name, a in arrays.items()]
    out = nc.dram_tensor("out", (B, S, D), F32, kind="ExternalOutput").ap()
    program(nc, *aps, out)
    r = _run(nc, [{f"in_{name}": a for name, a in arrays.items()}], core_ids=[0])
    return r.results[0]["out"]
```

```python
from contextlib import ExitStack

import numpy as np
import concourse.bass as bass
from concourse import mybir

F32 = mybir.dt.float32
BF16 = mybir.dt.bfloat16
I32 = mybir.dt.int32
ALU = mybir.AluOpType
ACT = mybir.ActivationFunctionType
AX = mybir.AxisListType.X

B, SIN, D = 8, 750, 64
TAPS = 16
S = SIN - TAPS + 1
J = 7
P = S // J
JA = 4
NA, NB = JA * P, (J - JA) * P
EPS = 1e-5
ROOT = D ** -0.5
HEADS, DK = 8, 8
DEPTH = 8
NODES = 2 ** DEPTH - 1
INNER = 2 ** (DEPTH - 1) - 1
PRE = 32
SLOTS = 12
CH = SLOTS // 2
TILE = 128
NT = 80
NPARTS = 3
WS = NPARTS * SLOTS // 2
PROD = NPARTS * NPARTS * SLOTS
GW = CH * D + D // 2
ROW = D + WS
STATE = 16
EXPERTS = 8
BT = B * J
SW = S + 1
HALF = SW // 2
LANES = 16
ORDER = [8 * r + k + 4 * i for r in range(2) for k in range(4) for i in range(2)]
assert (B * S + PRE * (TILE - 1)) // TILE <= NT and NT % 4 == 0


def after(step, times, names):
    return times * len(names) + names.index(step) + 1


def rounds(eng, body):
    for u in range(2):
        body(u, u, False)
    with eng.Fori(1, B // 2) as turn:
        for u in range(2):
            body(turn * 2 + u, u, True)


def wait(eng, sem, count):
    if not isinstance(count, int) or count > 0:
        eng.wait_ge(sem, count)


def has(b):
    return not isinstance(b, int) or 0 <= b < B


def pipelined(eng, step):
    for b in range(-2, 2):
        step(b, b % 2)
    with eng.Fori(1, B // 2 - 1) as turn:
        for u in range(2):
            step(turn * 2 + u, u)
    for b in range(B - 2, B):
        step(b, b % 2)


def pairs(eng, lo, hi, body, peeled=2):
    for t in range(lo, lo + peeled):
        body(t, t % 2)
    with eng.Fori((lo + peeled) // 2, hi // 2) as turn:
        for p in range(2):
            body(turn * 2 + p, p)


LN_VEC = ["sum", "mean", "centred", "var", "normal"]
LN_ACT = ["square"]
CENTRE = ["sum", "mean", "centred"]
A2V = ["kmax2", "nkmax", "qmax", "qsub", "qsum", "qrec", "qnorm"]
A2A = ["qv0", "qv1", "k0", "k1", "qexp"]
A2P = ["k", "qv"]
A3P = ["et", "qt", "ctx", "mix", "out"]
A3V = ["qt0", "qt1", "ctxm", "ksum", "krec", "mixn", "resid"]
A3A = ["et"]
T1F = ["xt", "st"]
T1P = ["c0", "c1", "c2", "c3"]
SCP = ["xt", "z", "b0", "c0", "b1", "c1"]
SCA = ["xt0", "xt1", "z", "abs", "exp", "log", "b0", "c0", "b1", "c1"]
SCV = ["relu", "delta", "xd"]
SPA = ["d1", "x1", "d2", "x2"]
SPP = ["dr", "xr", "d3", "x3"]
FIV = ["skip", "h0", "h1"]
ROP = ["xa", "xb", "route", "ct"]
ROA = ["square", "xa", "xb", "exp", "ct"]
ROV = ["sum", "mean", "centred", "var", "normal", "max", "sub", "sum_exp", "rec", "prob", "top1", "eq1", "cand1", "first1",
       "hot1", "rest", "top2", "eq2", "cand2", "first2", "hot2", "both", "topsum", "guard", "guardrec", "kept", "comb",
       "high", "left", "middle", "low"]
ROUTE_AT = {1: "centre", 3: "norm", 6: "turn", 8: "turned", 9: "logits", 10: "top", 12: "second", 14: "back"}
ROUTE_AT_SCAN = {5: "centre", 6: "norm", 8: "turn", 9: "turned", 10: "logits", 11: "top", 12: "second", 13: "back"}
UNITS = 16
BACK_AT = {4: 0, 6: 1}
TOKENS_J = [(0, 4), (4, J)]
PW = P + 1
PREP_AT = {4: ["centre"], 5: ["norm"], 7: ["turn"], 8: ["turned"], 9: ["z"], 10: ["softplus"], 11: ["delta"], 12: ["high"],
           13: ["middle"], 14: ["b0", "c0"]}
FIRST_PREP = [part for parts in PREP_AT.values() for part in parts]
SKIP_AT, BACK_LANE, ROWS_AT, SECOND_AT = 3, 4, 5, 6
CHUNKS = [(0, 2), (2, 4), (4, 6), (6, 7)]
T1X = ["xt0", "xt1"]
T1A = ["s0", "s1", "s2", "s3"]
T1B = ["bit0", "bit1"]
T1V = [f"{n}{q}" for q in range(4) for n in ("pick", "hot")] + [f"lev{l}" for l in range(DEPTH)]


RK_ROWS = 24
RK_GROUPS = RK_ROWS + 7
PW_STEPS = 17
RK_B2 = RK_GROUPS + 7
SEG = 4
SEGT = NT // SEG
PAIRS = NT // 2


def program(nc, x, conv_r, conv_i, phase, att_k, att_qv, att_r, att_i, head_mask, ident, tree_1, tree_2, tree_b2,
            path, sel_w, part_masks, tri, tile_base, ssm_a, ssm_b, ssm_c, ssm_dt, ssm_bd, ssm_d, sel_d, sel_y,
            moe_r, moe_1, moe_b1, moe_2, moe_b2, sel_e, out):
    with ExitStack() as ctx:
        def sb(name, shape, dt=F32):
            return ctx.enter_context(nc.sbuf_tensor(name, shape, dt))

        def region(name, words):
            whole = sb(name, [128, words])

            def phase_buffers():
                at = [0]

                def take(shape, dt=F32):
                    n = int(np.prod(shape[1:]))
                    w = n if dt != BF16 else n // 2
                    ap = whole[0:shape[0], at[0]:at[0] + w]
                    at[0] += w
                    assert at[0] <= words, (name, at[0])
                    if dt != F32:
                        ap = ap.bitcast(dt)
                    if len(shape) == 3:
                        ap = ap.rearrange("p (a b) -> p a b", a=shape[1])
                    if len(shape) == 4:
                        ap = ap.rearrange("p (a b c) -> p a b c", a=shape[1], b=shape[2])
                    return ap
                return take
            return phase_buffers

        def sem(name):
            return ctx.enter_context(nc.semaphore(name))

        xi_dram = nc.dram_tensor("xi_dram", [B, S * D], F32, kind="Internal")
        sorted_dram = nc.dram_tensor("sorted_dram", [TILE * NT, ROW], F32, kind="Internal")
        y_dram = nc.dram_tensor("y_dram", [TILE * NT, D], F32, kind="Internal")

        ps = ctx.enter_context(nc.psum_tensor("ps", [128, 8, 512], F32))
        h = sb("h", [P, B, J * D])
        idm = sb("idm", [128, 128]); idb = sb("idb", [128, 128], BF16); zero = sb("zero", [128, ROW])
        mu = sb("mu", [P, 2, J]); xc = sb("xc", [P, 2, J * D]); sq = sb("sq", [P, 2, J * D])
        vs = sb("vs", [P, 2, J]); rs = sb("rs", [P, 2, J]); power = sb("power", [P, 2, J])
        xn = sb("xn", [P, 2, J, D + 1])
        hot = sb("hot", [P, BT, PRE], BF16); lev = sb("lev", [P, BT, DEPTH])
        rows_all = sb("rows", [128, BT, ROW]); rows = rows_all[0:P, :, :]; sli = sb("sli", [P, 4, BT], I32); packed = sb("packed", [1, NT // 4], I32)
        selw = sb("selw", [PROD, CH * 128], BF16)
        w1t = sb("w1t", [128, NODES]); pth = sb("pth", [128, NODES + 1], BF16); trs = sb("trs", [P, 2 * P], BF16)
        base = sb("base", [1, NT]); masks = sb("masks", [PROD, NPARTS])

        front = region("front", 13900)
        take = front()
        wr = take([128, 8 * D]); wi = take([128, 8 * D]); weff = take([128, 8 * D])
        ph = take([128, 6, 8]); phi = take([128, 8], I32)
        wk = take([128, D]); wqv = take([128, 2 * D]); wrt = take([D, D]); wid = take([128, D]); hm = take([D, D])
        xi = take([128, 2, S]); kmx = take([D, 2, 4]); ke = take([D, 2, S]); ksum = take([D, 2, 4])
        qv = take([P, 2, J * 2 * D]); qmx = take([P, 2, BT]); qs = take([P, 2, J * D]); qe = take([P, 2, J * D])
        qsm = take([P, 2, BT]); qn = take([P, 2, J * D]); et = take([P, 2, J * D]); qt = take([D, 2, S])
        ctm = take([D, 2, D]); kr = take([D, 2, 2]); mixn = take([D, 2, D])
        take = front()
        rt = take([128, NT, ROW]); ys = take([128, NT, D])
        take = front()
        yg = take([P, BT, D])
        take = front()
        take([P, BT, D])
        stk = take([96, 2, 4, 2 * SW], BF16)
        take = front()
        take([P, BT, D])
        take([96, 2, 4, 2 * SW], BF16)
        xe = take([128, 2, SW]); ct = take([2 * NPARTS * EXPERTS, 2, SW], BF16)
        mo1 = take([128, 2 * EXPERTS * D]); sele = take([2 * NPARTS * EXPERTS, 2 * EXPERTS * D], BF16)
        take = front()
        gl = take([128, 2, HALF]); gs = take([128, 4, HALF]); ye = take([128, SW])

        mid = region("mid", 11000)
        take = mid()
        xt = take([128, 2, S]); bits = take([128, 2, S + 1], BF16)
        scr = take([P, 2, 2 * NODES]); pick = take([P, 2, J * NODES])
        xw = take([128, 4, SIN]); yc = take([128, S])
        take = mid()
        tot = take([P, PRE, BT + 1]); inc = take([P, PRE, BT + 1]); rank = take([P, BT, PRE]); gel = take([P, 2, BT, DEPTH])
        side = take([P, 6, BT]); cnt = take([P, 2, PRE]); cnti = take([P, PRE], I32); slf = take([P, 3, BT])
        cmp = take([1, NT, PRE]); pff = take([1, 2, NT])
        pw = take([P, BT, SLOTS]); pwl = take([P, BT, SLOTS])
        take = mid()
        xx = take([128, 4, 2 * D]); ws = take([128, 4, NPARTS * WS]); xxt = take([128, 4, TILE]); wt = take([PROD, 4, TILE], BF16)
        zz = take([128, 4, CH * TILE]); gw = take([128, 4, GW]); yb = take([128, 2, TILE])
        take = mid()
        b2t = take([PROD, PRE * D]); b2left = take([PROD, PRE * D]); b2h = take([PROD, NPARTS, PRE * D], BF16)

        take = mid()
        asc = take([128, 8]); wb = take([128, 256]); wc = take([128, 256]); wdt = take([128, 128]); bdc = take([128, 1])
        dsc = take([128, 1]); seld = take([96, 4 * 128], BF16); rest = take([128, 2, SW]); sely = take([128, 56])
        za = take([128, SW]); zb = take([128, SW]); zl = take([128, SW]); zr = take([128, SW]); yt = take([128, SW]); xp = take([P, J, 2, D])
        mor = take([128, 2 * EXPERTS]); mb1 = take([128, 4]); mo2 = take([128, 4 * D]); mb2 = take([2 * NPARTS * EXPERTS, 2 * D])
        b2l = take([2 * NPARTS * EXPERTS, 2 * D]); b2p = take([2 * NPARTS * EXPERTS, NPARTS, 2 * D], BF16); rankw = take([P, EXPERTS])
        small = [take([P, 2 * J * EXPERTS]) for _ in range(12)]
        tiny = [take([P, 2 * J]) for _ in range(10)]
        combl = take([P, 2 * J * EXPERTS]); combp = take([P, 2 * J, NPARTS * EXPERTS], BF16)
        oo = take([P, 2, J * D])

        rear = region("rear", PRE * CH * D + PRE * D)
        take = rear()
        w2t = take([128, PRE, GW])

        take = rear()
        xs = take([128, 2, SW]); dx = take([128, 2, SW]); part3 = take([128, 3, 2, SW], BF16); brep = take([128, 2, SW]); crep = take([128, 2, SW])
        da = take([128, 2, SW]); xdb = take([128, 2, SW]); hs = take([128, 2, SW])
        hc = rows_all[:, :, :].rearrange("p i w -> p (i w)")[:, 0:4 * SW].rearrange("p (a w) -> p a w", a=4)

        block = ctx.enter_context(nc.Block())
        s_w = sem("weights_in"); s_cw = sem("conv_weights_in"); s_x = [sem("xw_in0"), sem("xw_in1")]
        s_ph = sem("phase_vec"); s_pha = sem("phase_act"); s_const = sem("constants_set")
        c_centre = sem("conv_ln_centre"); c_square = sem("conv_ln_square"); c_var = sem("conv_ln_var"); c_rstd = sem("conv_ln_rstd"); c_normal = sem("conv_ln_normal")
        conv_done = sem("conv_done"); yc_act = sem("conv_out"); back_h = sem("conv_turned_back"); h_set = sem("h_set")
        ln_vec = [sem(f"ln{n}_vec") for n in range(3)]; ln_act = [sem(f"ln{n}_act") for n in range(3)]; ln_pool = [sem(f"ln{n}_pool") for n in range(3)]
        xi_out = [sem("xi_out0"), sem("xi_out1")]; xi_in = [sem("xi_in0"), sem("xi_in1")]
        a2p = sem("proj_pe"); a2v = sem("proj_vec"); a2a = sem("proj_act")
        a3p = sem("mix_pe"); a3v = sem("mix_vec"); a3a = sem("mix_act")
        s_sw = sem("scan_weights_in"); sset = sem("scan_const_set"); spa = sem("parts_act"); spp = sem("parts_pool"); stk_in = [sem("stacked0"), sem("stacked1")]; s_sel = sem("selectors_in")
        scp = sem("scan_prep_pe"); sca = sem("scan_prep_act"); scv = sem("scan_prep_vec")
        d_pe = sem("delta_spread"); x_pe = sem("xdelta_spread"); da_act = sem("decay"); xdb_vec = sem("drive"); scan_vec = sem("scanned")
        hc_pool = sem("read_out"); y_sum = sem("y_sum"); fiv = sem("scan_out_vec"); back_pe = sem("back_pe")
        rop = sem("route_pe"); roa = sem("route_act"); rov = sem("route_vec"); rstd_pool = sem("route_rstd"); b2_split = sem("b2_split")
        up_pe = sem("expert_up"); rep_pe = sem("weights_spread"); gelu_act = sem("expert_gelu"); gated_vec = sem("expert_gated")
        down_pe = sem("expert_down"); ye_act = sem("experts_out"); back_e = sem("experts_turned_back"); row_vec = sem("row_result"); hx_pool = sem("residual_pool"); row_out = sem("row_out")
        s_tw = sem("tree_weights_in"); s_w2 = sem("node_weights_in"); row_set = sem("row_set"); tset = sem("tree_const_set")
        t1f = sem("turn_score_pe"); t1x = sem("turned_score_act"); t1b = sem("bits_vec"); t1p = sem("score_pe"); t1a = sem("score_act"); t1v = sem("score_vec")
        rkv = sem("rank_vec"); rkp = sem("rank_pe"); rka = sem("rank_act")
        zero_out = sem("zero_out"); scattered = sem("scattered"); sorted_in = [sem(f"sorted_in{n}") for n in range(SEG)]
        pwp = sem("path_weights_pool"); xx_pool = sem("tile_doubled"); turn_pe = sem("tile_turned"); wt_act = sem("turned_weights_out")
        xxt_act = sem("turned_tokens_out"); spread_pe = sem("weights_spread_tile"); begun_pe = sem("y_begun"); s_b2 = sem("b2_in"); z_vec = sem("products")
        y_pe = sem("y_pe"); yb_act = sem("y_channels_out"); back_y = sem("y_turned_back"); y_act = sem("y_act")
        y_out = sem("y_out"); gathered = [sem(f"gathered{b}") for b in range(B)]; h_tree = sem("h_tree")
        pool_gate = sem("pool_gate")
        pe_gate = sem("pe_gate")

        def slot(b, u):
            return 8 * b + 16 - 8 * u

        def halves(ap):
            return ap.rearrange("p (n w) -> p n w", n=2)

        def v3(ap, j=J):
            return ap.rearrange("p (j d) -> p j d", j=j)

        @block.sync
        def _(sp):
            sp.dma_start(wr[:, :], conv_r).then_inc(s_cw, 16)
            sp.dma_start(wi[:, :], conv_i).then_inc(s_cw, 16)
            sp.dma_start(ph[:, 0, :], phase).then_inc(s_cw, 16)

            def load_windows(q):
                if q >= 2:
                    sp.wait_ge(conv_done, q - 1)
                for r in range(2):
                    sp.dma_start(xw[0:64, 2 * (q % 2) + r, :], x[:, 2 * q + r, :]).then_inc(s_x[q % 2], 16)
                    sp.dma_start(xw[64:128, 2 * (q % 2) + r, 0:SIN - 1], x[:, 2 * q + r, 1:SIN]).then_inc(s_x[q % 2], 16)

            def store_xi(b, u, again):
                sp.wait_ge(c_normal, b + 1)
                sp.dma_start(xi_dram[b].rearrange("(p j d) -> p j d", p=P, j=J), xn[:, u, :, 0:D]).then_inc(xi_out[u], 16)

            load_windows(0)
            load_windows(1)
            sp.dma_start(idm[:, :], ident).then_inc(s_w, 16)
            sp.dma_start(wk[:, :], att_k).then_inc(s_w, 16)
            sp.dma_start(wqv[:, :], att_qv).then_inc(s_w, 16)
            sp.dma_start(wrt[:, :], att_r).then_inc(s_w, 16)
            sp.dma_start(wid[:, :], att_i).then_inc(s_w, 16)
            sp.dma_start(hm[:, :], head_mask).then_inc(s_w, 16)
            for q in range(2, B // 2):
                load_windows(q)
            def load_xi(b, u, again):
                sp.wait_ge(xi_out[u], slot(b, u))
                if again:
                    sp.wait_ge(a3p, after("out", b - 2, A3P))
                sp.dma_start(xi[0:D, u, :], xi_dram[b].rearrange("(c s) -> c s", c=D)).then_inc(xi_in[u], 16)

            for b in range(B):
                store_xi(b, b % 2, True)
                if 2 <= b < 4:
                    load_xi(b - 2, b % 2, False)
            with sp.Fori(1, B // 2) as turn:
                for u in range(2):
                    load_xi(turn * 2 + u, u, True)
            sp.wait_ge(rkv, RK_GROUPS)
            sp.wait_ge(pwp, PW_STEPS)
            sp.dma_start(b2t, tree_b2).then_inc(s_b2, 16)
            for n in range(SEG):
                sp.wait_ge(scattered, 16 * BT)
                sp.dma_start(rt[:, n * SEGT:(n + 1) * SEGT, :],
                             sorted_dram.ap().rearrange("(p g) w -> p g w", p=128)[:, n * SEGT:(n + 1) * SEGT, :]
                             ).then_inc(sorted_in[n], 16)
            for n in range(SEG):
                sp.wait_ge(y_act, (n + 1) * SEGT // 2)
                sp.dma_start(y_dram.ap().rearrange("(p g) w -> p g w", p=128)[:, n * SEGT:(n + 1) * SEGT, :],
                             ys[:, n * SEGT:(n + 1) * SEGT, :]).then_inc(y_out, 16)
            sp.wait_ge(y_act, PAIRS)
            sp.wait_ge(y_out, 16 * SEG)
            for dst, src in ((asc, ssm_a), (wb, ssm_b), (wc, ssm_c), (wdt, ssm_dt), (bdc, ssm_bd), (dsc, ssm_d),
                             (sely, sel_y), (mor, moe_r), (mo1, moe_1), (mb1, moe_b1), (mo2, moe_2), (mb2, moe_b2)):
                sp.dma_start(dst, src).then_inc(s_sw, 16)
            for q in range(B // 2):
                if q >= 2:
                    sp.wait_ge(x_pe, LANES * (q - 1))
                sp.wait_ge(spa, after("x2", q, SPA))
                sp.wait_ge(spp, after("x3", q, SPP))
                for r in range(4):
                    for i in range(3):
                        sp.dma_start(stk[32 * i:32 * i + 32, q % 2, r, :],
                                     part3[32 * r:32 * r + 32, i, :, :].rearrange("p a w -> p (a w)")).then_inc(stk_in[q % 2], 16)

            for q in range(B // 2):
                sp.wait_ge(row_vec, 2 * q + 2)
                for r in range(2):
                    sp.dma_start(out[2 * q + r].rearrange("(p j) d -> p (j d)", j=J), oo[:, r, :]).then_inc(row_out, 16)
            sp.wait_ge(row_out, 16 * B)

        def ln_pool_steps(pool, n, b, u):
            pool.wait_ge(ln_vec[n], after("var", b, LN_VEC))
            pool.sem_inc(pool_gate)
            pool.tensor_scalar(rs[:, u, :], vs[:, u, :], EPS, None, ALU.add).then_inc(ln_pool[n], 1)
            pool.wait_ge(ln_pool[n], 2 * b + 1)
            pool.tensor_tensor(rs[:, u, :], rs[:, u, :], power[:, u, :], ALU.pow).then_inc(ln_pool[n], 1)

        @block.gpsimd
        def _(pool):
            for dst, src in ((w1t, tree_1), (pth[:, 0:NODES], path), (trs, tri), (masks, part_masks), (base, tile_base), (idb, ident), (selw, sel_w)):
                pool.dma_start(dst[:, :], src).then_inc(s_tw, 16)
            pool.wait_ge(tset, 2)
            pool.dma_start(sorted_dram.ap().rearrange("(p g) w -> p g w", p=128),
                           zero[:, :].unsqueeze(1).broadcast_to([128, NT, ROW])).then_inc(zero_out, 16)

            def rstd_conv(b, u, again):
                pool.wait_ge(c_var, b + 1)
                pool.sem_inc(pool_gate)
                pool.tensor_scalar(rs[:, u, :], vs[:, u, :], EPS, None, ALU.add).then_inc(c_rstd, 1)
                pool.wait_ge(c_rstd, 2 * b + 1)
                pool.tensor_tensor(rs[:, u, :], rs[:, u, :], power[:, u, :], ALU.pow).then_inc(c_rstd, 1)

            rounds(pool, rstd_conv)
            pool.wait_ge(a3v, after("resid", B - 1, A3V))
            pool.dma_start(w2t[:, :, 0:CH * D], tree_2).then_inc(s_w2, 16)

            def tree_step(b, u):
                if has(b + 1):
                    pool.wait_ge(ln_vec[1], after("normal", b + 1, LN_VEC))
                    pool.tensor_copy(rows[:, bass.ds((b + 1) * J, J), 0:D], xn[:, 1 - u, :, 0:D]).then_inc(row_set, 1)
                if has(b + 2):
                    ln_pool_steps(pool, 1, b + 2, u)

            pipelined(pool, tree_step)
            n_pw = [0]

            def step(ins):
                n_pw[0] += 1
                ins.then_inc(pwp, 1)
                pool.wait_ge(pwp, n_pw[0])

            pool.wait_ge(rka, 2)
            for k, (lv_, op) in enumerate(((5, ALU.is_le), (5, ALU.is_gt), (6, ALU.is_le), (6, ALU.is_gt))):
                step(pool.tensor_scalar(side[:, k, :], lev[:, :, lv_], 0.0, None, op))
            step(pool.tensor_tensor(side[:, 4, :], gel[:, 1, :, 7], side[:, 0, :], ALU.mult))
            step(pool.tensor_tensor(side[:, 5, :], gel[:, 1, :, 7], side[:, 1, :], ALU.mult))
            step(pool.tensor_copy(pw[:, :, 0:6], gel[:, 1, :, 0:6]))
            for k in range(2):
                step(pool.tensor_tensor(pw[:, :, 6 + k], gel[:, 1, :, 6], side[:, k, :], ALU.mult))
            for k in range(4):
                step(pool.tensor_tensor(pw[:, :, 8 + k], side[:, 4 + k // 2, :], side[:, 2 + k % 2, :], ALU.mult))
            high, middle, low = (rows[:, :, D:ROW].bitcast(BF16)[:, :, i * SLOTS:(i + 1) * SLOTS] for i in range(NPARTS))
            step(pool.tensor_copy(high, pw))
            step(pool.tensor_tensor(pwl, pw, high, ALU.subtract))
            step(pool.tensor_copy(middle, pwl))
            step(pool.tensor_tensor(low, pwl, middle, ALU.subtract))
            assert n_pw[0] == PW_STEPS
            pool.wait_ge(zero_out, 16)
            pool.wait_ge(row_set, B)
            pool.wait_ge(rkv, RK_ROWS)
            for i in range(BT):
                pool.indirect_dma_start(out=sorted_dram[:, :], out_offset=bass.IndirectOffsetOnAxis(ap=sli[:, 3, i:i + 1], axis=0),
                                        in_=rows[:, i, :], in_offset=None).then_inc(scattered, 16)

            def double(t, p):
                wait(pool, turn_pe, t - 1)
                for i in range(2):
                    g, u = t * 2 + i, 2 * p + i
                    pool.tensor_copy(ws[:, u, :].rearrange("p (a w) -> p a w", a=NPARTS),
                                     rt[:, g, D:ROW].unsqueeze(1).broadcast_to([128, NPARTS, WS]))
                    pool.tensor_copy(xx[:, u, :].rearrange("p (a d) -> p a d", a=2),
                                     rt[:, g, 0:D].unsqueeze(1).broadcast_to([128, 2, D])).then_inc(xx_pool, 1)

            pool.wait_ge(rkv, RK_B2)
            for n in range(SEG):
                pool.wait_ge(sorted_in[n], 16)
                pairs(pool, n * SEGT // 2, (n + 1) * SEGT // 2, double)
            def rstd_scan(q):
                pool.wait_ge(ln_vec[2], after("var", q, LN_VEC))
                pool.tensor_scalar(rs[:, :, :], vs[:, :, :], EPS, None, ALU.add).then_inc(ln_pool[2], 1)
                pool.wait_ge(ln_pool[2], 2 * q + 1)
                pool.tensor_tensor(rs[:, :, :], rs[:, :, :], power[:, :, :], ALU.pow).then_inc(ln_pool[2], 1)

            def remainders(q):
                for k, name in enumerate(("d1", "x1")):
                    pool.wait_ge(spa, after(name, q, SPA))
                    pool.tensor_tensor(rest[:, k, :], dx[:, k, :], part3[:, 0, k, :], ALU.subtract).then_inc(spp, 1)

            def low_parts(q):
                for k, name in enumerate(("d2", "x2")):
                    pool.wait_ge(spa, after(name, q, SPA))
                    pool.tensor_tensor(part3[:, 2, k, :], rest[:, k, :], part3[:, 1, k, :], ALU.subtract).then_inc(spp, 1)

            pool.wait_ge(y_out, 16 * SEG)
            pool.wait_ge(y_act, PAIRS)
            for i in range(BT):
                pool.indirect_dma_start(out=yg[:, i, :], out_offset=None, in_=y_dram[:, :],
                                        in_offset=bass.IndirectOffsetOnAxis(ap=sli[:, 3, i:i + 1], axis=0)).then_inc(gathered[i // J], 16)
                if i == 3 * J - 1:
                    rstd_scan(0)
                    pool.dma_start(seld, sel_d).then_inc(s_sel, 16)
                    pool.dma_start(sele, sel_e).then_inc(s_sel, 16)
                if i == 6 * J - 1:
                    remainders(0)
                if i == 6 * J + 1:
                    low_parts(0)

            def rstd_pair(q):
                pool.wait_ge(rov, after("var", q, ROV))
                pool.tensor_scalar(rs[:, :, :], vs[:, :, :], EPS, None, ALU.add).then_inc(rstd_pool, 1)
                pool.wait_ge(rstd_pool, 2 * q + 1)
                pool.tensor_tensor(rs[:, :, :], rs[:, :, :], power[:, :, :], ALU.pow).then_inc(rstd_pool, 1)

            for n in range(B // 2 * LANES):
                pool.wait_ge(scan_vec, n + 1)
                if n % 8 == 0:
                    pool.wait_ge(sca, after(f"c{n % LANES // 8}", n // LANES, SCA))
                if n >= 4:
                    pool.wait_ge(y_sum, n // 2 - 1)
                pool.tensor_tensor(hc[:, n % 4, :], hs[:, n % 2, :], crep[:, n % LANES // 8, :], ALU.mult).then_inc(hc_pool, 1)
                if n % LANES == 5 and n // LANES < B // 2 - 1:
                    rstd_scan(n // LANES + 1)
                if n == (B // 2 - 1) * LANES + 6:
                    rstd_pair(0)
                if n % LANES == 12 and n // LANES < B // 2 - 1:
                    remainders(n // LANES + 1)
                if n % LANES == 13 and n // LANES < B // 2 - 1:
                    low_parts(n // LANES + 1)

            pool.wait_ge(s_sw, 16 * 12)
            pool.tensor_copy(b2p[:, 0, :], mb2).then_inc(b2_split, 1)
            pool.wait_ge(b2_split, 1)
            pool.tensor_tensor(b2l, mb2, b2p[:, 0, :], ALU.subtract).then_inc(b2_split, 1)
            pool.wait_ge(b2_split, 2)
            pool.tensor_copy(b2p[:, 1, :], b2l).then_inc(b2_split, 1)
            pool.wait_ge(b2_split, 3)
            pool.tensor_tensor(b2p[:, 2, :], b2l, b2p[:, 1, :], ALU.subtract).then_inc(b2_split, 1)

            for q in range(B // 2):
                pool.wait_ge(rov, after("normal", q, ROV))
                for r in range(2):
                    pool.tensor_tensor(v3(h[:, 2 * q + r, :]), v3(h[:, 2 * q + r, :]), xp[:, :, r, :], ALU.add).then_inc(hx_pool, 1)
                if q < B // 2 - 1:
                    rstd_pair(q + 1)

        @block.tensor
        def _(pe):
            pe.wait_ge(s_ph, 12)

            def conv(q, m):
                lo, hi = (0, HALF) if m == 0 else (HALF, S)
                if m == 0:
                    pe.wait_ge(s_x[q % 2], 16 * 4 * (q // 2 + 1))
                if q >= 2 and m == 0:
                    pe.wait_ge(yc_act, 2 * q - 2)
                for k in range(TAPS // 2):
                    for r in range(2):
                        last = pe.matmul(ps[D * r:D * r + D, 2 * (q % 2) + m, 0:hi - lo], weff[:, k * D:(k + 1) * D],
                                         xw[:, 2 * (q % 2) + r, 2 * k + lo:2 * k + hi], start=(k == 0), stop=(k == TAPS // 2 - 1))
                if m == 1:
                    last.then_inc(conv_done, 1)

            def conv_back(q):
                if q == 0:
                    pe.wait_ge(s_w, 16 * 6)
                else:
                    pe.wait_ge(h_set, 2 * q)
                pe.wait_ge(yc_act, 2 * q + 2)
                for j in range(J):
                    last = pe.transpose(ps[0:P, 4 + j // 4, (j % 4) * 128:(j % 4 + 1) * 128], yc[:, j::J], idm[:, :])
                last.then_inc(back_h, 1)

            for q in range(B // 2):
                conv(q, 0)
                if q:
                    conv_back(q - 1)
                conv(q, 1)
            conv_back(B // 2 - 1)

            def attention_step(b, u):
                v = 1 - u
                if has(b):
                    wait(pe, a3v, after("ctxm", b - 1, A3V))
                    pe.wait_ge(a2a, after("k1", b, A2A))
                    pe.sem_inc(pe_gate)
                    for j in range(J):
                        last = pe.transpose(ps[0:P, 4, j * D:(j + 1) * D], ke[:, u, j::J], idm[0:D, 0:D])
                    last.then_inc(a3p, 1)
                if has(b + 1):
                    pe.wait_ge(xi_in[v], slot(b + 1, v))
                    if isinstance(b, int) and b == -1:
                        pe.wait_ge(h_set, B)
                        pe.wait_ge(s_w, 16 * 6)
                        pe.wait_ge(s_const, 2)
                    wait(pe, a2a, after("k1", b, A2A))
                    pe.sem_inc(pe_gate)
                    for n, (lo, hi) in enumerate(((0, HALF), (HALF, S))):
                        last = pe.matmul(ps[0:D, n, 0:hi - lo], wk[:, :], xi[:, v, lo:hi], start=True, stop=True)
                    last.then_inc(a2p, 1)
                if has(b):
                    pe.wait_ge(a2v, after("qnorm", b, A2V))
                    pe.sem_inc(pe_gate)
                    for j in range(J):
                        last = pe.transpose(ps[0:D, 5 + j // JA, (j % JA) * P:(j % JA + 1) * P],
                                            qn[:, u, j * D:(j + 1) * D], idm[0:P, 0:P])
                    last.then_inc(a3p, 1)
                if has(b + 1):
                    for j in range(J):
                        last = pe.matmul(ps[0:P, 2 + j // 4, (j % 4) * 128:(j % 4 + 1) * 128], xi[:, v, j::J], wqv[:, :],
                                         start=True, stop=True)
                    last.then_inc(a2p, 1)
                if has(b):
                    pe.wait_ge(a3a, after("et", b, A3A))
                    pe.sem_inc(pe_gate)
                    for j in range(J):
                        last = pe.matmul(ps[0:D, 4, 448:512], qv[:, u, j * 128 + 64:(j + 1) * 128],
                                         et[:, u, j * D:(j + 1) * D], start=(j == 0), stop=(j == J - 1))
                    last.then_inc(a3p, 1)
                    pe.wait_ge(a3v, after("ctxm", b, A3V))
                    pe.sem_inc(pe_gate)
                    pe.matmul(ps[0:D, 7, 448:512], ctm[:, u, :], wrt[:, :], start=True, stop=True).then_inc(a3p, 1)
                    pe.wait_ge(a3v, after("mixn", b, A3V))
                    pe.sem_inc(pe_gate)
                    for j in range(J):
                        pe.matmul(ps[0:P, 7, j * D:(j + 1) * D], qt[:, u, j * P:(j + 1) * P], mixn[:, u, :],
                                  start=True, stop=False)
                        last = pe.matmul(ps[0:P, 7, j * D:(j + 1) * D], xi[:, u, j::J], wid[:, :], start=False, stop=True)
                    last.then_inc(a3p, 1)

            pipelined(pe, attention_step)

            def chunk(b, u, q):
                lo, hi = CHUNKS[q]
                last_use = (b, q - 2) if q >= 2 else (b - 1, q + 2)
                wait(pe, t1a, after(f"s{last_use[1]}", last_use[0], T1A))
                wait(pe, t1v, after(f"hot{last_use[1]}", last_use[0], T1V))
                if q == 0:
                    wait(pe, t1b, after("bit1", b, T1B))
                pe.sem_inc(pe_gate)
                for j in range(lo, hi):
                    pe.matmul(ps[0:P, 4 + q % 2, (j - lo) * NODES:(j - lo + 1) * NODES], xt[:, u, j * P:(j + 1) * P], w1t[:, :],
                              start=True, stop=True)
                for j in range(lo, hi):
                    last = pe.matmul(ps[0:P, 6 + q % 2, (j - lo) * NODES:(j - lo + 1) * NODES],
                                     bits[:, u, j * P:(j + 1) * P], pth[:, 0:NODES], start=True, stop=True)
                last.then_inc(t1p, 1)

            def tree_step(b, u):
                if has(b + 1):
                    pe.wait_ge(ln_vec[1], after("normal", b + 1, LN_VEC))
                    if isinstance(b, int) and b == -1:
                        pe.wait_ge(a3v, after("resid", B - 1, A3V))
                        pe.wait_ge(s_tw, 16 * 7)
                        pe.wait_ge(tset, 3)
                    wait(pe, t1x, after("xt1", b, T1X))
                    pe.sem_inc(pe_gate)
                    for j in range(J):
                        last = pe.transpose(ps[0:D + 1, j // JA, (j % JA) * P:(j % JA + 1) * P], xn[:, 1 - u, j, :], idm[0:P, 0:P])
                    last.then_inc(t1f, 1)
                if has(b):
                    chunk(b, u, 0)
                    chunk(b, u, 1)
                if has(b + 1):
                    pe.wait_ge(t1x, after("xt1", b + 1, T1X))
                    wait(pe, t1b, after("bit1", b, T1B))
                    pe.sem_inc(pe_gate)
                    pe.matmul(ps[0:INNER, 2, 0:NA], w1t[:, 0:INNER], xt[:, 1 - u, 0:NA], start=True, stop=True)
                    pe.matmul(ps[0:INNER, 3, 0:NB], w1t[:, 0:INNER], xt[:, 1 - u, NA:S], start=True, stop=True).then_inc(t1f, 1)
                if has(b):
                    chunk(b, u, 2)
                    chunk(b, u, 3)

            pipelined(pe, tree_step)
            pe.wait_ge(t1v, after("lev7", B - 1, T1V))
            flat = hot[:, :, :].rearrange("p i g -> p (i g)")
            for q in range(4):
                pe.matmul(ps[0:P, q, 0:448], trs[:, 0:P], flat[:, q * 448:(q + 1) * 448], start=True, stop=True)
            for q in range(4):
                last = pe.matmul(ps[0:P, 4 + q, 0:448], trs[:, P:2 * P], flat[:, q * 448:(q + 1) * 448], start=True, stop=True)
            last.then_inc(rkp, 1)

            def turn_pair(t, p):
                wait(pe, xx_pool, 2 * t + 2)
                wait(pe, wt_act, t)
                pe.sem_inc(pe_gate)
                for i in range(2):
                    pe.transpose(ps[0:PROD, 6, 256 + 64 * i:320 + 64 * i].bitcast(BF16), ws[:, 2 * p + i, :].bitcast(BF16), idb[:, :])
                    last = pe.transpose(ps[:, 6, i * TILE:(i + 1) * TILE], xx[:, 2 * p + i, :], idm[:, :])
                last.then_inc(turn_pe, 1)

            def spread(t, p):
                for i in range(2):
                    if i == 0:
                        wait(pe, wt_act, t + 1)
                    wait(pe, z_vec, 2 * t - 1 + i)
                    pe.sem_inc(pe_gate)
                    for c in range(CH):
                        last = pe.matmul(ps[:, 2 * i + c // 4, (c % 4) * TILE:(c % 4 + 1) * TILE], selw[:, c * 128:(c + 1) * 128],
                                         wt[:, 2 * p + i, :], start=True, stop=True)
                    last.then_inc(spread_pe, 1)

            def apply(t, p):
                wait(pe, z_vec, 2 * t + 2)
                wait(pe, yb_act, t - 1)
                pe.sem_inc(pe_gate)
                for i in range(2):
                    last = pe.matmul(ps[D * i:D * i + D, 4 + p, 0:TILE], gw[0:PROD, 2 * p + i, CH * D:GW].bitcast(BF16),
                                     wt[:, 2 * p + i, :], start=True, stop=False)
                last.then_inc(begun_pe, 1)
                for c in range(CH):
                    for i in range(2):
                        last = pe.matmul(ps[D * i:D * i + D, 4 + p, 0:TILE], gw[:, 2 * p + i, c * D:(c + 1) * D],
                                         zz[:, 2 * p + i, c * TILE:(c + 1) * TILE], start=False, stop=(c == CH - 1))
                last.then_inc(y_pe, 1)

            def turn_back(t, p):
                wait(pe, yb_act, t + 1)
                wait(pe, y_act, t)
                pe.sem_inc(pe_gate)
                pe.transpose(ps[:, 7, 0:TILE], yb[:, p, :], idm[:, :]).then_inc(back_y, 1)

            def steps(t, p):
                static = isinstance(t, int)
                if not static or t < PAIRS:
                    spread(t, p)
                if not static or t >= 2:
                    turn_back(t - 2, p)
                if not static or t < PAIRS - 1:
                    turn_pair(t + 1, 1 - p)
                if not static or 1 <= t <= PAIRS:
                    apply(t - 1, 1 - p)

            pe.wait_ge(rkv, RK_GROUPS)
            turn_pair(0, 0)
            pairs(pe, 0, PAIRS - 2, steps, peeled=4)
            for t in range(PAIRS - 2, PAIRS + 2):
                steps(t, t % 2)

            def prepare(q, part):
                u = q % 2
                if part == "turn":
                    pe.wait_ge(ln_vec[2], after("normal", q, LN_VEC))
                    if q == 0:
                        pe.wait_ge(y_act, PAIRS)
                        pe.wait_ge(s_sw, 16 * 12)
                    if q:
                        pe.wait_ge(sca, after("c1", q - 1, SCA))
                    for j in range(J):
                        last = pe.transpose(ps[:, 6 + j // JA, (j % JA) * P:(j % JA + 1) * P], xp[:, j, :, :].rearrange("p b d -> p (b d)"), idm[0:P, 0:P])
                    last.then_inc(scp, 1)
                if part == "z":
                    pe.wait_ge(sca, after("xt1", q, SCA))
                    pe.wait_ge(sset, 1)
                    for n in range(2):
                        last = pe.matmul(ps[:, 6 + n, 0:HALF], wdt, xs[:, u, n * HALF:(n + 1) * HALF], start=True, stop=True)
                    last.then_inc(scp, 1)
                if part in ("b0", "c0", "b1", "c1"):
                    if part == "b0":
                        pe.wait_ge(sca, after("z", q, SCA))
                    else:
                        pe.wait_ge(sca, after({"c0": "b0", "b1": "c0", "c1": "b1"}[part], q, SCA))
                    if part == "b1" and q:
                        pe.wait_ge(fiv, after("h1", q - 1, FIV))
                    w = (wb if part[0] == "b" else wc)[:, 128 * int(part[1]):128 * int(part[1]) + 128]
                    for n in range(2):
                        last = pe.matmul(ps[:, 6 + n, 0:HALF], w, xs[:, u, n * HALF:(n + 1) * HALF],
                                         start=True, stop=True)
                    last.then_inc(scp, 1)

            def route(q, stage):
                u = q % 2
                if stage == "turn":
                    pe.wait_ge(rov, after("normal", q, ROV))
                    if q == 0:
                        pe.wait_ge(back_pe, B // 2 - 1)
                        pe.wait_ge(sca, after("c1", B // 2 - 1, SCA))
                    else:
                        pe.wait_ge(roa, after("ct", q - 1, ROA))
                    for j in range(JA):
                        last = pe.transpose(ps[:, 7, j * P:(j + 1) * P], xp[:, j, :, :].rearrange("p b d -> p (b d)"), idm[0:P, 0:P])
                    last.then_inc(rop, 1)
                if stage == "turned":
                    pe.wait_ge(roa, after("xa", q, ROA))
                    for j in range(JA, J):
                        last = pe.transpose(ps[:, 7, (j - JA) * P:(j - JA + 1) * P], xp[:, j, :, :].rearrange("p b d -> p (b d)"),
                                            idm[0:P, 0:P])
                    last.then_inc(rop, 1)
                if stage == "logits":
                    pe.wait_ge(roa, after("xb", q, ROA))
                    for j in range(J):
                        last = pe.matmul(ps[0:P, 7, j * 2 * EXPERTS:(j + 1) * 2 * EXPERTS], xe[:, u, j * P:(j + 1) * P], mor,
                                         start=True, stop=True)
                    last.then_inc(rop, 1)
                if stage == "back":
                    pe.wait_ge(rov, after("low", q, ROV))
                    for j in range(J):
                        last = pe.transpose(ps[0:2 * NPARTS * EXPERTS, 7, 0:PW // 2 * J].bitcast(BF16)[:, j * PW:j * PW + P],
                                            combp[:, 2 * j:2 * j + 2, :].rearrange("p r e -> p (r e)"), idb[0:P, 0:P])
                    last.then_inc(rop, 1)

            for part in FIRST_PREP:
                prepare(0, part)

            def sum_states(v):
                pe.wait_ge(hc_pool, 2 * v + 2)
                q, w = divmod(v, LANES // 2)
                if w == 0 and q:
                    pe.wait_ge(fiv, after("skip", q - 1, FIV))
                for m in range(2):
                    for n in (2 * v, 2 * v + 1):
                        lane = ORDER[n % LANES]
                        last = pe.matmul(ps[32 * (lane // 4):32 * (lane // 4) + 32, 4 + m, 0:HALF],
                                         sely[:, 24 - 8 * (lane % 4):56 - 8 * (lane % 4)], hc[:, n % 4, m * HALF:(m + 1) * HALF],
                                         start=(lane % 4 == 0), stop=(lane % 4 == 3))
                last.then_inc(y_sum, 1)

            def back(q):
                pe.wait_ge(fiv, after("skip", q, FIV))
                pe.wait_ge(sca, after("c0", q + 1, SCA) if q < B // 2 - 1 else after("c1", q, SCA))
                for j in range(J):
                    last = pe.transpose(ps[0:P, 6 + j // 4, (j % 4) * 128:(j % 4 + 1) * 128], yt[:, j:S:J], idm[:, :])
                last.then_inc(back_pe, 1)

            for q in range(B // 2):
                u = q % 2
                for k in range(LANES):
                    n = q * LANES + k
                    lane = ORDER[k]
                    sel = seld[:, lane % 4 * 128:(lane % 4 + 1) * 128]
                    if k == 0:
                        pe.wait_ge(stk_in[u], 16 * 12 * (q // 2 + 1))
                    if n == 0:
                        pe.wait_ge(s_sel, 32)
                    if n:
                        pe.wait_ge(da_act, n)
                    for m in range(2):
                        last = pe.matmul(ps[:, m, 0:HALF], sel, stk[:, u, lane // 4, m * HALF:(m + 1) * HALF],
                                         start=True, stop=True)
                    last.then_inc(d_pe, 1)
                    if n:
                        pe.wait_ge(xdb_vec, n)
                    for m in range(2):
                        last = pe.matmul(ps[:, 2 + m, 0:HALF], sel, stk[:, u, lane // 4, SW + m * HALF:SW + (m + 1) * HALF],
                                         start=True, stop=True)
                    last.then_inc(x_pe, 1)
                    if n >= 5 and n % 2:
                        sum_states((n - 5) // 2)
                    if q and k == BACK_LANE:
                        back(q - 1)
                    if k == SECOND_AT:
                        prepare(q, "b1")
                        prepare(q, "c1")
                    if q < B // 2 - 1 and k - 1 in PREP_AT:
                        for part in PREP_AT[k - 1]:
                            prepare(q + 1, part)
                    if q == B // 2 - 1 and k - 1 in ROUTE_AT_SCAN:
                        route(0, ROUTE_AT_SCAN[k - 1])
            sum_states(B // 2 * LANES // 2 - 2)
            sum_states(B // 2 * LANES // 2 - 1)
            back(B // 2 - 1)


            def unit(n):
                q, k = divmod(n, UNITS)
                return q, k // 8, k % 8 // 2, k % 2

            def up(n):
                q, m, g, r = unit(n)
                if n % UNITS == 0:
                    pe.wait_ge(roa, after("xb", q, ROA))
                if n == 0:
                    pe.wait_ge(fiv, after("h1", B // 2 - 1, FIV))
                    pe.wait_ge(da_act, B // 2 * LANES)
                if n >= 2:
                    pe.wait_ge(gelu_act, n - 1)
                pe.matmul(ps[:, n % 2, 0:HALF], mo1[:, (4 * r + g) * 128:(4 * r + g + 1) * 128],
                          xe[:, q % 2, m * HALF:(m + 1) * HALF], start=True, stop=True).then_inc(up_pe, 1)

            def spread_weights(n):
                q, m, g, r = unit(n)
                if n % UNITS == 0:
                    pe.wait_ge(roa, after("ct", q, ROA))
                if n >= 2:
                    pe.wait_ge(gated_vec, n - 1)
                pe.matmul(ps[:, 2 + n % 2, 0:HALF], sele[:, (4 * r + g) * 128:(4 * r + g + 1) * 128],
                          ct[:, q % 2, m * HALF:(m + 1) * HALF], start=True, stop=True).then_inc(rep_pe, 1)

            def down(v):
                q, m, g, _ = unit(2 * v)
                pe.wait_ge(gated_vec, 2 * v + 2)
                if g == 0 and v >= 8:
                    pe.wait_ge(ye_act, v // 4 - 1)
                if v == 3:
                    pe.wait_ge(b2_split, 4)
                out_r = [ps[D * r:D * r + D, 4 + m, 0:HALF] for r in range(2)]
                for r in range(2):
                    last = pe.matmul(out_r[r], mo2[:, g * D:(g + 1) * D], gs[:, (2 * v + r) % 4, :], start=(g == 0), stop=False)
                for i in range(NPARTS if g == 3 else 0):
                    for r in range(2):
                        last = pe.matmul(out_r[r], b2p[:, i, r * D:(r + 1) * D], ct[:, q % 2, m * HALF:(m + 1) * HALF],
                                         start=False, stop=(i == NPARTS - 1))
                last.then_inc(down_pe, 1)

            def result_back(q, n):
                lo, hi = TOKENS_J[n]
                pe.wait_ge(ye_act, 2 * q + 2)
                if q or n:
                    pe.wait_ge(row_vec, 2 * q + n)
                for j in range(lo, hi):
                    last = pe.transpose(ps[0:P, 6, (j - lo) * 128:(j - lo + 1) * 128], ye[:, j * P:(j + 1) * P], idm[:, :])
                last.then_inc(back_e, 1)

            units = B // 2 * UNITS
            up(0)
            for n in range(units):
                q, k = divmod(n, UNITS)
                spread_weights(n)
                if n >= 3 and n % 2:
                    down((n - 3) // 2)
                if n + 1 < units:
                    up(n + 1)
                if q and k in BACK_AT:
                    result_back(q - 1, BACK_AT[k])
                if q < B // 2 - 1 and k in ROUTE_AT:
                    route(q + 1, ROUTE_AT[k])
            down(units // 2 - 1)
            result_back(B // 2 - 1, 0)
            result_back(B // 2 - 1, 1)

        def ln_act_steps(act, n, b, u):
            act.wait_ge(ln_vec[n], after("centred", b, LN_VEC))
            act.activation(sq[:, u, :], xc[:, u, :], ACT.Square, scale=ROOT).then_inc(ln_act[n], 1)

        def ln_centre(dve, n, b, u):
            src = v3(h[:, b, :])
            dve.tensor_reduce(mu[:, u, :], src, AX, ALU.add).then_inc(ln_vec[n], 1)
            dve.wait_ge(ln_vec[n], after("sum", b, LN_VEC))
            dve.tensor_scalar(mu[:, u, :], mu[:, u, :], 1.0 / D, None, ALU.mult).then_inc(ln_vec[n], 1)
            dve.wait_ge(ln_vec[n], after("mean", b, LN_VEC))
            dve.tensor_tensor(v3(xc[:, u, :]), src, mu[:, u, :].unsqueeze(2).broadcast_to([P, J, D]),
                              ALU.subtract).then_inc(ln_vec[n], 1)

        def ln_var(dve, n, b, u):
            dve.wait_ge(ln_act[n], after("square", b, LN_ACT))
            dve.tensor_reduce(vs[:, u, :], v3(sq[:, u, :]), AX, ALU.add).then_inc(ln_vec[n], 1)

        def ln_normal(dve, n, b, u, dst):
            dve.wait_ge(ln_pool[n], 2 * b + 2)
            dve.tensor_tensor(dst, v3(xc[:, u, :]), rs[:, u, :].unsqueeze(2).broadcast_to([P, J, D]),
                              ALU.mult).then_inc(ln_vec[n], 1)

        @block.scalar
        def _(act):
            act.wait_ge(s_ph, 9)
            act.activation(ph[:, 4, :], ph[:, 2, :], ACT.Sin).then_inc(s_pha, 1)
            act.activation(ph[:, 5, :], ph[:, 3, :], ACT.Sin).then_inc(s_pha, 1)
            act.wait_ge(s_const, 2)

            for q in range(B // 2):
                act.wait_ge(conv_done, q + 1)
                if q:
                    act.wait_ge(back_h, q)
                for m, (lo, hi) in enumerate(((0, HALF), (HALF, S))):
                    act.activation(yc[:, lo:hi], ps[:, 2 * (q % 2) + m, 0:hi - lo], ACT.Copy).then_inc(yc_act, 1)
                act.wait_ge(back_h, q + 1)
                for n, (lo, hi) in enumerate(((0, 4), (4, 7))):
                    act.activation(h[:, 2 * q:2 * q + 2, :].rearrange("p b (j d) -> p j b d", j=J)[:, lo:hi],
                                   ps[0:P, 4 + n, 0:(hi - lo) * 128].rearrange("p (j b d) -> p j b d", b=2, d=D), ACT.Copy).then_inc(h_set, 1)
                for b in (2 * q, 2 * q + 1):
                    act.wait_ge(c_centre, after("centred", b, CENTRE))
                    act.activation(sq[:, b % 2, :], xc[:, b % 2, :], ACT.Square, scale=ROOT).then_inc(c_square, 1)

            def attention_step(b, u):
                v = 1 - u
                if has(b):
                    act.wait_ge(a3p, after("et", b, A3P))
                    act.activation(et[:, u, :], ps[0:P, 4, 0:448], ACT.Copy).then_inc(a3a, 1)
                if has(b + 1):
                    act.wait_ge(a2p, after("qv", b + 1, A2P))
                    wait(act, a3p, after("ctx", b - 1, A3P))
                    act.activation(qv[:, v, 0:512], ps[0:P, 2, :], ACT.Copy).then_inc(a2a, 1)
                    act.activation(qv[:, v, 512:896], ps[0:P, 3, 0:384], ACT.Copy).then_inc(a2a, 1)
                    act.wait_ge(a2v, after("nkmax", b + 1, A2V))
                    wait(act, a3v, after("ksum", b - 1, A3V))
                    for n, (lo, hi) in enumerate(((0, HALF), (HALF, S))):
                        act.activation(ke[:, v, lo:hi], ps[0:D, n, 0:hi - lo], ACT.Exp, bias=kmx[:, v, 2:3],
                                       accum_out=ksum[:, v, n:n + 1]).then_inc(a2a, 1)
                    act.wait_ge(a2v, after("qsub", b + 1, A2V))
                    act.activation(qe[:, v, :], qs[:, v, :], ACT.Exp).then_inc(a2a, 1)

            pipelined(act, attention_step)

            def tree_step(b, u):
                if has(b + 2):
                    ln_act_steps(act, 1, b + 2, u)
                if has(b + 1):
                    act.wait_ge(t1f, after("xt", b + 1, T1F))
                    wait(act, t1p, after("c3", b - 1, T1P))
                    act.activation(xt[0:D + 1, 1 - u, 0:NA], ps[0:D + 1, 0, 0:NA], ACT.Copy).then_inc(t1x, 1)
                    act.activation(xt[0:D + 1, 1 - u, NA:S], ps[0:D + 1, 1, 0:NB], ACT.Copy).then_inc(t1x, 1)
                for q, (lo, hi) in enumerate(CHUNKS if has(b) else []):
                    act.wait_ge(t1p, after(f"c{q}", b, T1P))
                    if q >= 2:
                        act.wait_ge(t1v, after(f"pick{q - 2}", b, T1V))
                    else:
                        wait(act, t1v, after(f"pick{q + 2}", b - 1, T1V))
                    n = (hi - lo) * NODES
                    act.activation(scr[:, q % 2, 0:n], ps[0:P, 4 + q % 2, 0:n], ACT.Copy).then_inc(t1a, 1)

            act.wait_ge(tset, 3)
            pipelined(act, tree_step)
            act.wait_ge(t1v, after("lev7", B - 1, T1V))
            act.activation(gel[:, 0, :, :], lev[:, :, :], ACT.Abs).then_inc(rka, 1)
            act.wait_ge(rka, 1)
            act.activation(gel[:, 1, :, :], gel[:, 0, :, :], ACT.Gelu).then_inc(rka, 1)

            def turned(t, p):
                wait(act, turn_pe, t + 1)
                wait(act, z_vec, 2 * t - 2)
                act.activation(xxt[:, 2 * p:2 * p + 2, :], ps[:, 6, 0:2 * TILE].rearrange("p (a t) -> p a t", a=2), ACT.Copy).then_inc(xxt_act, 1)
                wait(act, begun_pe, t - 1)
                act.activation(wt[:, 2 * p:2 * p + 2, :], ps[0:PROD, 6, 256:384].bitcast(BF16).rearrange("p (a t) -> p a t", a=2),
                               ACT.Copy).then_inc(wt_act, 1)

            def channels_out(t, p):
                wait(act, y_pe, t + 1)
                wait(act, back_y, t - 1)
                act.activation(yb[:, p, :], ps[:, 4 + p, 0:TILE], ACT.Copy).then_inc(yb_act, 1)

            def result(t, p):
                wait(act, back_y, t + 1)
                act.activation(ys[:, bass.ds(t * 2, 2), :], ps[:, 7, 0:TILE].rearrange("p (a d) -> p a d", a=2), ACT.Copy).then_inc(y_act, 1)

            def steps(t, p):
                static = isinstance(t, int)
                if not static or t >= 2:
                    result(t - 2, p)
                if not static or t < PAIRS - 1:
                    turned(t + 1, 1 - p)
                if not static or 1 <= t <= PAIRS:
                    channels_out(t - 1, 1 - p)

            act.wait_ge(rkv, RK_B2)
            turned(0, 0)
            pairs(act, 0, PAIRS - 2, steps, peeled=4)
            for t in range(PAIRS - 2, PAIRS + 2):
                steps(t, t % 2)

            def prepare(q, part):
                u = q % 2
                if part == "centre":
                    if q == 0:
                        act.wait_ge(s_sw, 16 * 12)
                        act.wait_ge(sset, 1)
                        act.activation(asc, asc, ACT.Exp).then_inc(sset, 1)
                    act.wait_ge(ln_vec[2], after("centred", q, LN_VEC))
                    act.activation(sq[:, :, :], xc[:, :, :], ACT.Square, scale=ROOT).then_inc(ln_act[2], 1)
                if part == "turned":
                    act.wait_ge(scp, after("xt", q, SCP))
                    if q >= 2:
                        act.wait_ge(fiv, after("skip", q - 2, FIV))
                    dst = xs[:, u, 0:S].rearrange("c (p j) -> c j p", j=J)
                    act.activation(dst[:, 0:JA, :], ps[:, 6, 0:NA].rearrange("c (j p) -> c j p", p=P), ACT.Copy).then_inc(sca, 1)
                    act.activation(dst[:, JA:J, :], ps[:, 7, 0:NB].rearrange("c (j p) -> c j p", p=P), ACT.Copy).then_inc(sca, 1)
                if part == "softplus":
                    act.wait_ge(scp, after("z", q, SCP))
                    if q:
                        act.wait_ge(scv, after("relu", q - 1, SCV))
                    act.activation(halves(zb), ps[:, 6:8, 0:HALF], ACT.Identity, bias=bdc).then_inc(sca, 1)
                    act.wait_ge(sca, after("z", q, SCA))
                    act.activation(za, zb, ACT.Abs).then_inc(sca, 1)
                    act.wait_ge(sca, after("abs", q, SCA))
                    act.activation(za, za, ACT.Exp, scale=-1.0).then_inc(sca, 1)
                    act.wait_ge(sca, after("exp", q, SCA))
                    if q:
                        act.wait_ge(scv, after("delta", q - 1, SCV))
                    act.activation(zl, za, ACT.Ln, bias=1.0).then_inc(sca, 1)
                if part == "high":
                    if q:
                        act.wait_ge(stk_in[(q - 1) % 2], 16 * 12 * ((q - 1) // 2 + 1))
                    for k, name in enumerate(("delta", "xd")):
                        act.wait_ge(scv, after(name, q, SCV))
                        act.activation(part3[:, 0, k, :], dx[:, k, :], ACT.Copy).then_inc(spa, 1)
                if part == "middle":
                    for k, name in enumerate(("dr", "xr")):
                        act.wait_ge(spp, after(name, q, SPP))
                        act.activation(part3[:, 1, k, :], rest[:, k, :], ACT.Copy).then_inc(spa, 1)
                if part in ("b0", "c0", "b1", "c1"):
                    if part[1] == "0" and q:
                        act.wait_ge(xdb_vec, LANES * (q - 1) + 8)
                        act.wait_ge(hc_pool, LANES * (q - 1) + 8)
                    if part[1] == "1" and q:
                        act.wait_ge(xdb_vec, LANES * q)
                        act.wait_ge(hc_pool, LANES * q)
                    act.wait_ge(scp, after(part, q, SCP))
                    dst = (brep if part[0] == "b" else crep)[:, int(part[1]), :]
                    act.activation(halves(dst), ps[:, 6:8, 0:HALF], ACT.Copy).then_inc(sca, 1)

            def route(q, stage):
                u = q % 2
                if stage == "centre":
                    act.wait_ge(rov, after("centred", q, ROV))
                    act.activation(sq[:, :, :], xc[:, :, :], ACT.Square, scale=ROOT).then_inc(roa, 1)
                if stage == "turn":
                    act.wait_ge(rop, after("xa", q, ROP))
                    act.activation(xe[:, u, 0:NA], ps[:, 7, 0:NA], ACT.Copy).then_inc(roa, 1)
                if stage == "turned":
                    act.wait_ge(rop, after("xb", q, ROP))
                    act.activation(xe[:, u, NA:S], ps[:, 7, 0:NB], ACT.Copy).then_inc(roa, 1)
                if stage == "logits":
                    act.wait_ge(rov, after("sub", q, ROV))
                    act.activation(small[1], small[0], ACT.Exp).then_inc(roa, 1)
                if stage == "back":
                    act.wait_ge(rop, after("ct", q, ROP))
                    act.activation(v3(ct[:, u, 0:S]), v3(ps[0:2 * NPARTS * EXPERTS, 7, 0:PW // 2 * J].bitcast(BF16))[:, :, 0:P], ACT.Copy).then_inc(roa, 1)

            for part in FIRST_PREP:
                prepare(0, part)
            for q in range(B // 2):
                for k in range(LANES):
                    n = q * LANES + k
                    act.wait_ge(d_pe, n + 1)
                    if n >= 2:
                        act.wait_ge(scan_vec, n - 1)
                    if n == 0:
                        act.wait_ge(sset, 3)
                    act.activation(halves(da[:, n % 2, :]), ps[:, 0:2, 0:HALF], ACT.Exp, scale=asc[:, ORDER[k] % 8:ORDER[k] % 8 + 1]).then_inc(da_act, 1)
                    if k == SECOND_AT:
                        prepare(q, "b1")
                        prepare(q, "c1")
                    if q < B // 2 - 1 and k in PREP_AT:
                        for part in PREP_AT[k]:
                            prepare(q + 1, part)
                    if q == B // 2 - 1 and k in ROUTE_AT_SCAN:
                        route(0, ROUTE_AT_SCAN[k])


            def experts_out(w):
                q, m = divmod(w, 2)
                act.wait_ge(down_pe, 4 * w + 4)
                if q:
                    act.wait_ge(back_e, 2 * q)
                act.activation(ye[:, m * HALF:(m + 1) * HALF], ps[:, 4 + m, 0:HALF], ACT.Copy).then_inc(ye_act, 1)

            for n in range(B // 2 * UNITS):
                q, k = divmod(n, UNITS)
                act.wait_ge(up_pe, n + 1)
                if n == 0:
                    act.wait_ge(fiv, after("h1", B // 2 - 1, FIV))
                if n >= 2:
                    act.wait_ge(gated_vec, n - 1)
                act.activation(gl[:, n % 2, :], ps[:, n % 2, 0:HALF], ACT.Gelu, bias=mb1[:, k % 8 // 2:k % 8 // 2 + 1]).then_inc(gelu_act, 1)
                if n > 3 and k % 8 == 3:
                    experts_out(n // 8 - 1)
                if q < B // 2 - 1 and k in ROUTE_AT:
                    route(q + 1, ROUTE_AT[k])
            experts_out(B - 1)

        @block.vector
        def _(dve):
            dve.memset(power[:, :, :], -0.5)
            dve.memset(zero[:, :], 0.0).then_inc(tset, 1)
            dve.memset(w2t[:, :, CH * D:GW], 0.0)
            dve.memset(xn[:, :, :, D:D + 1], 1.0).then_inc(tset, 1)
            dve.memset(xi[64:128, :, :], 0.0).then_inc(s_const, 1)
            dve.wait_ge(s_const, 1)
            dve.memset(xi[64:65, :, :], 1.0).then_inc(s_const, 1)
            dve.wait_ge(s_cw, 48)
            two_pi = 2.0 * np.pi
            hi = float(np.float32(6.28125))
            dve.tensor_scalar(ph[:, 1, :], ph[:, 0, :], float(1.0 / two_pi), None, ALU.mult).then_inc(s_ph, 1)
            dve.wait_ge(s_ph, 1)
            dve.tensor_copy(phi[:, :], ph[:, 1, :]).then_inc(s_ph, 1)
            dve.wait_ge(s_ph, 2)
            dve.tensor_copy(ph[:, 1, :], phi[:, :]).then_inc(s_ph, 1)
            dve.wait_ge(s_ph, 3)
            dve.scalar_tensor_tensor(ph[:, 2, :], ph[:, 1, :], -hi, ph[:, 0, :], ALU.mult, ALU.add).then_inc(s_ph, 1)
            dve.wait_ge(s_ph, 4)
            dve.scalar_tensor_tensor(ph[:, 2, :], ph[:, 1, :], -float(two_pi - hi), ph[:, 2, :], ALU.mult, ALU.add).then_inc(s_ph, 1)
            dve.wait_ge(s_ph, 5)
            dve.tensor_scalar(ph[:, 2, :], ph[:, 2, :], 3.1415925, -3.1415925, ALU.min, ALU.max).then_inc(s_ph, 1)
            dve.wait_ge(s_ph, 6)
            dve.tensor_scalar(ph[:, 3, :], ph[:, 2, :], -1.0, None, ALU.mult).then_inc(s_ph, 1)
            dve.wait_ge(s_ph, 7)
            dve.tensor_tensor(ph[:, 3, :], ph[:, 2, :], ph[:, 3, :], ALU.min).then_inc(s_ph, 1)
            dve.wait_ge(s_ph, 8)
            dve.tensor_scalar(ph[:, 3, :], ph[:, 3, :], float(np.pi / 2), None, ALU.add).then_inc(s_ph, 1)
            dve.wait_ge(s_pha, 2)

            def per_tap(row):
                return ph[:, row, :].unsqueeze(2).broadcast_to([128, 8, D])
            dve.tensor_tensor(v3(wr[:, :], 8), v3(wr[:, :], 8), per_tap(5), ALU.mult).then_inc(s_ph, 1)
            dve.tensor_tensor(v3(wi[:, :], 8), v3(wi[:, :], 8), per_tap(4), ALU.mult).then_inc(s_ph, 1)
            dve.wait_ge(s_ph, 11)
            dve.tensor_tensor(weff[:, :], wr[:, :], wi[:, :], ALU.subtract).then_inc(s_ph, 1)

            dve.wait_ge(s_w, 16 * 6)

            def over_channels(ap):
                return ap.unsqueeze(2).broadcast_to([P, J, D])

            def norm_step(b, u):
                if has(b):
                    dve.wait_ge(c_rstd, 2 * b + 2)
                    wait(dve, xi_out[u], slot(b - 2, u))
                    dve.tensor_tensor(xn[:, u, :, 0:D], v3(xc[:, u, :]), over_channels(rs[:, u, :]), ALU.mult).then_inc(c_normal, 1)
                    dve.wait_ge(c_normal, b + 1)
                if has(b + 2):
                    dve.wait_ge(h_set, b + 4 - u)
                    src = v3(h[:, b + 2, :])
                    dve.tensor_reduce(mu[:, u, :], src, AX, ALU.add).then_inc(c_centre, 1)
                    dve.wait_ge(c_centre, after("sum", b + 2, CENTRE))
                    dve.tensor_scalar(mu[:, u, :], mu[:, u, :], 1.0 / D, None, ALU.mult).then_inc(c_centre, 1)
                    dve.wait_ge(c_centre, after("mean", b + 2, CENTRE))
                    dve.tensor_tensor(v3(xc[:, u, :]), src, over_channels(mu[:, u, :]), ALU.subtract).then_inc(c_centre, 1)
                if has(b + 1):
                    dve.wait_ge(c_square, b + 2)
                    dve.tensor_reduce(vs[:, 1 - u, :], v3(sq[:, 1 - u, :]), AX, ALU.add).then_inc(c_var, 1)

            pipelined(dve, norm_step)

            def heads(ap):
                return ap.rearrange("p (j g k) -> p j g k", j=J, g=HEADS)

            def per_head(ap):
                return ap.rearrange("p (j g) -> p j g", j=J)

            def over_head(ap):
                return per_head(ap).unsqueeze(3).broadcast_to([P, J, HEADS, DK])

            def attention_step(b, u):
                v = 1 - u
                if has(b + 1):
                    dve.wait_ge(a2p, after("k", b + 1, A2P))
                    wait(dve, a2a, after("k1", b - 1, A2A))
                    dve.tensor_reduce(kmx[:, v, 0:1], ps[0:D, 0, 0:HALF], AX, ALU.max)
                    dve.tensor_reduce(kmx[:, v, 1:2], ps[0:D, 1, 0:S - HALF], AX, ALU.max).then_inc(a2v, 1)
                    dve.wait_ge(a2v, after("kmax2", b + 1, A2V))
                    dve.tensor_reduce(kmx[:, v, 2:3], kmx[:, v, 0:2], AX, ALU.max, negate=True).then_inc(a2v, 1)
                if has(b):
                    dve.wait_ge(a3p, after("qt", b, A3P))
                    dve.tensor_copy(qt[:, u, 0:NA], ps[0:D, 5, 0:NA]).then_inc(a3v, 1)
                    dve.tensor_copy(qt[:, u, NA:S], ps[0:D, 6, 0:NB]).then_inc(a3v, 1)
                    dve.wait_ge(a3p, after("ctx", b, A3P))
                    dve.tensor_tensor(ctm[:, u, :], ps[0:D, 4, 448:512], hm[:, :], ALU.mult).then_inc(a3v, 1)
                    dve.tensor_tensor(kr[:, u, 0:1], ksum[:, u, 0:1], ksum[:, u, 1:2], ALU.add).then_inc(a3v, 1)
                    dve.wait_ge(a3v, after("ksum", b, A3V))
                    dve.reciprocal(kr[:, u, 1:2], kr[:, u, 0:1]).then_inc(a3v, 1)
                    dve.wait_ge(a3v, after("krec", b, A3V))
                    dve.wait_ge(a3p, after("mix", b, A3P))
                    dve.tensor_scalar(mixn[:, u, :], ps[0:D, 7, 448:512], kr[:, u, 1:2], None, ALU.mult).then_inc(a3v, 1)
                if has(b + 1):
                    dve.wait_ge(a2a, after("qv1", b + 1, A2A))
                    q = qv[:, v, :].rearrange("p (j w) -> p j w", j=J)[:, :, 0:D].rearrange("p j (g k) -> p j g k", g=HEADS)
                    dve.tensor_reduce(per_head(qmx[:, v, :]), q, AX, ALU.max).then_inc(a2v, 1)
                    dve.wait_ge(a2v, after("qmax", b + 1, A2V))
                    dve.tensor_tensor(heads(qs[:, v, :]), q, over_head(qmx[:, v, :]), ALU.subtract).then_inc(a2v, 1)
                if has(b):
                    dve.wait_ge(a3p, after("out", b, A3P))
                    dve.tensor_tensor(h[:, b, :], ps[0:P, 7, 0:448], h[:, b, :], ALU.add).then_inc(a3v, 1)
                if has(b + 1):
                    dve.wait_ge(a2a, after("qexp", b + 1, A2A))
                    dve.tensor_reduce(per_head(qsm[:, v, :]), heads(qe[:, v, :]), AX, ALU.add).then_inc(a2v, 1)
                    dve.wait_ge(a2v, after("qsum", b + 1, A2V))
                    dve.reciprocal(qmx[:, v, :], qsm[:, v, :]).then_inc(a2v, 1)
                    dve.wait_ge(a2v, after("qrec", b + 1, A2V))
                    wait(dve, a3p, after("qt", b - 1, A3P))
                    dve.tensor_tensor(heads(qn[:, v, :]), heads(qe[:, v, :]), over_head(qmx[:, v, :]), ALU.mult).then_inc(a2v, 1)

            pipelined(dve, attention_step)

            def picks(b, u, q):
                lo, hi = CHUNKS[q]
                n = (hi - lo) * NODES
                dve.wait_ge(t1a, after(f"s{q}", b, T1A))
                dve.scalar_tensor_tensor(pick[:, u, lo * NODES:lo * NODES + n], ps[0:P, 6 + q % 2, 0:n], 0.0, scr[:, q % 2, 0:n],
                                         ALU.is_equal, ALU.mult).then_inc(t1v, 1)
                dve.tensor_scalar(hot[:, bass.ds(b * J + lo, hi - lo), :],
                                  ps[0:P, 6 + q % 2, 0:n].rearrange("p (j n) -> p j n", n=NODES)[:, :, PRE - 1:2 * PRE - 1],
                                  0.0, None, ALU.is_equal).then_inc(t1v, 1)

            def tree_step(b, u):
                if has(b + 2):
                    ln_centre(dve, 1, b + 2, u)
                if has(b):
                    picks(b, u, 0)
                    picks(b, u, 1)
                if has(b + 2):
                    ln_var(dve, 1, b + 2, u)
                if has(b + 1):
                    dve.wait_ge(t1f, after("st", b + 1, T1F))
                    wait(dve, t1p, after("c3", b - 1, T1P))
                    dve.tensor_scalar(bits[0:INNER, 1 - u, 0:NA], ps[0:INNER, 2, 0:NA], 0.0, None, ALU.is_gt).then_inc(t1b, 1)
                    dve.tensor_scalar(bits[0:INNER, 1 - u, NA:S], ps[0:INNER, 3, 0:NB], 0.0, None, ALU.is_gt).then_inc(t1b, 1)
                if has(b):
                    picks(b, u, 2)
                if has(b + 2):
                    wait(dve, row_set, b + 1)
                    ln_normal(dve, 1, b + 2, u, xn[:, u, :, 0:D])
                if has(b):
                    picks(b, u, 3)
                    dve.wait_ge(t1v, after("hot3", b, T1V))
                    for l in range(DEPTH):
                        src = pick[:, u, :].rearrange("p (j n) -> p j n", n=NODES)[:, :, 2 ** l - 1:2 ** (l + 1) - 1]
                        dve.tensor_reduce(lev[:, bass.ds(b * J, J), l], src, AX, ALU.add).then_inc(t1v, 1)

            dve.memset(xt[64:128, :, :], 0.0)
            dve.memset(bits[:, :, :], 1.0).then_inc(tset, 1)
            dve.wait_ge(tset, 3)
            dve.wait_ge(a3v, after("resid", B - 1, A3V))
            pipelined(dve, tree_step)
            n_rk = [0]

            def step(ins):
                n_rk[0] += 1
                ins.then_inc(rkv, 1)
                dve.wait_ge(rkv, n_rk[0])

            dve.wait_ge(rkp, 1)
            for q in range(4):
                step(dve.tensor_copy(tot[:, :, 14 * q:14 * q + 14].rearrange("p g i -> p i g"),
                                     ps[0:P, 4 + q, 0:448].rearrange("p (i g) -> p i g", g=PRE)))
            step(dve.tensor_reduce(cnt[:, 0, :], tot[:, :, 0:BT], AX, ALU.add))
            step(dve.tensor_scalar(cnti[:, :], cnt[:, 0, :], float(TILE - 1), None, ALU.add))
            step(dve.tensor_scalar(cnti[:, :], cnti[:, :], 7, 7, ALU.logical_shift_right, ALU.logical_shift_left))
            step(dve.tensor_copy(cnt[:, 1, :], cnti[:, :]))
            step(dve.tensor_tensor(tot[:, :, BT], cnt[:, 1, :], cnt[:, 0, :], ALU.subtract))
            tf, nf = (t[:, :, :].rearrange("p g i -> p (g i)") for t in (tot, inc))
            step(dve.tensor_tensor_scan(nf, tf, tf, 0.0, ALU.add, ALU.max))
            step(dve.tensor_tensor(tf, nf, tf, ALU.subtract))
            for q in range(4):
                step(dve.tensor_tensor(rank[:, 14 * q:14 * q + 14, :], ps[0:P, q, 0:448].rearrange("p (i g) -> p i g", g=PRE),
                                       tot[:, :, 14 * q:14 * q + 14].rearrange("p g i -> p i g"), ALU.add))
            step(dve.tensor_tensor(rank[:, :, :], rank[:, :, :], hot[:, :, :], ALU.mult))
            step(dve.tensor_reduce(slf[:, 0, :], rank[:, :, :], AX, ALU.add))
            step(dve.tensor_copy(sli[:, 0, :], slf[:, 0, :]))
            step(dve.tensor_scalar(sli[:, 1, :], sli[:, 0, :], TILE - 1, None, ALU.bitwise_and))
            step(dve.tensor_scalar(sli[:, 2, :], sli[:, 0, :], 7, None, ALU.logical_shift_right))
            step(dve.tensor_copy(slf[:, 1, :], sli[:, 1, :]))
            step(dve.tensor_copy(slf[:, 2, :], sli[:, 2, :]))
            step(dve.scalar_tensor_tensor(slf[:, 0, :], slf[:, 1, :], float(NT), slf[:, 2, :], ALU.mult, ALU.add))
            step(dve.tensor_copy(sli[:, 3, :], slf[:, 0, :]))
            assert n_rk[0] == RK_ROWS
            step(dve.tensor_tensor(cmp[:, :, :], base[:, :].unsqueeze(2).broadcast_to([1, NT, PRE]),
                                   inc[0:1, :, BT].unsqueeze(1).broadcast_to([1, NT, PRE]), ALU.is_ge))
            step(dve.tensor_reduce(pff[:, 0, :], cmp[:, :, :], AX, ALU.add))
            step(dve.tensor_scalar(pff[:, 1, :], pff[:, 0, :], float(PRE - 1), None, ALU.min))
            sums = [pff[:, 0, 20 * i:20 * i + NT // 4] for i in range(3)]
            step(dve.scalar_tensor_tensor(sums[0], pff[:, 1, 3:NT:4], float(PRE), pff[:, 1, 2:NT:4], ALU.mult, ALU.add))
            step(dve.scalar_tensor_tensor(sums[1], sums[0], float(PRE), pff[:, 1, 1:NT:4], ALU.mult, ALU.add))
            step(dve.scalar_tensor_tensor(sums[2], sums[1], float(PRE), pff[:, 1, 0:NT:4], ALU.mult, ALU.add))
            step(dve.tensor_copy(packed[:, :], sums[2]))
            assert n_rk[0] == RK_GROUPS
            dve.wait_ge(s_b2, 16)
            dve.wait_ge(tset, 2)
            high, middle, low = (b2h[:, i, :] for i in range(NPARTS))
            step(dve.tensor_copy(high, b2t))
            step(dve.tensor_tensor(b2left, b2t, high, ALU.subtract))
            step(dve.tensor_copy(middle, b2left))
            step(dve.tensor_tensor(low, b2left, middle, ALU.subtract))

            def by_group(ap):
                return ap.rearrange("p (g d) -> p g d", g=PRE)
            parts = w2t[0:PROD, :, CH * D:GW].bitcast(BF16)
            step(dve.tensor_scalar(parts, by_group(high), masks[:, 0:1], None, ALU.mult))
            step(dve.scalar_tensor_tensor(parts, by_group(middle), masks[:, 1:2], parts, ALU.mult, ALU.add))
            step(dve.scalar_tensor_tensor(parts, by_group(low), masks[:, 2:3], parts, ALU.mult, ALU.add))
            assert n_rk[0] == RK_B2

            def product(t, p, groups):
                wait(dve, y_pe, t - 1)
                for i in range(2):
                    dve.tensor_copy(gw[:, 2 * p + i, :], w2t[:, groups[i], :])
                for i in range(2):
                    wait(dve, spread_pe, 2 * t + 1 + i)
                    if i == 0:
                        wait(dve, xxt_act, t + 1)
                    dve.tensor_tensor(zz[:, 2 * p + i, :].rearrange("p (c t) -> p c t", c=CH),
                                      ps[:, 2 * i:2 * i + 2, :].rearrange("p a c -> p (a c)")[:, 0:CH * TILE].rearrange("p (c t) -> p c t", c=CH),
                                      xxt[:, 2 * p + i, :].unsqueeze(1).broadcast_to([128, CH, TILE]), ALU.mult).then_inc(z_vec, 1)

            def two_pairs(turn):
                four = dve.value_load(packed[0:1, bass.ds(turn, 1)], min_val=0, max_val=PRE ** 4 - 1)
                product(turn * 2, 0, (four % PRE, four // PRE % PRE))
                product(turn * 2 + 1, 1, (four // PRE ** 2 % PRE, four // PRE ** 3))

            dve.wait_ge(s_w2, 16)
            two_pairs(0)
            with dve.Fori(1, PAIRS // 2) as turn:
                two_pairs(turn)

            def prepare(q, part):
                u = q % 2

                def rows_of(ap):
                    return ap.rearrange("p b (j d) -> p b j d", j=J)
                src = rows_of(h[:, 2 * q:2 * q + 2, :])
                if part == "centre":
                    if q == 0:
                        dve.wait_ge(s_sw, 16 * 12)
                        dve.wait_ge(y_act, PAIRS)
                        dve.memset(xs[:, :, S:SW], 0.0).then_inc(sset, 1)
                        dve.wait_ge(sset, 2)
                        dve.tensor_scalar(asc, asc, -1.0, None, ALU.mult).then_inc(sset, 1)
                    for b in (2 * q, 2 * q + 1):
                        dve.wait_ge(gathered[b], 16 * J)
                        dve.tensor_tensor(h[:, b, :], yg[:, b * J:(b + 1) * J, :].rearrange("p j d -> p (j d)"), h[:, b, :],
                                          ALU.add).then_inc(h_tree, 1)
                    dve.wait_ge(h_tree, 2 * q + 2)
                    dve.tensor_reduce(mu[:, :, :], src, AX, ALU.add).then_inc(ln_vec[2], 1)
                    dve.wait_ge(ln_vec[2], after("sum", q, LN_VEC))
                    dve.tensor_scalar(mu[:, :, :], mu[:, :, :], 1.0 / D, None, ALU.mult).then_inc(ln_vec[2], 1)
                    dve.wait_ge(ln_vec[2], after("mean", q, LN_VEC))
                    dve.tensor_tensor(rows_of(xc[:, :, :]), src, mu[:, :, :].unsqueeze(3).broadcast_to([P, 2, J, D]),
                                      ALU.subtract).then_inc(ln_vec[2], 1)
                if part == "norm":
                    dve.wait_ge(ln_act[2], after("square", q, LN_ACT))
                    dve.tensor_reduce(vs[:, :, :], rows_of(sq[:, :, :]), AX, ALU.add).then_inc(ln_vec[2], 1)
                if part == "turn":
                    dve.wait_ge(ln_pool[2], 2 * q + 2)
                    if q:
                        dve.wait_ge(scp, after("xt", q - 1, SCP))
                    dve.tensor_tensor(xp.rearrange("p j b d -> p b j d"), rows_of(xc[:, :, :]),
                                      rs[:, :, :].unsqueeze(3).broadcast_to([P, 2, J, D]), ALU.mult).then_inc(ln_vec[2], 1)
                if part == "delta":
                    dve.wait_ge(sca, after("z", q, SCA))
                    dve.tensor_scalar(zr, zb, 0.0, None, ALU.max).then_inc(scv, 1)
                    dve.wait_ge(scv, after("relu", q, SCV))
                    dve.wait_ge(sca, after("log", q, SCA))
                    if q:
                        dve.wait_ge(spp, after("xr", q - 1, SPP))
                    dve.tensor_tensor(dx[:, 0, :], zr, zl, ALU.add).then_inc(scv, 1)
                    dve.wait_ge(scv, after("delta", q, SCV))
                    dve.tensor_tensor(dx[:, 1, :], xs[:, u, :], dx[:, 0, :], ALU.mult).then_inc(scv, 1)

            def route(q, stage):
                def pair(ap):
                    return ap.rearrange("p b (j d) -> p b j d", j=J)

                def wide(ap, n):
                    return ap.unsqueeze(len(ap.shape)).broadcast_to(list(ap.shape) + [n])

                def next_(name, ins):
                    ins.then_inc(rov, 1)
                    dve.wait_ge(rov, after(name, q, ROV))

                src = pair(h[:, 2 * q:2 * q + 2, :])
                e3 = [t.rearrange("p (j e) -> p j e", e=EXPERTS) for t in small]
                rw = rankw[:, :].unsqueeze(1).broadcast_to([P, 2 * J, EXPERTS])
                lg = ps[0:P, 7, 0:2 * J * EXPERTS].rearrange("p (j e) -> p j e", e=EXPERTS)
                if stage == "centre":
                    if q == 0:
                        dve.wait_ge(scp, after("xt", B // 2 - 1, SCP))
                        for e in range(EXPERTS):
                            dve.memset(rankw[:, e:e + 1], float(EXPERTS - e))
                        dve.memset(xe[:, :, S:SW], 0.0)
                        dve.memset(ct[:, :, S:SW], 0.0).then_inc(sset, 1)
                        dve.wait_ge(sset, 4)
                    dve.wait_ge(fiv, after("h1", q, FIV))
                    next_("sum", dve.tensor_reduce(mu[:, :, :], src, AX, ALU.add))
                    next_("mean", dve.tensor_scalar(mu[:, :, :], mu[:, :, :], 1.0 / D, None, ALU.mult))
                    dve.tensor_tensor(pair(xc[:, :, :]), src, wide(mu[:, :, :], D), ALU.subtract).then_inc(rov, 1)
                if stage == "norm":
                    dve.wait_ge(roa, after("square", q, ROA))
                    dve.tensor_reduce(vs[:, :, :], pair(sq[:, :, :]), AX, ALU.add).then_inc(rov, 1)
                if stage == "turn":
                    dve.wait_ge(rstd_pool, 2 * q + 2)
                    if q:
                        dve.wait_ge(hx_pool, 2 * q)
                        dve.wait_ge(rop, after("xb", q - 1, ROP))
                    dve.tensor_tensor(xp.rearrange("p j b d -> p b j d"), pair(xc[:, :, :]), wide(rs[:, :, :], D),
                                      ALU.mult).then_inc(rov, 1)
                if stage == "logits":
                    dve.wait_ge(rop, after("route", q, ROP))
                    next_("max", dve.tensor_reduce(tiny[0], lg, AX, ALU.max))
                    dve.tensor_tensor(e3[0], lg, wide(tiny[0], EXPERTS), ALU.subtract).then_inc(rov, 1)
                if stage == "top":
                    dve.wait_ge(roa, after("exp", q, ROA))
                    next_("sum_exp", dve.tensor_reduce(tiny[1], e3[1], AX, ALU.add))
                    next_("rec", dve.reciprocal(tiny[2], tiny[1]))
                    next_("prob", dve.tensor_tensor(e3[2], e3[1], wide(tiny[2], EXPERTS), ALU.mult))
                    next_("top1", dve.tensor_reduce(tiny[3], e3[2], AX, ALU.max))
                    next_("eq1", dve.tensor_tensor(e3[3], e3[2], wide(tiny[3], EXPERTS), ALU.is_equal))
                    next_("cand1", dve.tensor_tensor(e3[4], e3[3], rw, ALU.mult))
                    next_("first1", dve.tensor_reduce(tiny[4], e3[4], AX, ALU.max))
                    next_("hot1", dve.tensor_tensor(e3[5], e3[4], wide(tiny[4], EXPERTS), ALU.is_equal))
                if stage == "second":
                    next_("rest", dve.scalar_tensor_tensor(e3[6], e3[5], -2.0, e3[2], ALU.mult, ALU.add))
                    next_("top2", dve.tensor_reduce(tiny[5], e3[6], AX, ALU.max))
                    next_("eq2", dve.tensor_tensor(e3[7], e3[6], wide(tiny[5], EXPERTS), ALU.is_equal))
                    next_("cand2", dve.tensor_tensor(e3[8], e3[7], rw, ALU.mult))
                    next_("first2", dve.tensor_reduce(tiny[6], e3[8], AX, ALU.max))
                    next_("hot2", dve.tensor_tensor(e3[9], e3[8], wide(tiny[6], EXPERTS), ALU.is_equal))
                    next_("both", dve.tensor_tensor(e3[10], e3[5], e3[9], ALU.add))
                    next_("topsum", dve.tensor_tensor(tiny[7], tiny[3], tiny[5], ALU.add))
                    next_("guard", dve.tensor_scalar(tiny[8], tiny[7], 1e-12, None, ALU.max))
                    next_("guardrec", dve.reciprocal(tiny[9], tiny[8]))
                    next_("kept", dve.tensor_tensor(e3[10], e3[10], e3[2], ALU.mult))
                    next_("comb", dve.tensor_tensor(e3[11], e3[10], wide(tiny[9], EXPERTS), ALU.mult))
                    if q:
                        dve.wait_ge(rop, after("ct", q - 1, ROP))
                    left = combl.rearrange("p (j e) -> p j e", e=EXPERTS)
                    high, middle, low = (combp[:, :, i * EXPERTS:(i + 1) * EXPERTS] for i in range(NPARTS))
                    next_("high", dve.tensor_copy(high, e3[11]))
                    next_("left", dve.tensor_tensor(left, e3[11], high, ALU.subtract))
                    next_("middle", dve.tensor_copy(middle, left))
                    dve.tensor_tensor(low, left, middle, ALU.subtract).then_inc(rov, 1)

            def result(q, n):
                lo, hi = TOKENS_J[n]
                dve.wait_ge(back_e, 2 * q + n + 1)
                dve.wait_ge(hx_pool, 2 * q + 2)
                if q:
                    dve.wait_ge(row_out, 16 * 2 * q)
                o, hv = (t.rearrange("p b (j d) -> p j b d", j=J)[:, lo:hi] for t in (oo, h[:, 2 * q:2 * q + 2, :]))
                dve.tensor_tensor(o, ps[0:P, 6, 0:(hi - lo) * 128].rearrange("p (j b d) -> p j b d", b=2, d=D), hv,
                                  ALU.add).then_inc(row_vec, 1)

            for part in FIRST_PREP:
                prepare(0, part)
            def drive(n):
                q, k = divmod(n, LANES)
                dve.wait_ge(x_pe, n + 1)
                if k % 8 == 0:
                    dve.wait_ge(sca, after(f"b{k // 8}", q, SCA))
                if n >= 2:
                    dve.wait_ge(scan_vec, n - 1)
                dve.tensor_tensor(halves(xdb[:, n % 2, :]), ps[:, 2:4, 0:HALF], halves(brep[:, k // 8, :]), ALU.mult).then_inc(xdb_vec, 1)

            def skip(q):
                dve.wait_ge(y_sum, LANES // 2 * (q + 1))
                if q:
                    dve.wait_ge(back_pe, q)
                dve.scalar_tensor_tensor(halves(yt), halves(xs[:, q % 2, :]), dsc, ps[:, 4:6, 0:HALF], ALU.mult, ALU.add).then_inc(fiv, 1)

            def add_rows(q):
                dve.wait_ge(back_pe, q + 1)
                for n, (lo, hi) in enumerate(TOKENS_J):
                    hv = h[:, 2 * q:2 * q + 2, :].rearrange("p b (j d) -> p j b d", j=J)[:, lo:hi]
                    dve.tensor_tensor(hv, ps[0:P, 6 + n, 0:(hi - lo) * 128].rearrange("p (j b d) -> p j b d", b=2, d=D), hv,
                                      ALU.add).then_inc(fiv, 1)

            for q in range(B // 2):
                drive(q * LANES)
                for k in range(LANES):
                    n = q * LANES + k
                    if k < LANES - 1:
                        drive(n + 1)
                    dve.wait_ge(xdb_vec, n + 1)
                    dve.wait_ge(da_act, n + 1)
                    if n >= 2:
                        dve.wait_ge(hc_pool, n - 1)
                    dve.tensor_tensor_scan(hs[:, n % 2, :], da[:, n % 2, :], xdb[:, n % 2, :], 0.0, ALU.mult, ALU.add).then_inc(scan_vec, 1)
                    if q and k == SKIP_AT:
                        skip(q - 1)
                    if q and k == ROWS_AT:
                        add_rows(q - 1)
                    if q < B // 2 - 1 and k in PREP_AT:
                        for part in PREP_AT[k]:
                            prepare(q + 1, part)
                    if q == B // 2 - 1 and k in ROUTE_AT_SCAN:
                        route(0, ROUTE_AT_SCAN[k])
            skip(B // 2 - 1)
            add_rows(B // 2 - 1)

            for n in range(B // 2 * UNITS):
                q, k = divmod(n, UNITS)
                dve.wait_ge(gelu_act, n + 1)
                dve.wait_ge(rep_pe, n + 1)
                if n >= 4:
                    dve.wait_ge(down_pe, n // 2 - 1)
                dve.tensor_tensor(gs[:, n % 4, :], gl[:, n % 2, :], ps[:, 2 + n % 2, 0:HALF], ALU.mult).then_inc(gated_vec, 1)
                if q and k in BACK_AT:
                    result(q - 1, BACK_AT[k])
                if q < B // 2 - 1 and k in ROUTE_AT:
                    route(q + 1, ROUTE_AT[k])
            result(B // 2 - 1, 0)
            result(B // 2 - 1, 1)


def constants():
    c = {}
    c["head_mask"] = np.kron(np.eye(HEADS), np.ones((DK, DK))).astype(np.float32)
    c["ident"] = np.eye(128, dtype=np.float32)
    path = np.zeros((INNER + 1, NODES), np.float32)
    for n in range(NODES):
        child = n
        while child:
            parent = (child - 1) // 2
            right = child == 2 * parent + 2
            path[parent, n] = 1.0 if right else -1.0
            path[INNER, n] -= 1.0 if right else 0.0
            child = parent
    c["path"] = path
    tri = np.zeros((P, 2, P), np.float32)
    tri[:, 0, :] = np.triu(np.ones((P, P)), 1)
    tri[:, 1, :] = 1.0
    c["tri"] = tri.reshape(P, 2 * P)
    c["tile_base"] = (np.arange(NT, dtype=np.float32) * TILE).reshape(1, NT)
    c["sel_w"] = np.zeros((PROD, SLOTS * D), np.float32)
    c["sel_w"][0:NPARTS * SLOTS] = np.tile(np.kron(np.eye(SLOTS), np.ones((1, D))), (NPARTS, 1))
    c["part_masks"] = np.repeat(np.eye(NPARTS, dtype=np.float32), NPARTS * SLOTS, axis=0)
    sel_d = np.zeros((96, 4, 8, STATE), np.float32)
    for r in range(96):
        sel_d[r, (r % 32) // 8, r % 8, :] = 1.0
    c["sel_d"] = sel_d.reshape(96, 4 * 128)
    sel_y = np.zeros((128, 56), np.float32)
    for r in range(128):
        sel_y[r, 24 + r // STATE] = 1.0
    c["sel_y"] = sel_y
    one = np.tile(np.kron(np.eye(EXPERTS), np.ones((1, D))), (NPARTS, 1))
    c["sel_e"] = np.kron(np.eye(2), one).astype(np.float32)
    return c


def layout(inputs):
    g = {k: np.asarray(v) for k, v in inputs.items()}
    a = {}
    a["x"] = g["x"].transpose(2, 0, 1)
    for name, key in (("conv_r", "L0_tok_w_real"), ("conv_i", "L0_tok_w_imag")):
        a[name] = g[key].reshape(D, D, TAPS // 2, 2).transpose(3, 1, 2, 0).reshape(128, TAPS // 2 * D)
    a["phase"] = np.repeat(g["L0_tok_phases"].reshape(TAPS // 2, 2).T, D, axis=0)
    def filled(w):
        return np.concatenate([w, np.zeros((128 - w.shape[0], w.shape[1]), w.dtype)])

    a["att_k"] = filled(np.concatenate([g["L0_attn_Wk"].T, g["L0_attn_bk"][None]]))
    a["att_qv"] = filled(np.concatenate([np.concatenate([g["L0_attn_Wq"].T, g["L0_attn_bq"][None]]),
                                  np.concatenate([g["L0_attn_Wv"].T, g["L0_attn_bv"][None]])], axis=1))
    a["att_r"] = g["L0_attn_Wr"].T
    a["att_i"] = filled(np.concatenate([np.eye(D, dtype=np.float32), g["L0_attn_br"][None]]))
    a["tree_1"] = filled(np.concatenate([g["L0_ffn_w1s"].T, g["L0_ffn_b1s"][None]]))
    node = np.zeros((PRE, SLOTS), np.int64)
    for q in range(PRE):
        node[q] = ([2 ** s - 1 + (q >> (5 - s)) for s in range(6)] + [63 + 2 * q + s for s in range(2)]
                   + [127 + 4 * q + s for s in range(4)])
    w2 = g["L0_ffn_w2s"][node].reshape(PRE, CH, 2, D, D)
    a["tree_2"] = w2.transpose(2, 3, 0, 1, 4).reshape(128, PRE, CH * D)
    a["tree_b2"] = np.tile(g["L0_ffn_b2s"][node].transpose(1, 0, 2).reshape(SLOTS, PRE * D), (NPARTS * NPARTS, 1))
    a["ssm_a"] = g["L1_attn_A_log"].reshape(8, 8 * STATE).T
    zero = np.zeros((D, D), np.float32)
    for name, key in (("ssm_b", "L1_attn_W_B"), ("ssm_c", "L1_attn_W_C")):
        w = np.tile(g[key].T, (1, 8))
        a[name] = np.block([[w, np.zeros_like(w)], [np.zeros_like(w), w]])
    a["ssm_dt"] = np.block([[g["L1_attn_W_delta"].T, zero], [zero, g["L1_attn_W_delta"].T]])
    a["ssm_bd"] = np.tile(g["L1_attn_b_delta"], 2)[:, None]
    a["ssm_d"] = np.tile(g["L1_attn_D_param"], 2)[:, None]
    def two_rows(w):
        return np.block([[w, np.zeros_like(w)], [np.zeros_like(w), w]])

    a["moe_r"] = two_rows(g["L1_ffn_router_w"].T)
    a["moe_1"] = two_rows(g["L1_ffn_w1"].transpose(1, 0, 2).reshape(D, EXPERTS * D))
    a["moe_b1"] = g["L1_ffn_b1"].reshape(4, 128).T
    a["moe_2"] = g["L1_ffn_w2"].reshape(4, 128, D).transpose(1, 0, 2).reshape(128, 4 * D)
    a["moe_b2"] = two_rows(np.tile(g["L1_ffn_b2"], (NPARTS, 1)))
    return a


_ORDER = ["x", "conv_r", "conv_i", "phase", "att_k", "att_qv", "att_r", "att_i", "head_mask", "ident", "tree_1",
          "tree_2", "tree_b2", "path", "sel_w", "part_masks", "tri", "tile_base", "ssm_a", "ssm_b", "ssm_c", "ssm_dt", "ssm_bd", "ssm_d",
          "sel_d", "sel_y", "moe_r", "moe_1", "moe_b1", "moe_2", "moe_b2", "sel_e"]


def kernel(**inputs):
    import concourse.bacc as _bacc
    from concourse.bass_utils import run_bass_kernel_spmd as _run

    nc = _bacc.Bacc("TRN2", target_bir_lowering=False, num_devices=1)
    arrays = {**layout(inputs), **constants()}
    arrays = {name: np.ascontiguousarray(arrays[name]) for name in _ORDER}
    aps = [nc.dram_tensor(f"in_{name}", a.shape, mybir.dt.from_np(a.dtype), kind="ExternalInput").ap()
           for name, a in arrays.items()]
    out = nc.dram_tensor("out", (B, S, D), F32, kind="ExternalOutput").ap()
    program(nc, *aps, out)
    r = _run(nc, [{f"in_{name}": a for name, a in arrays.items()}], core_ids=[0])
    return r.results[0]["out"]
```
